# Optimizing a Trainium2 kernel written in Bass

```python
import numpy as np
import jax
import jax.numpy as jnp

def _softmax(x, axis=-1):
    return jax.nn.softmax(x, axis=axis)

def _gelu(x):
    return jax.nn.gelu(x, approximate=True)

def _silu(x):
    return jax.nn.silu(x)

def _sigmoid(x):
    return jax.nn.sigmoid(x)

def _layernorm(x, axis=-1, eps=1e-05):
    m = jnp.mean(x, axis=axis, keepdims=True)
    v = jnp.var(x, axis=axis, keepdims=True)
    return (x - m) / jnp.sqrt(v + eps)

def _scatter_add(tgt, idx, src, axis=0):
    return tgt.at[idx].add(src)

def _segment_sum(src, seg, n):
    return jax.ops.segment_sum(src, seg, n)
kernel_name = 'mk_prb_d2_jaxref_r8_e5613a'

def setup_inputs(seed: int=0):
    np.random.seed(seed)
    _w = jnp.asarray

    def _L0_attn_setup():
        import jax, jax.numpy as jnp
        import numpy as np
        D_MODEL = 128
        D_STATE = 16
        D_CONV = 4
        EXPAND = 2
        D_INNER = EXPAND * D_MODEL
        DT_RANK = (D_MODEL + 15) // 16
        BATCH = 2
        SEQLEN = 256
        key = jax.random.key(seed)
        ks = jax.random.split(key, 8)
        s = lambda k, shape, scale: jax.random.normal(k, shape, dtype=jnp.float32) * scale
        return {'x': s(ks[0], (BATCH, SEQLEN, D_MODEL), 1.0), 'W_in': s(ks[1], (D_MODEL, 2 * D_INNER), D_MODEL ** (-0.5)), 'conv_w': s(ks[2], (D_INNER, 1, D_CONV), 0.3), 'conv_b': jnp.zeros((D_INNER,), dtype=jnp.float32), 'W_x': s(ks[3], (D_INNER, DT_RANK + 2 * D_STATE), D_INNER ** (-0.5)), 'W_dt': s(ks[4], (DT_RANK, D_INNER), 2.0 * DT_RANK ** (-0.5)), 'b_dt': s(ks[5], (D_INNER,), 0.1), 'A_log': jnp.log(jnp.tile(jnp.arange(1, D_STATE + 1, dtype=jnp.float32), (D_INNER, 1))), 'D': jnp.ones((D_INNER,), dtype=jnp.float32), 'W_out': s(ks[6], (D_INNER, D_MODEL), D_INNER ** (-0.5))}
    _L0_attn_in = _L0_attn_setup()

    def _L0_ffn_setup():
        import jax, jax.numpy as jnp
        import numpy as np
        B, T, C = (1, 256, 128)
        E = 32
        TOPK = 4
        H = 64
        HS = 128
        ROUTE_SCALE = 1.0

        def _swiglu(x, gate_w, down_w):
            u = x @ gate_w
            y, g = jnp.split(u, 2, axis=-1)
            return jax.nn.silu(g) * y @ down_w
        key = jax.random.key(seed)
        ks = jax.random.split(key, 6)
        s = 0.02
        return {'x': jax.random.normal(ks[0], (B, T, C), jnp.float32), 'gate_w': jax.random.normal(ks[1], (C, E), jnp.float32) * s, 'gate_bias': jnp.zeros((E,), jnp.float32), 'shared_gate_w': jax.random.normal(ks[2], (C, 2 * HS), jnp.float32) * s, 'shared_down_w': jax.random.normal(ks[3], (HS, C), jnp.float32) * s, 'expert_gate_w': jax.random.normal(ks[4], (E, C, 2 * H), jnp.float32) * s, 'expert_down_w': jax.random.normal(ks[5], (E, H, C), jnp.float32) * s}
    _L0_ffn_in = _L0_ffn_setup()

    def _L1_attn_setup():
        import jax, jax.numpy as jnp
        import numpy as np
        NUM_HEADS = 16
        LORA_SCALE = 32.0 / 8.0
        ROPE_BASE = 10000.0

        def make_sincos(seq_len, dim):
            pos = jnp.arange(seq_len, dtype=jnp.float32)
            i = jnp.arange(0, dim, 2, dtype=jnp.float32) / dim
            theta = pos[:, None] / ROPE_BASE ** i[None, :]
            return (jnp.sin(theta), jnp.cos(theta))

        def apply_rope(x, sin, cos):
            x_even = x[..., 0::2]
            x_odd = x[..., 1::2]
            rot_even = x_even * cos - x_odd * sin
            rot_odd = x_even * sin + x_odd * cos
            return jnp.stack([rot_even, rot_odd], axis=-1).reshape(x.shape)
        key = jax.random.key(seed)
        ks = jax.random.split(key, 9)
        B, T, D, R = (4, 256, 128, 8)
        s = 1.0 / np.sqrt(D)
        return {'query': jax.random.normal(ks[0], (B, T, D), dtype=jnp.float32), 'wq': jax.random.normal(ks[1], (D, D), dtype=jnp.float32) * s, 'wk': jax.random.normal(ks[2], (D, D), dtype=jnp.float32) * s, 'wv': jax.random.normal(ks[3], (D, D), dtype=jnp.float32) * s, 'wo': jax.random.normal(ks[4], (D, D), dtype=jnp.float32) * s, 'Aq': jax.random.normal(ks[5], (D, R), dtype=jnp.float32) * s, 'Bq': jax.random.normal(ks[6], (R, D), dtype=jnp.float32) * 0.01, 'Av': jax.random.normal(ks[7], (D, R), dtype=jnp.float32) * s, 'Bv': jax.random.normal(ks[8], (R, D), dtype=jnp.float32) * 0.01}
    _L1_attn_in = _L1_attn_setup()

    def _L1_ffn_setup():
        import jax, jax.numpy as jnp
        import numpy as np
        DIM = 128
        HIDDEN = 384
        SCALE = 1.0 / 127.0

        def _dequant(w_int, dtype):
            return w_int.astype(dtype) * jnp.asarray(SCALE, dtype)
        key = jax.random.key(seed)
        k_x, k_g, k_u, k_d = jax.random.split(key, 4)
        x = jax.random.normal(k_x, (4, 256, DIM), dtype=jnp.float32)
        w_gate = jax.random.randint(k_g, (HIDDEN, DIM), -127, 128, dtype=jnp.int32)
        w_up = jax.random.randint(k_u, (HIDDEN, DIM), -127, 128, dtype=jnp.int32)
        w_down = jax.random.randint(k_d, (DIM, HIDDEN), -127, 128, dtype=jnp.int32)
        return {'x': x, 'w_gate': w_gate, 'w_up': w_up, 'w_down': w_down}
    _L1_ffn_in = _L1_ffn_setup()
    _d = {'L0_attn_x': _L0_attn_in['x'], 'L0_attn_W_in': _L0_attn_in['W_in'], 'L0_attn_conv_w': _L0_attn_in['conv_w'], 'L0_attn_conv_b': _L0_attn_in['conv_b'], 'L0_attn_W_x': _L0_attn_in['W_x'], 'L0_attn_W_dt': _L0_attn_in['W_dt'], 'L0_attn_b_dt': _L0_attn_in['b_dt'], 'L0_attn_A_log': _L0_attn_in['A_log'], 'L0_attn_D': _L0_attn_in['D'], 'L0_attn_W_out': _L0_attn_in['W_out'], 'L0_ffn_gate_w': _L0_ffn_in['gate_w'], 'L0_ffn_gate_bias': _L0_ffn_in['gate_bias'], 'L0_ffn_shared_gate_w': _L0_ffn_in['shared_gate_w'], 'L0_ffn_shared_down_w': _L0_ffn_in['shared_down_w'], 'L0_ffn_expert_gate_w': _L0_ffn_in['expert_gate_w'], 'L0_ffn_expert_down_w': _L0_ffn_in['expert_down_w'], 'L1_attn_wq': _L1_attn_in['wq'], 'L1_attn_wk': _L1_attn_in['wk'], 'L1_attn_wv': _L1_attn_in['wv'], 'L1_attn_wo': _L1_attn_in['wo'], 'L1_attn_Aq': _L1_attn_in['Aq'], 'L1_attn_Bq': _L1_attn_in['Bq'], 'L1_attn_Av': _L1_attn_in['Av'], 'L1_attn_Bv': _L1_attn_in['Bv'], 'L1_ffn_w_gate': _L1_ffn_in['w_gate'], 'L1_ffn_w_up': _L1_ffn_in['w_up'], 'L1_ffn_w_down': _L1_ffn_in['w_down']}
    _x0 = _d['L0_attn_x']
    _d['L0_attn_x'] = jax.random.normal(jax.random.fold_in(jax.random.key(seed), 1), (4, 512, 128), dtype=_x0.dtype)
    del _x0
    return _d

def reference(L0_attn_x, L0_attn_W_in, L0_attn_conv_w, L0_attn_conv_b, L0_attn_W_x, L0_attn_W_dt, L0_attn_b_dt, L0_attn_A_log, L0_attn_D, L0_attn_W_out, L0_ffn_gate_w, L0_ffn_gate_bias, L0_ffn_shared_gate_w, L0_ffn_shared_down_w, L0_ffn_expert_gate_w, L0_ffn_expert_down_w, L1_attn_wq, L1_attn_wk, L1_attn_wv, L1_attn_wo, L1_attn_Aq, L1_attn_Bq, L1_attn_Av, L1_attn_Bv, L1_ffn_w_gate, L1_ffn_w_up, L1_ffn_w_down):

    def _L0_attn_ref(x, W_in, conv_w, conv_b, W_x, W_dt, b_dt, A_log, D, W_out):
        import jax, jax.numpy as jnp
        import numpy as np
        D_MODEL = 128
        D_STATE = 16
        D_CONV = 4
        EXPAND = 2
        D_INNER = EXPAND * D_MODEL
        DT_RANK = (D_MODEL + 15) // 16
        BATCH = 2
        SEQLEN = 256
        dt_rank = W_dt.shape[0]
        d_state = A_log.shape[1]
        Bsz, L, _ = x.shape
        d_inner = conv_w.shape[0]
        xr = x @ W_in
        xi, res = jnp.split(xr, 2, axis=-1)
        xc = jax.lax.conv_general_dilated(xi.transpose(0, 2, 1), conv_w, window_strides=(1,), padding=[(conv_w.shape[-1] - 1, 0)], feature_group_count=d_inner) + conv_b[None, :, None]
        u = jax.nn.silu(xc.transpose(0, 2, 1))
        dbc = u @ W_x
        delta_r = dbc[..., :dt_rank]
        Bm = dbc[..., dt_rank:dt_rank + d_state]
        Cm = dbc[..., dt_rank + d_state:]
        delta = jax.nn.softplus(delta_r @ W_dt + b_dt)
        A = -jnp.exp(A_log)
        deltaA = jnp.exp(delta[..., None] * A)
        dBu = delta[..., None] * Bm[:, :, None, :] * u[..., None]

        def step(h, inp):
            dA_t, dBu_t, C_t = inp
            h = dA_t * h + dBu_t
            y_t = jnp.einsum('bdn,bn->bd', h, C_t)
            return (h, y_t)
        h0 = jnp.zeros((Bsz, d_inner, d_state), dtype=x.dtype)
        _, ys = jax.lax.scan(step, h0, (deltaA.transpose(1, 0, 2, 3), dBu.transpose(1, 0, 2, 3), Cm.transpose(1, 0, 2)))
        y = ys.transpose(1, 0, 2) + u * D
        y = y * jax.nn.silu(res)
        return y @ W_out

    def _L0_ffn_ref(x, gate_w, gate_bias, shared_gate_w, shared_down_w, expert_gate_w, expert_down_w):
        import jax, jax.numpy as jnp
        import numpy as np
        B, T, C = (1, 256, 128)
        E = 32
        TOPK = 4
        H = 64
        HS = 128
        ROUTE_SCALE = 1.0

        def _swiglu(x, gate_w, down_w):
            u = x @ gate_w
            y, g = jnp.split(u, 2, axis=-1)
            return jax.nn.silu(g) * y @ down_w
        Bx, Tx, Cx = x.shape
        xf = x.reshape(-1, Cx)
        N = xf.shape[0]
        shared = _swiglu(x, shared_gate_w, shared_down_w)
        scores = jax.nn.sigmoid(xf @ gate_w)
        _, topk_idx = jax.lax.top_k(scores + gate_bias, TOPK)
        w = jnp.take_along_axis(scores, topk_idx, axis=-1)
        w = w / jnp.sum(w, axis=-1, keepdims=True) * ROUTE_SCALE
        combine = jnp.zeros((N, E), xf.dtype).at[jnp.arange(N)[:, None], topk_idx].add(w)
        out = jnp.zeros_like(xf)
        for e in range(E):
            out = out + combine[:, e:e + 1] * _swiglu(xf, expert_gate_w[e], expert_down_w[e])
        return shared + out.reshape(Bx, Tx, Cx)

    def _L1_attn_ref(query, wq, wk, wv, wo, Aq, Bq, Av, Bv):
        import jax, jax.numpy as jnp
        import numpy as np
        NUM_HEADS = 16
        LORA_SCALE = 32.0 / 8.0
        ROPE_BASE = 10000.0

        def make_sincos(seq_len, dim):
            pos = jnp.arange(seq_len, dtype=jnp.float32)
            i = jnp.arange(0, dim, 2, dtype=jnp.float32) / dim
            theta = pos[:, None] / ROPE_BASE ** i[None, :]
            return (jnp.sin(theta), jnp.cos(theta))

        def apply_rope(x, sin, cos):
            x_even = x[..., 0::2]
            x_odd = x[..., 1::2]
            rot_even = x_even * cos - x_odd * sin
            rot_odd = x_even * sin + x_odd * cos
            return jnp.stack([rot_even, rot_odd], axis=-1).reshape(x.shape)
        B, T, D = query.shape
        H = NUM_HEADS
        dh = D // H
        q = query @ wq + query @ Aq @ Bq * LORA_SCALE
        k = query @ wk
        v = query @ wv + query @ Av @ Bv * LORA_SCALE

        def split(x):
            return x.reshape(B, T, H, dh).transpose(0, 2, 1, 3)
        q, k, v = (split(q), split(k), split(v))
        sin, cos = make_sincos(T, dh)
        q = apply_rope(q, sin, cos)
        k = apply_rope(k, sin, cos)
        scores = jnp.einsum('bhqd,bhkd->bhqk', q, k) / jnp.sqrt(jnp.float32(dh))
        causal = jnp.triu(jnp.ones((T, T), dtype=bool), k=1)
        scores = jnp.where(causal[None, None], jnp.float32(-1000000000.0), scores)
        attn = jax.nn.softmax(scores, axis=-1)
        out = jnp.einsum('bhqk,bhkd->bhqd', attn, v)
        out = out.transpose(0, 2, 1, 3).reshape(B, T, D)
        return out @ wo

    def _L1_ffn_ref(x, w_gate, w_up, w_down):
        import jax, jax.numpy as jnp
        import numpy as np
        DIM = 128
        HIDDEN = 384
        SCALE = 1.0 / 127.0

        def _dequant(w_int, dtype):
            return w_int.astype(dtype) * jnp.asarray(SCALE, dtype)
        wg = _dequant(w_gate, x.dtype)
        wu = _dequant(w_up, x.dtype)
        wd = _dequant(w_down, x.dtype)
        gate = jnp.einsum('bsd,hd->bsh', x, wg)
        up = jnp.einsum('bsd,hd->bsh', x, wu)
        h = jax.nn.silu(gate) * up
        return jnp.einsum('bsh,dh->bsd', h, wd)
    x = L0_attn_x
    xn = _layernorm(x, axis=-1)
    x = x + _L0_attn_ref(xn, L0_attn_W_in, L0_attn_conv_w, L0_attn_conv_b, L0_attn_W_x, L0_attn_W_dt, L0_attn_b_dt, L0_attn_A_log, L0_attn_D, L0_attn_W_out) + _L0_ffn_ref(xn, L0_ffn_gate_w, L0_ffn_gate_bias, L0_ffn_shared_gate_w, L0_ffn_shared_down_w, L0_ffn_expert_gate_w, L0_ffn_expert_down_w)
    xn = _layernorm(x, axis=-1)
    x = x + _L1_attn_ref(xn, L1_attn_wq, L1_attn_wk, L1_attn_wv, L1_attn_wo, L1_attn_Aq, L1_attn_Bq, L1_attn_Av, L1_attn_Bv) + _L1_ffn_ref(xn, L1_ffn_w_gate, L1_ffn_w_up, L1_ffn_w_down)
    return x

_drawn_inputs = setup_inputs


def setup_inputs(seed=0):
    import zlib

    import numpy as np

    out = dict(_drawn_inputs(seed))
    spreads = {'L0_attn_conv_b': (0.0, 0.1), 'L0_attn_D': (1.0, 0.2), 'L0_ffn_gate_bias': (0.0, 0.8)}
    factors = {'L0_attn_b_dt': 6.998,
     'L0_ffn_gate_w': 8.0,
     'L0_ffn_shared_gate_w': 6.854,
     'L0_ffn_shared_down_w': 6.828,
     'L0_ffn_expert_gate_w': 8.0,
     'L0_ffn_expert_down_w': 8.0,
     'L1_attn_wq': 8.0,
     'L1_attn_wk': 8.0,
     'L1_attn_wv': 8.0,
     'L1_attn_wo': 8.0,
     'L1_attn_Aq': 8.0,
     'L1_attn_Bq': 8.0,
     'L1_attn_Av': 8.0,
     'L1_attn_Bv': 8.0}
    for name, (base, spread) in spreads.items():
        noise = np.random.default_rng([zlib.crc32(name.encode()), seed]).standard_normal(out[name].shape)
        drawn = base * np.exp(spread * noise) if base else spread * noise
        out[name] = jnp.asarray(drawn.astype(out[name].dtype))
    for name, factor in factors.items():
        out[name] = (out[name] * factor).astype(out[name].dtype)
    return out
```

```python
from contextlib import ExitStack

import concourse.bass as bass
from concourse import mybir

F32 = mybir.dt.float32
BF16 = mybir.dt.bfloat16
I32 = mybir.dt.int32
U32 = mybir.dt.uint32
ALU = mybir.AluOpType
ACT = mybir.ActivationFunctionType
AX_X = mybir.AxisListType.X

P = 128
BATCH, SEQ = 4, 512
TILES = BATCH * SEQ // P
TPB = SEQ // P
HALVES = 2
STATES = 16
TAPS = 4
PAD = TAPS - 1
DT_RANK = 8
BC = 2 * STATES
PARTS = 3
EXPERTS, TOPK, EH = 32, 4, 64
PAIRS = EXPERTS // 2
SHARED = PAIRS
EPS = 1e-5
HEADS, DH = 16, 8
GROUPS, GH = 4, 4
COMBOS = 6
QROWS = COMBOS * DH
HIDDEN, HID_CHUNKS = 384, 3
LORA_R, LORA_SCALE = 8, 32.0 / 8.0
QUANT = 1.0 / 127.0
MASKED = -1e30
SCALE = float(DH) ** -0.5


def prologue(nc, D, T, ctx):
    sb = lambda n, s, d=F32: ctx.enter_context(nc.sbuf_tensor(n, s, d))
    sem = lambda n: ctx.enter_context(nc.semaphore(n))
    pre = ctx.enter_context(nc.psum_tensor("pre", [P, 8, 512], F32))
    logits = pre[:, 4, :]
    comb_t = pre[:, 5:7, :].rearrange("p a b -> p (a b)").bitcast(BF16)

    stats = sb("stats", [P, TILES, 6])
    mean_var = sb("mean_var", [P, TILES, 2])
    rstd = sb("rstd", [P, TILES])
    std = sb("std", [P, TILES])
    eps = sb("eps", [P, 1])
    std_done, eps_set = sem("std_done"), sem("eps_set")
    xn = sb("xn", [P, TILES, P])
    gate_w = sb("gate_w", [P, EXPERTS])
    gate_bias = sb("gate_bias", [P, EXPERTS])
    iota = sb("iota", [P, EXPERTS])
    scores = sb("scores", [P, TILES, EXPERTS])
    biased = sb("biased", [P, TILES, EXPERTS])
    top_val = sb("top_val", [P, TILES, 8])
    top_idx = sb("top_idx", [P, TILES, 8], U32)
    top_f = sb("top_f", [P, TILES, 8])
    hit = sb("hit", [P, 2, TILES, EXPERTS])
    wsum = sb("wsum", [P, TILES])
    winv = sb("winv", [P, TILES])
    rest = sb("rest", [P, TILES, EXPERTS])
    parts = sb("parts", [P, TILES, PARTS * EXPERTS], BF16)

    x_in = [sem(f"x_in{g}") for g in range(BATCH)]
    small_in, weights_in = sem("small_in"), T["weights_in"]
    pads_set = sem("pads_set")
    stat_done, aggr_done, rstd_done, centred, xn_ready = (sem(n) for n in (
        "stat_done", "aggr_done", "rstd_done", "centred", "xn_ready"))
    turned, xnT_ready = sem("turned"), sem("xnT_ready")
    logits_ready, scores_ready = sem("logits_ready"), sem("scores_ready")
    top_done, route = sem("top_done"), sem("route")
    comb_turned, comb_ready = sem("comb_turned"), sem("comb_ready")
    a_ready = sem("a_ready")

    xtm, xnT, combT = T["xtm"], T["xnT"], T["combT"]
    x_dram = D["x"].rearrange("b (n p) c -> b p n c", p=P)
    n_weights = T["n_weights"]

    block = ctx.enter_context(nc.Block())

    @block.sync
    def _(sp):
        for b in range(BATCH):
            sp.dma_start(xtm[:, b * TPB:(b + 1) * TPB, :], x_dram[b]).then_inc(x_in[b], 16)
        for name, dst, src in T["weight_loads"]:
            sp.dma_start(dst, src).then_inc(weights_in, 16)
        sp.wait_ge(weights_in, 16 * n_weights)

    @block.gpsimd
    def _(pool):
        nc.gpsimd.memset(eps[:], EPS).then_inc(eps_set, 1)
        nc.gpsimd.memset(T["xpad"][:], 0.0).then_inc(pads_set, 1)
        pool.wait_ge(pads_set, 1)

    @block.scalar
    def _(act):
        act.dma_start(T["ident"][:], D["ident"]).then_inc(small_in, 16)
        act.dma_start(T["identb"][:], D["identb"]).then_inc(small_in, 16)
        act.dma_start(gate_w[:], D["gate_w"]).then_inc(small_in, 16)
        act.dma_start(gate_bias[:], D["gate_bias"]).then_inc(small_in, 16)
        act.dma_start(iota[:], D["iota"]).then_inc(small_in, 16)
        act.dma_start(T["A"][:], D["a_log"]).then_inc(small_in, 16)
        act.wait_ge(eps_set, 1)
        for b in range(BATCH):
            t = slice(b * TPB, (b + 1) * TPB)
            act.wait_ge(aggr_done, (b + 1) * TPB)
            nc.scalar.activation(std[:, t], mean_var[:, t, 1], ACT.Sqrt, bias=eps[:]).then_inc(std_done, 1)
        act.wait_ge(small_in, 16 * 6)
        nc.scalar.activation(T["A"][:], T["A"][:], ACT.Exp).then_inc(a_ready, 1)
        for g in range(BATCH):
            act.wait_ge(turned, g + 1)
            nc.scalar.copy(xnT[:, g * SEQ:(g + 1) * SEQ], pre[:, g, :]).then_inc(xnT_ready, 1)
        act.wait_ge(logits_ready, 1)
        nc.scalar.activation(scores[:].rearrange("p a b -> p (a b)"), logits, ACT.Sigmoid).then_inc(scores_ready, 1)
        act.wait_ge(comb_turned, 1)
        nc.scalar.copy(combT[:], comb_t[0:PARTS * EXPERTS, :]).then_inc(comb_ready, 1)
        act.wait_ge(comb_ready, 1)

    @block.vector
    def _(dve):
        for b in range(BATCH):
            dve.wait_ge(x_in[b], 16)
            for n in range(b * TPB, (b + 1) * TPB):
                nc.vector.bn_stats(stats[:, n, :], xtm[:, n, :]).then_inc(stat_done, 1)
            for n in range(b * TPB, (b + 1) * TPB):
                dve.wait_ge(stat_done, n + 1)
                nc.vector.bn_aggr(mean_var[:, n, :], stats[:, n, :]).then_inc(aggr_done, 1)
            t = slice(b * TPB, (b + 1) * TPB)
            dve.wait_ge(std_done, b + 1)
            nc.vector.reciprocal(rstd[:, t], std[:, t]).then_inc(rstd_done, 1)
            dve.wait_ge(rstd_done, b + 1)
            for n in range(b * TPB, (b + 1) * TPB):
                last = nc.vector.tensor_scalar(xn[:, n, :], xtm[:, n, :], mean_var[:, n, 0:1], rstd[:, n:n + 1],
                                               ALU.subtract, ALU.mult)
            last.then_inc(xn_ready, 1)
        dve.wait_ge(a_ready, 1)
        nc.vector.tensor_scalar(T["A"][:], T["A"][:], -1.0, None, ALU.mult).then_inc(route, 1)

        dve.wait_ge(scores_ready, 1)
        bias = gate_bias[:].unsqueeze(1).to_broadcast([P, TILES, EXPERTS])
        nc.vector.tensor_tensor(biased[:], scores[:], bias, ALU.add).then_inc(route, 1)
        dve.wait_ge(route, 2)
        for n in range(TILES):
            nc.vector.max(top_val[:, n, :], biased[:, n, :]).then_inc(top_done, 1)
        for n in range(TILES):
            dve.wait_ge(top_done, n + 1)
            nc.vector.max_index(top_idx[:, n, :], top_val[:, n, :], biased[:, n, :]).then_inc(top_done, 1)
        dve.wait_ge(top_done, 2 * TILES)
        nc.vector.tensor_copy(top_f[:], top_idx[:]).then_inc(route, 1)
        dve.wait_ge(route, 3)
        iota_b = iota[:].unsqueeze(1).to_broadcast([P, TILES, EXPERTS])
        step = 3
        for k in range(TOPK):
            chosen = top_f[:, :, k:k + 1].to_broadcast([P, TILES, EXPERTS])
            nc.vector.tensor_tensor(hit[:, min(k, 1)], iota_b, chosen, ALU.is_equal).then_inc(route, 1)
            step += 1
            dve.wait_ge(route, step)
            if k > 0:
                nc.vector.tensor_tensor(hit[:, 0], hit[:, 0], hit[:, 1], ALU.add).then_inc(route, 1)
                step += 1
                dve.wait_ge(route, step)
        nc.vector.tensor_tensor(scores[:], scores[:], hit[:, 0], ALU.mult).then_inc(route, 1)
        dve.wait_ge(route, step + 1)
        nc.vector.reduce_sum(wsum[:], scores[:], AX_X).then_inc(route, 1)
        dve.wait_ge(route, step + 2)
        nc.vector.reciprocal(winv[:], wsum[:]).then_inc(route, 1)
        dve.wait_ge(route, step + 3)
        nc.vector.tensor_tensor(scores[:], scores[:], winv[:].unsqueeze(2).to_broadcast([P, TILES, EXPERTS]),
                                ALU.mult).then_inc(route, 1)
        dve.wait_ge(route, step + 4)
        E = EXPERTS
        nc.vector.tensor_copy(parts[:, :, 0:E], scores[:]).then_inc(route, 1)
        dve.wait_ge(route, step + 5)
        nc.vector.tensor_tensor(rest[:], scores[:], parts[:, :, 0:E], ALU.subtract).then_inc(route, 1)
        dve.wait_ge(route, step + 6)
        nc.vector.tensor_copy(parts[:, :, E:2 * E], rest[:]).then_inc(route, 1)
        dve.wait_ge(route, step + 7)
        nc.vector.tensor_tensor(parts[:, :, 2 * E:3 * E], rest[:], parts[:, :, E:2 * E],
                                ALU.subtract).then_inc(T["comb_parts"], 1)
        dve.wait_ge(T["comb_parts"], 1)

    @block.tensor
    def _(pe):
        pe.wait_ge(small_in, 16 * 6)
        for b in range(BATCH):
            pe.wait_ge(xn_ready, b + 1)
            for n in range(TPB):
                last = nc.tensor.transpose(pre[:, b, n * P:(n + 1) * P], xn[:, b * TPB + n, :], T["ident"][:])
            last.then_inc(turned, 1)
        for n in range(TILES):
            if n % TPB == 0:
                pe.wait_ge(xnT_ready, n // TPB + 1)
            last = nc.tensor.matmul(logits[:, n * EXPERTS:(n + 1) * EXPERTS], xnT[:, n * P:(n + 1) * P], gate_w[:],
                                    start=True, stop=True)
        last.then_inc(logits_ready, 1)
        pe.wait_ge(T["comb_parts"], 1)
        for n in range(TILES):
            last = nc.tensor.transpose(comb_t[0:PARTS * EXPERTS, n * P:(n + 1) * P], parts[:, n, :], T["identb"][:])
        last.then_inc(comb_turned, 1)


def layer0(nc, T, ctx):
    sb = lambda n, s, d=F32: ctx.enter_context(nc.sbuf_tensor(n, s, d))
    sem = lambda n: ctx.enter_context(nc.semaphore(n))
    bank = ctx.enter_context(nc.psum_tensor("bank0", [P, 8, 512], F32))
    B_BANK, C_BANK, Y_BANK, V_BANK, G_BANK, W_BANK, O_BANK = 0, 1, 2, 4, 5, 6, 7

    xtm, xnT, combT, xpad, A = (T[n] for n in ("xtm", "xnT", "combT", "xpad", "A"))
    ident = T["ident"]
    conv = sb("conv", [P, HALVES, SEQ])
    sres = sb("sres", [P, HALVES, SEQ])
    u = sb("u", [P, HALVES, SEQ])
    softabs = sb("softabs", [P, HALVES, SEQ])
    zpos = sb("zpos", [P, HALVES, SEQ])
    delta = sb("delta", [P, HALVES, SEQ])
    du = sb("du", [P, HALVES, SEQ])
    dt_low = sb("dt_low", [DT_RANK, SEQ])
    bc_hi = sb("bc_hi", [PARTS * BC, SEQ], BF16)
    bc_rest = sb("bc_rest", [PARTS * BC, SEQ])
    bc_mid = sb("bc_mid", [PARTS * BC, SEQ], BF16)
    bc = sb("bc", [PARTS * BC, SEQ], BF16)
    dA = sb("dA", [P, 4, HALVES, SEQ])
    dBu = sb("dBu", [P, 2, HALVES, SEQ])
    h = sb("h", [P, 2, HALVES, SEQ])
    hC = sb("hC", [P, 2, HALVES, SEQ])
    silu_g = sb("silu_g", [P, 2, SEQ])
    hidden = sb("hidden", [P, 2, SEQ])
    weighted = sb("weighted", [P, 2, SEQ])
    y = sb("y", [P, HALVES, SEQ])
    outT = sb("outT", [P, SEQ])

    xi_ready, res_ready, xpad_ready, sres_ready, conv_step, u_ready = (sem(n) for n in (
        "xi_ready", "res_ready", "xpad_ready", "sres_ready", "conv_step", "u_ready"))
    bc_ready, dt_ready, dt_low_ready, bc_step, bc_parts, z_ready = (sem(n) for n in (
        "bc_ready", "dt_ready", "dt_low_ready", "bc_step", "bc_parts", "z_ready"))
    abs_done, expz_done, softlog_ready, zpos_done, delta_ready, du_ready = (sem(n) for n in (
        "abs_done", "expz_done", "softlog_ready", "zpos_done", "delta_ready", "du_ready"))
    B_ready, C_ready, g_ready, v_ready, w_ready = (sem(n) for n in (
        "B_ready", "C_ready", "g_ready", "v_ready", "w_ready"))
    dA_ready, silu_ready, dBu_done, scan_done, hC_done, hidden_done, weighted_done = (sem(n) for n in (
        "dA_ready", "silu_ready", "dBu_done", "scan_done", "hC_done", "hidden_done", "weighted_done"))
    summed, down_done, y_step, y_ready, out_ready, outT_ready, turned0, batch_done = (sem(n) for n in (
        "summed", "down_done", "y_step", "y_ready", "out_ready", "outT_ready", "turned0", "batch_done"))

    block = ctx.enter_context(nc.Block())
    N, M = STATES, STATES + 1

    @block.tensor
    def _(pe):
        pe.wait_ge(T["weights_in"], 16 * T["n_weights"])
        with pe.Fori(0, BATCH) as b:
            xs = xnT[:, bass.ts(b, SEQ)]
            pe.wait_ge(batch_done, b + 1)
            for m in range(4):
                mm = nc.tensor.matmul(bank[:, m, :], T["W_in"][:, m * P:(m + 1) * P], xs, start=True, stop=True)
                if m % 2:
                    mm.then_inc((xi_ready, res_ready)[m // 2], 1)
            pe.wait_ge(u_ready, b + 1)
            for k in range(HALVES):
                mm = nc.tensor.matmul(bank[0:DT_RANK, C_BANK, :], T["W_dtr"][:, k, :], u[:, k, :],
                                      start=(k == 0), stop=(k == 1))
            mm.then_inc(dt_ready, 1)
            for k in range(HALVES):
                mm = nc.tensor.matmul(bank[0:PARTS * BC, B_BANK, :], T["W_bc"][:, k, :], u[:, k, :],
                                      start=(k == 0), stop=(k == 1))
            mm.then_inc(bc_ready, 1)
            pe.wait_ge(dt_low_ready, b + 1)
            for k in range(HALVES):
                mm = nc.tensor.matmul(bank[:, V_BANK + k, :], T["W_dt"][:, k * P:(k + 1) * P], dt_low[:, :],
                                      start=True, stop=True)
            mm.then_inc(z_ready, 1)
            pe.wait_ge(bc_parts, b + 1)
            pe.wait_ge(sres_ready, b + 1)

            def down(i):
                if i < SHARED:
                    pe.wait_ge(weighted_done, b * N + i + 1)
                    w = T["down"][:, i, :]
                else:
                    pe.wait_ge(hidden_done, b * M + i + 1)
                    w = T["shared_down"][:]
                nc.tensor.matmul(bank[:, O_BANK, :], w, weighted[:, i % 2, :], start=(i == 0),
                                 stop=False).then_inc(down_done, 1)

            def sum_states(i):
                pe.wait_ge(hC_done, b * N + i + 1)
                for k in range(HALVES):
                    mm = nc.tensor.matmul(bank[:, Y_BANK + k, :], ident[:], hC[:, i % 2, k, :],
                                          start=(i == 0), stop=(i == N - 1))
                mm.then_inc(summed, 1)

            for i in range(M):
                if i < N:
                    if i > 0:
                        pe.wait_ge(dBu_done, b * N + i)
                    nc.tensor.matmul(bank[:, B_BANK, :], T["sel_bc"][:, i, :], bc[:], start=True,
                                     stop=True).then_inc(B_ready, 1)
                if i == 0:
                    pe.wait_ge(du_ready, b + 1)
                if i > 0:
                    pe.wait_ge(silu_ready, b * M + i)
                wg = T["gate_g"][:, i, :] if i < SHARED else T["shared_gate"][:, P:2 * P]
                nc.tensor.matmul(bank[:, G_BANK, :], wg, xs, start=True, stop=True).then_inc(g_ready, 1)
                if i > 0:
                    pe.wait_ge(hidden_done, b * M + i)
                wv = T["gate_v"][:, i, :] if i < SHARED else T["shared_gate"][:, 0:P]
                nc.tensor.matmul(bank[:, V_BANK, :], wv, xs, start=True, stop=True).then_inc(v_ready, 1)
                if i > 0:
                    down(i - 1)
                if i < N:
                    nc.tensor.matmul(bank[:, W_BANK, :], T["sel_pair"][:, i, :], combT[:, bass.ts(b, SEQ)],
                                     start=True, stop=True).then_inc(w_ready, 1)
                    if i > 0:
                        pe.wait_ge(hC_done, b * N + i)
                    nc.tensor.matmul(bank[:, C_BANK, :], T["sel_bc"][:, STATES + i, :], bc[:], start=True,
                                     stop=True).then_inc(C_ready, 1)
                if i > 0:
                    sum_states(i - 1)
            down(SHARED)
            pe.wait_ge(y_ready, b + 1)
            for k in range(HALVES):
                mm = nc.tensor.matmul(bank[:, O_BANK, :], T["W_out"][:, k, :], y[:, k, :], start=False, stop=(k == 1))
            mm.then_inc(out_ready, 1)
            pe.wait_ge(outT_ready, b + 1)
            for n in range(TPB):
                mm = nc.tensor.transpose(bank[:, W_BANK, n * P:(n + 1) * P], outT[:, n * P:(n + 1) * P], ident[:])
            mm.then_inc(turned0, 1)

    @block.scalar
    def _(act):
        with act.Fori(0, BATCH) as b:
            act.wait_ge(xi_ready, b + 1)
            nc.scalar.copy(xpad[:, :, PAD:PAD + SEQ], bank[:, 0:2, :]).then_inc(xpad_ready, 1)
            act.wait_ge(res_ready, b + 1)
            nc.scalar.activation(sres[:], bank[:, 2:4, :], ACT.Silu).then_inc(sres_ready, 1)
            act.wait_ge(conv_step, b * 8 + 8)
            for k in range(HALVES):
                ins = nc.scalar.activation(u[:, k, :], conv[:, k, :], ACT.Silu, bias=T["conv_b"][:, k:k + 1])
            ins.then_inc(u_ready, 1)
            act.wait_ge(z_ready, b + 1)
            for k in range(HALVES):
                ins = nc.scalar.activation(softabs[:, k, :], bank[:, V_BANK + k, :], ACT.Abs,
                                           bias=T["b_dt"][:, k:k + 1])
            ins.then_inc(abs_done, 1)
            act.wait_ge(abs_done, b + 1)
            nc.scalar.activation(softabs[:], softabs[:], ACT.Exp, scale=-1.0).then_inc(expz_done, 1)
            act.wait_ge(expz_done, b + 1)
            nc.scalar.activation(softabs[:], softabs[:], ACT.Ln, bias=1.0).then_inc(softlog_ready, 1)
            act.wait_ge(delta_ready, b + 1)

            def decay(i):
                if i >= 4:
                    act.wait_ge(scan_done, b * N + i - 3)
                for k in range(HALVES):
                    ins = nc.scalar.activation(dA[:, i % 4, k, :], delta[:, k, :], ACT.Exp, scale=A[:, k, i:i + 1])
                ins.then_inc(dA_ready, 1)

            def gate(i):
                act.wait_ge(g_ready, b * M + i + 1)
                if i >= 2:
                    act.wait_ge(hidden_done, b * M + i - 1)
                nc.scalar.activation(silu_g[:, i % 2, :], bank[:, G_BANK, :], ACT.Silu).then_inc(silu_ready, 1)

            decay(0)
            decay(1)
            for j in range(0, STATES, 2):
                gate(j)
                gate(j + 1)
                if j + 2 < STATES:
                    decay(j + 2)
                    decay(j + 3)
            gate(SHARED)
            act.wait_ge(out_ready, b + 1)
            nc.scalar.copy(outT[:], bank[:, O_BANK, :]).then_inc(outT_ready, 1)

    @block.vector
    def _(dve):
        nc.vector.memset(bc_rest[0:1, 0:1], 0.0).then_inc(batch_done, 1)
        with dve.Fori(0, BATCH) as b:
            dve.wait_ge(batch_done, b + 1)
            dve.wait_ge(xpad_ready, b + 1)
            for n, tap in enumerate(reversed(range(TAPS))):
                for k in range(HALVES):
                    src, w = xpad[:, k, tap:tap + SEQ], T["conv_w"][:, k, tap:tap + 1]
                    if n == 0:
                        nc.vector.tensor_scalar(conv[:, k, :], src, w, None, ALU.mult).then_inc(conv_step, 1)
                    else:
                        dve.wait_ge(conv_step, b * 8 + 2 * n + k - 1)
                        nc.vector.scalar_tensor_tensor(out=conv[:, k, :], in0=src, scalar=w, in1=conv[:, k, :],
                                                       op0=ALU.mult, op1=ALU.add).then_inc(conv_step, 1)
            dve.wait_ge(dt_ready, b + 1)
            nc.vector.tensor_copy(dt_low[:], bank[0:DT_RANK, C_BANK, :]).then_inc(dt_low_ready, 1)
            dve.wait_ge(bc_ready, b + 1)
            src = bank[0:PARTS * BC, B_BANK, :]
            nc.vector.tensor_copy(bc_hi[:], src).then_inc(bc_step, 1)
            dve.wait_ge(bc_step, b * 5 + 1)
            nc.vector.tensor_tensor(bc_rest[:], src, bc_hi[:], ALU.subtract).then_inc(bc_step, 1)
            dve.wait_ge(bc_step, b * 5 + 2)
            nc.vector.tensor_copy(bc_mid[:], bc_rest[:]).then_inc(bc_step, 1)
            nc.vector.tensor_copy(bc[0:BC, :], bc_hi[0:BC, :]).then_inc(bc_step, 1)
            dve.wait_ge(bc_step, b * 5 + 3)
            nc.vector.tensor_copy(bc[BC:2 * BC, :], bc_mid[BC:2 * BC, :]).then_inc(bc_step, 1)
            nc.vector.tensor_tensor(bc[2 * BC:, :], bc_rest[2 * BC:, :], bc_mid[2 * BC:, :],
                                    ALU.subtract).then_inc(bc_parts, 1)
            dve.wait_ge(z_ready, b + 1)
            dve.wait_ge(abs_done, b + 1)
            for k in range(HALVES):
                ins = nc.vector.tensor_scalar(zpos[:, k, :], bank[:, V_BANK + k, :], T["b_dt"][:, k:k + 1], 0.0,
                                              ALU.add, ALU.max)
            ins.then_inc(zpos_done, 1)
            dve.wait_ge(zpos_done, b + 1)
            dve.wait_ge(softlog_ready, b + 1)
            nc.vector.tensor_tensor(delta[:], zpos[:], softabs[:], ALU.add).then_inc(delta_ready, 1)
            dve.wait_ge(delta_ready, b + 1)
            nc.vector.tensor_tensor(du[:], delta[:], u[:], ALU.mult).then_inc(du_ready, 1)
            dve.wait_ge(du_ready, b + 1)

            def spread(n):
                return bank[:, n, :].unsqueeze(1).to_broadcast([P, HALVES, SEQ])

            def expert_hidden(i):
                dve.wait_ge(v_ready, b * M + i + 1)
                dve.wait_ge(silu_ready, b * M + i + 1)
                dst = hidden if i < SHARED else weighted
                if i >= 2:
                    dve.wait_ge(weighted_done, b * N + i - 1)
                if i == SHARED:
                    dve.wait_ge(down_done, b * M + i - 1)
                nc.vector.tensor_tensor(dst[:, i % 2, :], silu_g[:, i % 2, :], bank[:, V_BANK, :],
                                        ALU.mult).then_inc(hidden_done, 1)

            def expert_weight(i):
                dve.wait_ge(hidden_done, b * M + i + 1)
                dve.wait_ge(w_ready, b * N + i + 1)
                if i >= 2:
                    dve.wait_ge(down_done, b * M + i - 1)
                nc.vector.tensor_tensor(weighted[:, i % 2, :], hidden[:, i % 2, :], bank[:, W_BANK, :],
                                        ALU.mult).then_inc(weighted_done, 1)

            for i in range(STATES):
                dve.wait_ge(B_ready, b * N + i + 1)
                if i >= 2:
                    dve.wait_ge(scan_done, b * N + i - 1)
                nc.vector.tensor_tensor(dBu[:, i % 2], du[:], spread(B_BANK), ALU.mult).then_inc(dBu_done, 1)
                dve.wait_ge(dBu_done, b * N + i + 1)
                dve.wait_ge(dA_ready, b * N + i + 1)
                for k in range(HALVES):
                    ins = nc.vector.tensor_tensor_scan(h[:, i % 2, k, :], dA[:, i % 4, k, :], dBu[:, i % 2, k, :],
                                                       0.0, ALU.mult, ALU.add)
                ins.then_inc(scan_done, 1)
                if i > 0:
                    expert_hidden(i - 1)
                    expert_weight(i - 1)
                dve.wait_ge(C_ready, b * N + i + 1)
                dve.wait_ge(scan_done, b * N + i + 1)
                if i >= 2:
                    dve.wait_ge(summed, b * N + i - 1)
                nc.vector.tensor_tensor(hC[:, i % 2], h[:, i % 2], spread(C_BANK), ALU.mult).then_inc(hC_done, 1)
            expert_hidden(STATES - 1)
            expert_weight(STATES - 1)
            expert_hidden(SHARED)
            dve.wait_ge(summed, b * N + N)
            for k in range(HALVES):
                ins = nc.vector.scalar_tensor_tensor(out=y[:, k, :], in0=u[:, k, :], scalar=T["D"][:, k:k + 1],
                                                     in1=bank[:, Y_BANK + k, :], op0=ALU.mult, op1=ALU.add)
            ins.then_inc(y_step, 1)
            dve.wait_ge(y_step, b + 1)
            nc.vector.tensor_tensor(y[:], y[:], sres[:], ALU.mult).then_inc(y_ready, 1)
            dve.wait_ge(turned0, b + 1)
            xs = xtm[:, bass.ts(b, TPB), :]
            turned_out = bank[:, W_BANK, :].rearrange("p (n c) -> p n c", c=P)
            nc.vector.tensor_tensor(xs, xs, turned_out, ALU.add).then_inc(batch_done, 1)
        dve.wait_ge(batch_done, BATCH + 1)


def layer1_front(nc, D, T, ctx):
    sb = lambda n, s, d=F32: ctx.enter_context(nc.sbuf_tensor(n, s, d))
    sem = lambda n: ctx.enter_context(nc.semaphore(n))
    bank = ctx.enter_context(nc.psum_tensor("bank1", [P, 8, 512], F32))
    X_BANK, ROT_BANK, VAL_BANK, HG_BANK, HV_BANK = 0, 1, 5, 6, 7
    xtm, ident, v_all = T["xtm"], T["ident"], T["v_all"]

    w_int = sb("w_int", [P, 3, HIDDEN], I32)
    w_ffn = sb("w_ffn", [P, 3, HIDDEN])
    lora_a = sb("lora_a", [LORA_R, 2, P])
    lora_b = sb("lora_b", [LORA_R, 2, P])
    w_q = sb("w_q", [P, P])
    w_k = sb("w_k", [P, P])
    w_v = sb("w_v", [P, P])
    w_qs = sb("w_qs", [P, P])
    w_ks = sb("w_ks", [P, P])
    cos = sb("cos", [P, SEQ])
    sin = sb("sin", [P, SEQ])
    eps = sb("eps1", [P, 1])
    mean = sb("mean1", [P, TPB])
    varsum = sb("varsum1", [P, TPB])
    square = sb("square1", [P, TPB, P])
    square_done = sem("square_done")
    std = sb("std1", [P, TPB])
    rstd = sb("rstd1", [P, TPB])
    xn = sb("xn1", [P, TPB, P])
    xnT = sb("xnT1", [P, SEQ])
    silu_g = sb("silu_g1", [P, 2, SEQ])
    hid = sb("hid", [P, HID_CHUNKS, SEQ])
    rot_c = sb("rot_c", [P, 2, SEQ])
    rot_s = sb("rot_s", [P, 2, SEQ])
    qk_parts = sb("qk_parts", [P, 2, PARTS, SEQ], BF16)

    w_in, lora_ready, w_ready, eps_set, w_cast = (sem(n) for n in (
        "w1_in", "lora_ready", "w_ready", "eps1_set", "w_cast"))
    stat_done, aggr_done, std_done, rstd_done, xn_ready, turned, xnT_ready = (sem(n) for n in (
        "stat1_done", "aggr1_done", "std1_done", "rstd1_done", "xn1_ready", "turned1", "xnT1_ready"))
    hg_ready, hv_ready, silu_ready, hid_done, down_ready, front_done = (sem(n) for n in (
        "hg_ready", "hv_ready", "silu1_ready", "hid_done", "down_ready", "front_done"))
    rot_ready, v_ready, v_kept, rot_step, parts_ready, parts_out = (sem(n) for n in (
        "rot_ready", "v1_ready", "v_kept", "rot_step", "parts_ready", "parts_out"))
    mid_done = sem("mid_done")
    n_w = 10
    block = ctx.enter_context(nc.Block())

    @block.sync
    def _(sp):
        for dst, name in ((w_int[:], "w_ffn"), (lora_a[:, 0, :], "Aq_t"), (lora_a[:, 1, :], "Av_t"),
                          (lora_b[:, 0, :], "Bq"), (lora_b[:, 1, :], "Bv"), (w_q[:], "wq"), (w_k[:], "wk"),
                          (w_v[:], "wv"), (cos[:], "cos"), (sin[:], "sin")):
            sp.dma_start(dst, D[name]).then_inc(w_in, 16)
        sp.dma_start(T["masks"][:], D["masks"]).then_inc(parts_out, 16)
        with sp.Fori(0, BATCH) as b:
            sp.wait_ge(parts_ready, b + 1)
            for name, k, runs in (("q_stack", 0, ((0, 0, 3), (3, 0, 2), (5, 0, 1))),
                                  ("k_stack", 1, ((0, 0, 1), (1, 0, 1), (2, 0, 1), (3, 1, 1), (4, 1, 1), (5, 2, 1)))):
                for c, part, n in runs:
                    for m in range(n):
                        dst = T[name][b, :, c + m, :, :]
                        sp.dma_start(dst, qk_parts[:, k, part + m, :]).then_inc(parts_out, 16)
        sp.wait_ge(parts_out, 16 + 16 * 2 * COMBOS * BATCH)

    @block.gpsimd
    def _(pool):
        nc.gpsimd.memset(eps[:], EPS).then_inc(eps_set, 1)
        nc.gpsimd.memset(T["v_aug"][:], 0.0).then_inc(eps_set, 1)
        pool.wait_ge(eps_set, 2)
        nc.gpsimd.memset(T["v_aug"][:, :, :, :, DH:DH + 1], 1.0).then_inc(eps_set, 1)
        nc.gpsimd.memset(T["q_rows"][:], 1.0).then_inc(eps_set, 1)
        nc.gpsimd.memset(T["k_rows"][:], 1.0).then_inc(eps_set, 1)
        pool.wait_ge(eps_set, 5)

    @block.scalar
    def _(act):
        act.wait_ge(eps_set, 1)
        act.wait_ge(w_in, 16 * n_w)
        for m in range(3):
            ins = nc.scalar.activation(w_ffn[:, m, :], w_int[:, m, :], ACT.Copy)
        ins.then_inc(w_cast, 1)
        with act.Fori(0, BATCH) as b:
            act.wait_ge(aggr_done, b + 1)
            nc.scalar.activation(std[:], varsum[:], ACT.Sqrt, bias=eps[:], scale=1.0 / P).then_inc(std_done, 1)
            act.wait_ge(turned, b + 1)
            nc.scalar.copy(xnT[:], bank[:, X_BANK, :]).then_inc(xnT_ready, 1)
            for m in range(HID_CHUNKS):
                act.wait_ge(hg_ready, b * HID_CHUNKS + m + 1)
                if m >= 2:
                    act.wait_ge(hid_done, b * HID_CHUNKS + m - 1)
                nc.scalar.activation(silu_g[:, m % 2, :], bank[:, HG_BANK, :], ACT.Silu).then_inc(silu_ready, 1)
            act.wait_ge(v_ready, b + 1)
            nc.scalar.copy(v_all[:, bass.ts(b, TPB), :], bank[:, VAL_BANK, :].rearrange("p (n c) -> p n c", c=P)
                           ).then_inc(v_kept, 1)

    @block.vector
    def _(dve):
        dve.wait_ge(lora_ready, 1)
        for w, k in ((w_q, 0), (w_v, 1)):
            nc.vector.scalar_tensor_tensor(out=w[:], in0=bank[:, 0, k * P:(k + 1) * P], scalar=LORA_SCALE, in1=w[:],
                                           op0=ALU.mult, op1=ALU.add).then_inc(w_ready, 1)
        dve.wait_ge(w_ready, 2)
        for w, ws in ((w_q, w_qs), (w_k, w_ks)):
            nc.vector.tensor_copy(ws[:, 0::2], w[:, 1::2]).then_inc(w_ready, 1)
            nc.vector.tensor_copy(ws[:, 1::2], w[:, 0::2]).then_inc(w_ready, 1)
        dve.wait_ge(w_cast, 1)
        nc.vector.tensor_scalar(w_ffn[:], w_ffn[:], QUANT, None, ALU.mult).then_inc(w_ready, 1)
        nc.vector.memset(mean[:], 0.0).then_inc(front_done, 1)
        with dve.Fori(0, BATCH) as b:
            dve.wait_ge(front_done, b + 1)
            column = lambda t: t[:].unsqueeze(2).to_broadcast([P, TPB, P])
            nc.vector.reduce_sum(mean[:], xtm[:, bass.ts(b, TPB), :], AX_X).then_inc(stat_done, 1)
            dve.wait_ge(stat_done, b * 3 + 1)
            nc.vector.tensor_scalar(mean[:], mean[:], 1.0 / P, None, ALU.mult).then_inc(stat_done, 1)
            dve.wait_ge(stat_done, b * 3 + 2)
            nc.vector.tensor_tensor(xn[:], xtm[:, bass.ts(b, TPB), :], column(mean), ALU.subtract).then_inc(stat_done, 1)
            dve.wait_ge(stat_done, b * 3 + 3)
            nc.vector.tensor_tensor(square[:], xn[:], xn[:], ALU.mult).then_inc(square_done, 1)
            dve.wait_ge(square_done, b + 1)
            nc.vector.reduce_sum(varsum[:], square[:], AX_X).then_inc(aggr_done, 1)
            dve.wait_ge(std_done, b + 1)
            nc.vector.reciprocal(rstd[:], std[:]).then_inc(rstd_done, 1)
            dve.wait_ge(rstd_done, b + 1)
            nc.vector.tensor_tensor(xn[:], xn[:], column(rstd), ALU.mult).then_inc(xn_ready, 1)

            def hidden(m):
                dve.wait_ge(silu_ready, b * HID_CHUNKS + m + 1)
                dve.wait_ge(hv_ready, b * HID_CHUNKS + m + 1)
                nc.vector.tensor_tensor(hid[:, m, :], silu_g[:, m % 2, :], bank[:, HV_BANK, :],
                                        ALU.mult).then_inc(hid_done, 1)

            hidden(0)
            dve.wait_ge(rot_ready, b + 1)
            table = lambda t: t[:].unsqueeze(1).to_broadcast([P, 2, SEQ])
            nc.vector.tensor_tensor(rot_c[:], bank[:, ROT_BANK:ROT_BANK + 2, :], table(cos), ALU.mult).then_inc(rot_step, 1)
            hidden(1)
            nc.vector.tensor_tensor(rot_s[:], bank[:, ROT_BANK + 2:ROT_BANK + 4, :], table(sin),
                                    ALU.mult).then_inc(rot_step, 1)
            hidden(2)
            dve.wait_ge(rot_step, b * 5 + 2)
            nc.vector.tensor_tensor(rot_c[:], rot_c[:], rot_s[:], ALU.add).then_inc(rot_step, 1)
            dve.wait_ge(rot_step, b * 5 + 3)
            dve.wait_ge(parts_out, b * (16 * 2 * COMBOS) + 16)
            hi, mid, low = (qk_parts[:, :, m, :] for m in range(PARTS))
            nc.vector.tensor_copy(hi, rot_c[:]).then_inc(rot_step, 1)
            dve.wait_ge(rot_step, b * 5 + 4)
            nc.vector.tensor_tensor(rot_s[:], rot_c[:], hi, ALU.subtract).then_inc(rot_step, 1)
            dve.wait_ge(rot_step, b * 5 + 5)
            nc.vector.tensor_copy(mid, rot_s[:]).then_inc(mid_done, 1)
            dve.wait_ge(mid_done, b + 1)
            nc.vector.tensor_tensor(low, rot_s[:], mid, ALU.subtract).then_inc(parts_ready, 1)
            dve.wait_ge(down_ready, b + 1)
            xs = xtm[:, bass.ts(b, TPB), :]
            nc.vector.tensor_tensor(xs, xs, bank[:, X_BANK, :].rearrange("p (n c) -> p n c", c=P),
                                    ALU.add).then_inc(front_done, 1)
        dve.wait_ge(front_done, BATCH + 1)

    @block.tensor
    def _(pe):
        pe.wait_ge(w_in, 16 * n_w)
        for k in range(2):
            mm = nc.tensor.matmul(bank[:, 0, k * P:(k + 1) * P], lora_a[:, k, :], lora_b[:, k, :],
                                  start=True, stop=True)
        mm.then_inc(lora_ready, 1)
        pe.wait_ge(w_ready, 7)
        with pe.Fori(0, BATCH) as b:
            pe.wait_ge(xn_ready, b + 1)
            for n in range(TPB):
                mm = nc.tensor.transpose(bank[:, X_BANK, n * P:(n + 1) * P], xn[:, n, :], ident[:])
            mm.then_inc(turned, 1)
            pe.wait_ge(xnT_ready, b + 1)

            def hidden(m):
                if m:
                    pe.wait_ge(silu_ready, b * HID_CHUNKS + m)
                nc.tensor.matmul(bank[:, HG_BANK, :], w_ffn[:, 0, m * P:(m + 1) * P], xnT[:], start=True,
                                 stop=True).then_inc(hg_ready, 1)
                if m:
                    pe.wait_ge(hid_done, b * HID_CHUNKS + m)
                nc.tensor.matmul(bank[:, HV_BANK, :], w_ffn[:, 1, m * P:(m + 1) * P], xnT[:], start=True,
                                 stop=True).then_inc(hv_ready, 1)

            hidden(0)
            for k, w in enumerate((w_q, w_k, w_qs, w_ks)):
                mm = nc.tensor.matmul(bank[:, ROT_BANK + k, :], w[:], xnT[:], start=True, stop=True)
            mm.then_inc(rot_ready, 1)
            hidden(1)
            for n in range(TPB):
                mm = nc.tensor.matmul(bank[:, VAL_BANK, n * P:(n + 1) * P], xnT[:, n * P:(n + 1) * P], w_v[:],
                                      start=True, stop=True)
            mm.then_inc(v_ready, 1)
            hidden(2)
            pe.wait_ge(hid_done, b * HID_CHUNKS + HID_CHUNKS)
            for n in range(TPB):
                for m in range(HID_CHUNKS):
                    mm = nc.tensor.matmul(bank[:, X_BANK, n * P:(n + 1) * P], hid[:, m, n * P:(n + 1) * P],
                                          w_ffn[:, 2, m * P:(m + 1) * P], start=(m == 0), stop=(m == HID_CHUNKS - 1))
            mm.then_inc(down_ready, 1)


def attention(nc, D, T, out, ctx):
    sb = lambda n, s, d=F32: ctx.enter_context(nc.sbuf_tensor(n, s, d))
    sem = lambda n: ctx.enter_context(nc.semaphore(n))
    bank = ctx.enter_context(nc.psum_tensor("bank2", [P, 8, 512], F32))
    S1, S2, AV_BANK, M_BANK, T_BANK = 0, 2, 5, 6, 7
    xtm, ident, identb = T["xtm"], T["ident"], T["identb"]
    q_rows, k_rows, v_aug, v_all = T["q_rows"], T["k_rows"], T["v_aug"], T["v_all"]
    mask_qk, mask_kq = T["masks"][:, 0, :], T["masks"][:, 1, :]
    m_dram = T["m_rows"]
    NQ = TPB
    PCOLS = sum(SEQ - j * P for j in range(NQ))
    first = [sum(SEQ - i * P for i in range(j)) for j in range(NQ + 1)]

    w_o = sb("w_o", [P, P])
    rowmax = sb("rowmax", [P, 2, NQ, GH])
    negmax = sb("negmax", [P, NQ, GH])
    negrest = sb("negrest", [P, NQ, GH])
    neg_parts = sb("neg_parts", [P, 2, NQ, PARTS, GH], BF16)
    neg_t = sb("neg_t", [NQ * PARTS * GH, 2, P], BF16)
    probs = sb("probs", [P, 2, PCOLS])
    avT = sb("avT", [P, SEQ])
    inv_sum = sb("inv_sum", [P, NQ, GH])
    att = sb("att", [P, NQ, P])
    attT = sb("attT", [P, SEQ])
    result = sb("result", [P, NQ, P])

    stack_in = [sem(f"stack_in{k}") for k in range(2)]
    m_out, m_in = sem("m_out"), sem("m_in")
    s1_ready, max_done, neg_step, neg_ready, m_turned, neg_t_ready = (sem(n) for n in (
        "s1_ready", "max_done", "neg_step", "neg_ready", "m_turned", "neg_t_ready"))
    v_set, s2a_ready, s2b_ready, p_a, p_b, av_done, avT_ready, av_turned, inv_done, att_done = (sem(n) for n in (
        "v_set", "s2a_ready", "s2b_ready", "p_a", "p_b", "av_done", "avT_ready", "av_turned", "inv_done", "att_done"))
    att_turned, attT_ready, o_ready, result_ready, result_out = (sem(n) for n in (
        "att_turned", "attT_ready", "o_ready", "result_ready", "result_out"))

    chunks = ([(i, heads) for i in (0, 1) for heads in ((0, 2), (1, 3))]
              + [(i, (hl,)) for i in (2, 3) for hl in range(GH)])
    NCH = len(chunks)
    G, H = GROUPS, HEADS
    out_dram = out.rearrange("b (n p) c -> b p n c", p=P)
    block = ctx.enter_context(nc.Block())

    @block.sync
    def _(sp):
        sp.dma_start(w_o[:], D["wo"]).then_inc(result_out, 16)
        with sp.Fori(0, BATCH) as b:
            def load_stack(g):
                if g >= 2:
                    sp.wait_ge(s2b_ready, b * H + (g - 1) * GH)
                else:
                    sp.wait_ge(result_ready, b + 1)
                for par in range(2):
                    for rows, name in ((q_rows, "q_stack"), (k_rows, "k_stack")):
                        src = T[name][b].rearrange("h c r t -> h (c r) t")
                        src = src[GH * g + par:GH * (g + 1):2].rearrange("h r t -> r h t")
                        sp.dma_start(rows[64 * par:64 * par + QROWS, g % 2, :, :], src).then_inc(stack_in[g % 2], 16)

            def place_max(g):
                sp.wait_ge(neg_t_ready, b * G + g + 1)
                sp.dma_start(m_dram[g % 2], neg_t[:, g % 2, :]).then_inc(m_out, 16)
                sp.wait_ge(m_out, b * (16 * G) + 16 * (g + 1))
                for par in range(2):
                    src = m_dram[g % 2].rearrange("(i j h two) q -> two j h i q", i=NQ, j=PARTS, two=2)[par]
                    dst = q_rows[64 * par + QROWS:64 * par + QROWS + PARTS, g % 2, :, :]
                    sp.dma_start(dst.rearrange("j h (i q) -> j h i q", q=P), src).then_inc(m_in, 16)

            load_stack(0)
            load_stack(1)
            place_max(0)
            place_max(1)
            load_stack(2)
            place_max(2)
            load_stack(3)
            place_max(3)
            sp.wait_ge(result_ready, b + 2)
            sp.dma_start(out_dram[b], result[:]).then_inc(result_out, 16)
        sp.wait_ge(result_out, 16 + 16 * BATCH)

    @block.gpsimd
    def _(pool):
        with pool.Fori(0, BATCH) as b:
            for g in range(G):
                if g < 2:
                    pool.wait_ge(result_ready, b + 1)
                else:
                    pool.wait_ge(av_done, b * H + (g - 1) * GH)
                for hl in range(GH):
                    c = (GH * g + hl) * DH
                    ins = nc.gpsimd.tensor_copy(v_aug[:, g % 2, :, hl, 0:DH], v_all[:, bass.ts(b, TPB), c:c + DH])
                ins.then_inc(v_set, 1)

    @block.tensor
    def _(pe):
        with pe.Fori(0, BATCH) as b:
            def stack(t, g, hl, rows, cols):
                lo = 64 * (hl % 2)
                return t[lo:lo + rows, g % 2, hl // 2, cols]

            def max_pass(g):
                pe.wait_ge(stack_in[g % 2], b * (2 * 64) + 64 * (g // 2 + 1))
                for n, (i, heads) in enumerate(chunks):
                    done = g * NCH + n
                    if done >= 2:
                        pe.wait_ge(max_done, b * (G * NCH) + done - 1)
                    width = (i + 1) * P
                    for s, hl in enumerate(heads):
                        dst = bank[:, S1 + done % 2, s * width:(s + 1) * width]
                        nc.tensor.matmul(dst, stack(q_rows, g, hl, QROWS, slice(i * P, (i + 1) * P)),
                                         stack(k_rows, g, hl, QROWS, slice(0, width)), start=True, stop=False)
                        mm = nc.tensor.matmul(dst[:, i * P:], identb[:], mask_qk, start=False, stop=True)
                    mm.then_inc(s1_ready, 1)

            def turn_max(g):
                pe.wait_ge(neg_ready, b * G + g + 1)
                if g > 0:
                    pe.wait_ge(neg_t_ready, b * G + g)
                src = neg_parts[:, g % 2].rearrange("p i j h -> p (i j h)")
                nc.tensor.matmul(bank[0:NQ * PARTS * GH, M_BANK, 0:P], src, identb[:], start=True,
                                 stop=True).then_inc(m_turned, 1)

            def scores(g, hl):
                h = g * GH + hl
                for j in range(NQ):
                    if j == 0 and h > 0:
                        pe.wait_ge(p_a, b * H + h)
                    if j == 2 and h > 0:
                        pe.wait_ge(p_b, b * H + h)
                    width = SEQ - j * P
                    dst = bank[:, S2 + min(j, 2), (2 * P if j == 3 else 0):(2 * P if j == 3 else 0) + width]
                    nc.tensor.matmul(dst, stack(k_rows, g, hl, QROWS + PARTS, slice(j * P, (j + 1) * P)),
                                     stack(q_rows, g, hl, QROWS + PARTS, slice(j * P, SEQ)), start=True, stop=False)
                    mm = nc.tensor.matmul(dst[:, 0:P], identb[:], mask_kq, start=False, stop=True)
                    if j % 2:
                        mm.then_inc((s2a_ready, s2b_ready)[j // 2], 1)

            def values(g, hl):
                h = g * GH + hl
                pe.wait_ge(p_b, b * H + h + 1)
                if hl == 0 and g > 0:
                    pe.wait_ge(avT_ready, b * G + g)
                for j in range(NQ):
                    mm = nc.tensor.matmul(bank[32 * hl:32 * hl + 32, AV_BANK, j * P:SEQ], v_aug[:, g % 2, j, hl, :],
                                          probs[:, h % 2, first[j]:first[j + 1]], start=(j == 0), stop=(j == NQ - 1))
                mm.then_inc(av_done, 1)

            def turn_values(g):
                pe.wait_ge(avT_ready, b * G + g + 1)
                if g > 0:
                    pe.wait_ge(att_done, b * G + g)
                for n in range(NQ):
                    mm = nc.tensor.transpose(bank[:, T_BANK, n * P:(n + 1) * P], avT[:, n * P:(n + 1) * P], ident[:])
                mm.then_inc(av_turned, 1)

            def exp_pass(g, follow):
                pe.wait_ge(m_in, b * (32 * G) + 32 * (g + 1))
                pe.wait_ge(v_set, b * G + g + 1)
                scores(g, 0)
                for hl in range(GH):
                    if hl + 1 < GH:
                        scores(g, hl + 1)
                    values(g, hl)
                    if hl == 0 and g > 0:
                        turn_values(g - 1)
                    if hl == 1 and follow is not None:
                        turn_max(follow)

            pe.wait_ge(result_ready, b + 1)
            max_pass(0)
            max_pass(1)
            turn_max(0)
            for g in range(G):
                exp_pass(g, g + 1 if g + 1 < G else None)
                if g + 2 < G:
                    max_pass(g + 2)
            turn_values(G - 1)
            pe.wait_ge(att_done, b * G + G)
            pe.wait_ge(result_out, 16)
            for n in range(NQ):
                mm = nc.tensor.transpose(bank[:, M_BANK, n * P:(n + 1) * P], att[:, n, :], ident[:])
            mm.then_inc(att_turned, 1)
            pe.wait_ge(attT_ready, b + 1)
            for n in range(NQ):
                mm = nc.tensor.matmul(bank[:, T_BANK, n * P:(n + 1) * P], attT[:, n * P:(n + 1) * P], w_o[:],
                                      start=True, stop=True)
            mm.then_inc(o_ready, 1)

    @block.scalar
    def _(act):
        with act.Fori(0, BATCH) as b:
            for g in range(G):
                if g == 0:
                    act.wait_ge(m_turned, b * G + 1)
                    nc.scalar.copy(neg_t[:, 0, :], bank[0:NQ * PARTS * GH, M_BANK, 0:P]
                                   ).then_inc(neg_t_ready, 1)
                for hl in range(GH):
                    h = g * GH + hl
                    act.wait_ge(s2a_ready, b * H + h + 1)
                    if h >= 2:
                        act.wait_ge(av_done, b * H + h - 1)
                    src = bank[:, S2:S2 + 2, :].rearrange("p a c -> p (a c)")[:, 0:first[2]]
                    nc.scalar.activation(probs[:, h % 2, 0:first[2]], src, ACT.Exp, scale=SCALE).then_inc(p_a, 1)
                    act.wait_ge(s2b_ready, b * H + h + 1)
                    nc.scalar.activation(probs[:, h % 2, first[2]:PCOLS], bank[:, S2 + 2, 0:PCOLS - first[2]],
                                         ACT.Exp, scale=SCALE).then_inc(p_b, 1)
                    if hl == 2 and g + 1 < G:
                        act.wait_ge(m_turned, b * G + g + 2)
                        nc.scalar.copy(neg_t[:, (g + 1) % 2, :],
                                       bank[0:NQ * PARTS * GH, M_BANK, 0:P]).then_inc(neg_t_ready, 1)
                act.wait_ge(av_done, b * H + (g + 1) * GH)
                if g > 0:
                    act.wait_ge(av_turned, b * G + g)
                nc.scalar.copy(avT[:], bank[:, AV_BANK, :]).then_inc(avT_ready, 1)
            act.wait_ge(att_turned, b + 1)
            nc.scalar.copy(attT[:], bank[:, M_BANK, :]).then_inc(attT_ready, 1)

    @block.vector
    def _(dve):
        nc.vector.memset(result[:], 0.0).then_inc(result_ready, 1)
        with dve.Fori(0, BATCH) as b:
            dve.wait_ge(result_ready, b + 1)

            def maxima(g):
                for n, (i, heads) in enumerate(chunks):
                    done = g * NCH + n
                    dve.wait_ge(s1_ready, b * (G * NCH) + done + 1)
                    width = (i + 1) * P
                    src = bank[:, S1 + done % 2, 0:len(heads) * width].rearrange("p (h k) -> p h k", k=width)
                    nc.vector.reduce_max(rowmax[:, g % 2, i, heads[0]:heads[-1] + 1:2], src, AX_X).then_inc(max_done, 1)
                dve.wait_ge(max_done, b * (G * NCH) + (g + 1) * NCH)
                s = b * (4 * G) + 4 * g
                nc.vector.tensor_scalar(negmax[:], rowmax[:, g % 2], -1.0, None, ALU.mult).then_inc(neg_step, 1)
                dve.wait_ge(neg_step, s + 1)
                if g >= 2:
                    dve.wait_ge(m_turned, b * G + g - 1)
                hi, mid, low = (neg_parts[:, g % 2, :, j, :] for j in range(PARTS))
                nc.vector.tensor_copy(hi, negmax[:]).then_inc(neg_step, 1)
                dve.wait_ge(neg_step, s + 2)
                nc.vector.tensor_tensor(negrest[:], negmax[:], hi, ALU.subtract).then_inc(neg_step, 1)
                dve.wait_ge(neg_step, s + 3)
                nc.vector.tensor_copy(mid, negrest[:]).then_inc(neg_step, 1)
                dve.wait_ge(neg_step, s + 4)
                nc.vector.tensor_tensor(low, negrest[:], mid, ALU.subtract).then_inc(neg_ready, 1)
                dve.wait_ge(neg_ready, b * G + g + 1)

            def normalise(g):
                dve.wait_ge(av_turned, b * G + g + 1)
                src = bank[:, T_BANK, :].rearrange("p (n h d) -> p n h d", n=NQ, h=GH)
                nc.vector.reciprocal(inv_sum[:], src[:, :, :, DH]).then_inc(inv_done, 1)
                dve.wait_ge(inv_done, b * G + g + 1)
                dst = att[:, :, g * GH * DH:(g + 1) * GH * DH].rearrange("p n (h d) -> p n h d", h=GH)
                nc.vector.tensor_tensor(dst, src[:, :, :, 0:DH], inv_sum[:].unsqueeze(3).to_broadcast([P, NQ, GH, DH]),
                                        ALU.mult).then_inc(att_done, 1)

            maxima(0)
            maxima(1)
            for g in range(G):
                if g + 2 < G:
                    if g > 0:
                        normalise(g - 1)
                    maxima(g + 2)
                elif g > 0:
                    normalise(g - 1)
            normalise(G - 1)
            dve.wait_ge(o_ready, b + 1)
            dve.wait_ge(result_out, b * 16 + 16)
            nc.vector.tensor_tensor(result[:], xtm[:, bass.ts(b, TPB), :],
                                    bank[:, T_BANK, :].rearrange("p (n c) -> p n c", c=P),
                                    ALU.add).then_inc(result_ready, 1)
        dve.wait_ge(result_ready, BATCH + 1)


def program(nc, D, out):
    with ExitStack() as ctx:
        sb = lambda n, s, d=F32: ctx.enter_context(nc.sbuf_tensor(n, s, d))
        T = {}
        T["xtm"] = sb("xtm", [P, TILES, P])
        T["ident"] = sb("identf", [P, P])
        T["identb"] = sb("identb", [P, P], BF16)
        T["weights_in"] = ctx.enter_context(nc.semaphore("weights_in"))
        T["comb_parts"] = ctx.enter_context(nc.semaphore("comb_parts"))
        with ExitStack() as c0:
            w = lambda n, s, d=F32: c0.enter_context(nc.sbuf_tensor(n, s, d))
            T["xnT"] = w("xnT", [P, BATCH * SEQ])
            T["combT"] = w("combT", [PARTS * EXPERTS, BATCH * SEQ], BF16)
            T["xpad"] = w("xpad", [P, HALVES, PAD + SEQ])
            T["A"] = w("A", [P, HALVES, STATES])
            shapes = {
                "W_in": ([P, 4 * P], F32), "conv_w": ([P, HALVES, TAPS], F32), "conv_b": ([P, HALVES], F32),
                "W_dtr": ([P, HALVES, DT_RANK], F32), "W_bc": ([P, HALVES, PARTS * BC], F32),
                "W_dt": ([DT_RANK, HALVES * P], F32), "b_dt": ([P, HALVES], F32), "D": ([P, HALVES], F32),
                "W_out": ([P, HALVES, P], F32), "sel_bc": ([PARTS * BC, BC, P], BF16),
                "sel_pair": ([PARTS * EXPERTS, PAIRS, P], BF16), "gate_g": ([P, PAIRS, P], F32),
                "gate_v": ([P, PAIRS, P], F32), "down": ([P, PAIRS, P], F32), "shared_gate": ([P, 2 * P], F32),
                "shared_down": ([P, P], F32),
            }
            loads = []
            for name, (shape, dt) in shapes.items():
                T[name] = w(name, shape, dt)
                loads.append((name, T[name][:], D[name]))
            T["weight_loads"], T["n_weights"] = loads, len(loads)
            with ExitStack() as c:
                prologue(nc, D, T, c)
            with ExitStack() as c:
                layer0(nc, T, c)
        with ExitStack() as c1:
            w = lambda n, s, d=F32: c1.enter_context(nc.sbuf_tensor(n, s, d))
            T["v_all"] = w("v_all", [P, TILES, P])
            T["v_aug"] = w("v_aug", [P, 2, TPB, GH, 32])
            T["q_rows"] = w("q_rows", [P, 2, GH // 2, SEQ], BF16)
            T["k_rows"] = w("k_rows", [P, 2, GH // 2, SEQ], BF16)
            T["masks"] = w("masks", [P, 2, P], BF16)
            for name in ("q_stack", "k_stack"):
                T[name] = nc.dram_tensor(name, (BATCH, HEADS, COMBOS, DH, SEQ), BF16, kind="Internal").ap()
            T["m_rows"] = nc.dram_tensor("m_rows", (2, TPB * PARTS * GH, P), BF16, kind="Internal").ap()
            with ExitStack() as c:
                layer1_front(nc, D, T, c)
            with ExitStack() as c:
                attention(nc, D, T, out, c)


def kernel(**inputs):
    import ml_dtypes
    import numpy as np
    import concourse.bacc as bacc
    from concourse import mybir as mb
    from concourse.bass_utils import run_bass_kernel_spmd

    I = {k: np.asarray(v) for k, v in inputs.items()}
    bf16 = ml_dtypes.bfloat16

    def halves(a):
        return a.reshape((HALVES, P) + a.shape[1:]).swapaxes(0, 1)

    ident = np.eye(P, dtype=np.float32)
    sel_bc = np.zeros((PARTS, BC, BC, P), np.float32)
    sel_pair = np.zeros((PARTS, EXPERTS, PAIRS, 2, EH), np.float32)
    for r in range(BC):
        sel_bc[:, r, r, :] = 1
    for e in range(EXPERTS):
        sel_pair[:, e, e // 2, e % 2, :] = 1

    w_x = halves(I["L0_attn_W_x"])
    gate = I["L0_ffn_expert_gate_w"].transpose(1, 0, 2)
    theta = (np.arange(SEQ, dtype=np.float32)[:, None]
             / np.float32(10000.0) ** (np.arange(0, DH, 2, dtype=np.float32) / DH)[None, :])
    spread = lambda t: np.tile(np.repeat(t.T, 2, axis=0), (HEADS, 1))
    sign = np.tile(np.array([-1, 1], np.float32), P // 2)[:, None]
    later = np.triu(np.full((P, P), MASKED, np.float32), k=1)
    ffn = np.stack([I["L1_ffn_w_gate"].T, I["L1_ffn_w_up"].T,
                    I["L1_ffn_w_down"].T.reshape(HID_CHUNKS, P, P).swapaxes(0, 1).reshape(P, HIDDEN)], axis=1)
    arrays = {
        "cos": spread(np.cos(theta)), "sin": spread(np.sin(theta)) * sign,
        "masks": np.stack([later, later.T], axis=1).astype(bf16), "w_ffn": ffn,
        "Aq_t": I["L1_attn_Aq"].T, "Av_t": I["L1_attn_Av"].T, "Bq": I["L1_attn_Bq"], "Bv": I["L1_attn_Bv"],
        "wq": I["L1_attn_wq"], "wk": I["L1_attn_wk"], "wv": I["L1_attn_wv"], "wo": I["L1_attn_wo"],
        "x": I["L0_attn_x"], "W_in": I["L0_attn_W_in"], "conv_w": halves(I["L0_attn_conv_w"][:, 0, :]),
        "conv_b": halves(I["L0_attn_conv_b"]), "W_dtr": w_x[:, :, 0:DT_RANK],
        "W_bc": np.concatenate([w_x[:, :, DT_RANK:]] * PARTS, axis=2), "W_dt": I["L0_attn_W_dt"],
        "b_dt": halves(I["L0_attn_b_dt"]), "a_log": halves(I["L0_attn_A_log"]), "D": halves(I["L0_attn_D"]),
        "W_out": halves(I["L0_attn_W_out"]), "gate_w": I["L0_ffn_gate_w"],
        "gate_bias": np.broadcast_to(I["L0_ffn_gate_bias"][None, :], (P, EXPERTS)),
        "gate_v": gate[:, :, 0:EH].reshape(P, PAIRS, P), "gate_g": gate[:, :, EH:].reshape(P, PAIRS, P),
        "down": I["L0_ffn_expert_down_w"].reshape(PAIRS, P, P).swapaxes(0, 1),
        "shared_gate": I["L0_ffn_shared_gate_w"], "shared_down": I["L0_ffn_shared_down_w"],
        "ident": ident, "identb": ident.astype(bf16), "sel_bc": sel_bc.reshape(PARTS * BC, BC, P).astype(bf16),
        "sel_pair": sel_pair.reshape(PARTS * EXPERTS, PAIRS, P).astype(bf16),
        "iota": np.broadcast_to(np.arange(EXPERTS, dtype=np.float32)[None, :], (P, EXPERTS)),
    }
    nc = bacc.Bacc("TRN2", target_bir_lowering=False, num_devices=1)
    feed, D = {}, {}
    for name, a in arrays.items():
        a = np.ascontiguousarray(a)
        feed["in_" + name] = a
        D[name] = nc.dram_tensor("in_" + name, a.shape, mb.dt.from_np(a.dtype), kind="ExternalInput").ap()
    out = nc.dram_tensor("out_0", (BATCH, SEQ, P), mb.dt.float32, kind="ExternalOutput").ap()
    program(nc, D, out)
    r = run_bass_kernel_spmd(nc, [feed], core_ids=[0])
    return r.results[0]["out_0"]
```

```python
from contextlib import ExitStack

import concourse.bass as bass
from concourse import mybir

F32 = mybir.dt.float32
BF16 = mybir.dt.bfloat16
I32 = mybir.dt.int32
U32 = mybir.dt.uint32
ALU = mybir.AluOpType
ACT = mybir.ActivationFunctionType
AX_X = mybir.AxisListType.X

P = 128
BATCH, SEQ = 4, 512
TILES = BATCH * SEQ // P
TPB = SEQ // P
HALVES = 2
STATES = 16
TAPS = 4
PAD = TAPS - 1
DT_RANK = 8
BC = 2 * STATES
PARTS = 3
EXPERTS, TOPK, EH = 32, 4, 64
PAIRS = EXPERTS // 2
SHARED = PAIRS
EPS = 1e-5
HEADS, DH = 16, 8
GROUPS, GH = 4, 4
COMBOS = 6
QROWS = COMBOS * DH
HIDDEN, HID_CHUNKS = 384, 3
LORA_R, LORA_SCALE = 8, 32.0 / 8.0
QUANT = 1.0 / 127.0
MASKED = -1e30
SCALE = float(DH) ** -0.5




def prepare(nc, D, T, ctx):
    sb = lambda n, s, d=F32: ctx.enter_context(nc.sbuf_tensor(n, s, d))
    sem = lambda n: ctx.enter_context(nc.semaphore(n))
    bank = ctx.enter_context(nc.psum_tensor("bank0", [P, 8, 512], F32))
    XI, RES, DT, BCB, Z = 0, 2, 4, 5, 6
    logits = bank[:, DT, :]
    comb_t = bank[:, 0:2, :].rearrange("p a b -> p (a b)").bitcast(BF16)

    stats = sb("stats", [P, TILES, 6])
    mean_var = sb("mean_var", [P, TILES, 2])
    std = sb("std", [P, TILES])
    rstd = sb("rstd", [P, TILES])
    eps = sb("eps", [P, 1])
    xn = sb("xn", [P, TILES, P])
    gate_w = sb("gate_w", [P, EXPERTS])
    gate_bias = sb("gate_bias", [P, EXPERTS])
    iota = sb("iota", [P, EXPERTS])
    scores = sb("scores", [P, TILES, EXPERTS])
    biased = sb("biased", [P, TILES, EXPERTS])
    top_val = sb("top_val", [P, TILES, 8])
    top_idx = sb("top_idx", [P, TILES, 8], U32)
    top_f = sb("top_f", [P, TILES, 8])
    hit = sb("hit", [P, 2, TILES, EXPERTS])
    wsum = sb("wsum", [P, TILES])
    winv = sb("winv", [P, TILES])
    rest = sb("rest", [P, TILES, EXPERTS])
    parts = sb("parts", [P, TILES, PARTS * EXPERTS], BF16)
    W_in = sb("W_in", [P, 4 * P])
    taps = sb("taps", [P, TAPS, HALVES * P])
    W_tap = sb("W_tap", [P, TAPS, HALVES * P])
    conv_b = sb("conv_b", [P, HALVES])
    W_dtr = sb("W_dtr", [P, HALVES, DT_RANK])
    W_bc = sb("W_bc", [P, HALVES, PARTS * BC])
    W_dt = sb("W_dt", [DT_RANK, HALVES * P])
    b_dt = sb("b_dt", [P, HALVES])
    skip = sb("skip", [P, HALVES])
    dt_low = sb("dt_low", [DT_RANK, SEQ])
    bc_hi = sb("bc_hi", [PARTS * BC, SEQ], BF16)
    bc_mid = sb("bc_mid", [PARTS * BC, SEQ], BF16)
    bc_rest = sb("bc_rest", [PARTS * BC, SEQ])
    softlog = sb("softlog", [P, HALVES, SEQ])
    zpos = sb("zpos", [P, HALVES, SEQ])

    xtm, xnP, combT, A = T["xtm"], T["xnP"], T["combT"], T["A"]
    u, sres, delta, du, bc = T["u"], T["sres"], T["delta"], T["du"], T["bc"]

    x_in = [sem(f"x_in{g}") for g in range(BATCH)]
    small_in, win_in, proj_in = sem("small_in"), sem("win_in"), sem("proj_in")
    eps_set, pads_set, a_ready, a_neg, tap_ready = (sem(n) for n in ("eps_set", "pads_set", "a_ready", "a_neg", "tap_ready"))
    stat_done, aggr_done, std_done, rstd_done, xn_ready, turned, xnT_ready = (sem(n) for n in (
        "stat_done", "aggr_done", "std_done", "rstd_done", "xn_ready", "turned", "xnT_ready"))
    logits_ready, scores_ready, top_done, route, comb_parts, comb_turned, comb_ready = (sem(n) for n in (
        "logits_ready", "scores_ready", "top_done", "route", "comb_parts", "comb_turned", "comb_ready"))
    xi_ready, res_ready, u_ready, sres_ready, dt_ready, dt_low_ready, bc_ready, z_ready = (sem(n) for n in (
        "xi_ready", "res_ready", "u_ready", "sres_ready", "dt_ready", "dt_low_ready", "bc_ready", "z_ready"))
    bc_step, bc_parts, abs_done, expz_done, softlog_ready, zpos_done, delta_ready, du_ready, skip_ready = (
        sem(n) for n in ("bc_step", "bc_parts", "abs_done", "expz_done", "softlog_ready", "zpos_done",
                         "delta_ready", "du_ready", "skip_ready"))
    x_dram = D["x"].rearrange("b (n p) c -> b p n c", p=P)
    small = ((T["ident"], "ident"), (T["identb"], "identb"), (gate_w, "gate_w"), (gate_bias, "gate_bias"),
             (iota, "iota"), (A, "a_log"))
    proj = ((conv_b, "conv_b"), (W_dtr, "W_dtr"), (W_bc, "W_bc"), (W_dt, "W_dt"), (b_dt, "b_dt"), (skip, "D"))
    n_small, n_proj = len(small), len(proj)
    block = ctx.enter_context(nc.Block())

    @block.sync
    def _(sp):
        for b in range(BATCH):
            sp.dma_start(xtm[:, b * TPB:(b + 1) * TPB, :], x_dram[b]).then_inc(x_in[b], 16)
        sp.dma_start(W_in[:], D["W_in"]).then_inc(win_in, 16)
        sp.dma_start(taps[:], D["taps"]).then_inc(win_in, 16)
        for dst, name in proj:
            sp.dma_start(dst[:], D[name]).then_inc(proj_in, 16)
        for dst, src in T["expert_loads"]:
            sp.dma_start(dst, src).then_inc(T["experts_in"], 16)
        sp.wait_ge(T["experts_in"], 16 * len(T["expert_loads"]))

    @block.gpsimd
    def _(pool):
        nc.gpsimd.memset(eps[:], EPS).then_inc(eps_set, 1)
        nc.gpsimd.memset(xnP[:, :, 0:PAD], 0.0).then_inc(pads_set, 1)
        pool.wait_ge(proj_in, 16 * n_proj)
        with pool.Fori(0, BATCH) as b:
            pool.wait_ge(pads_set, 1)
            pool.wait_ge(delta_ready, b + 1)
            nc.gpsimd.tensor_tensor(du[:, b], delta[:, b], u[:, b], ALU.mult).then_inc(du_ready, 1)
            pool.wait_ge(pads_set, 1)
            pool.wait_ge(du_ready, b + 1)
            pool.wait_ge(bc_ready, b + 1)
            nc.gpsimd.tensor_tensor(u[:, b], u[:, b], skip[:].unsqueeze(2).to_broadcast([P, HALVES, SEQ]),
                                    ALU.mult).then_inc(skip_ready, 1)
        pool.wait_ge(skip_ready, BATCH)

    @block.scalar
    def _(act):
        for dst, name in small:
            act.dma_start(dst[:], D[name]).then_inc(small_in, 16)
        act.wait_ge(eps_set, 1)
        for b in range(BATCH):
            t = slice(b * TPB, (b + 1) * TPB)
            act.wait_ge(aggr_done, (b + 1) * TPB)
            nc.scalar.activation(std[:, t], mean_var[:, t, 1], ACT.Sqrt, bias=eps[:]).then_inc(std_done, 1)
        act.wait_ge(small_in, 16 * n_small)
        nc.scalar.activation(A[:], A[:], ACT.Exp).then_inc(a_ready, 1)
        for b in range(BATCH):
            act.wait_ge(turned, b + 1)
            nc.scalar.copy(xnP[:, b, PAD:], bank[:, b, :]).then_inc(xnT_ready, 1)
        act.wait_ge(logits_ready, 1)
        nc.scalar.activation(scores[:].rearrange("p a b -> p (a b)"), logits, ACT.Sigmoid).then_inc(scores_ready, 1)
        act.wait_ge(proj_in, 16 * n_proj)

        def gates(b):
            act.wait_ge(scores_ready, 1)
            act.wait_ge(xi_ready, b + 1)
            for k in range(HALVES):
                ins = nc.scalar.activation(u[:, b, k, :], bank[:, XI + k, :], ACT.Silu, bias=conv_b[:, k:k + 1])
            ins.then_inc(u_ready, 1)
            act.wait_ge(scores_ready, 1)
            act.wait_ge(res_ready, b + 1)
            nc.scalar.activation(sres[:, b], bank[:, RES:RES + 2, :], ACT.Silu).then_inc(sres_ready, 1)

        def low_rank(b):
            act.wait_ge(dt_ready, b + 1)
            nc.scalar.copy(dt_low[:], bank[0:DT_RANK, DT, :]).then_inc(dt_low_ready, 1)

        def soft(b):
            act.wait_ge(z_ready, b + 1)
            if not isinstance(b, int) or b > 0:
                act.wait_ge(delta_ready, b)
            for k in range(HALVES):
                ins = nc.scalar.activation(softlog[:, k, :], bank[:, Z + k, :], ACT.Abs, bias=b_dt[:, k:k + 1])
            ins.then_inc(abs_done, 1)
            act.wait_ge(abs_done, b + 1)
            nc.scalar.activation(softlog[:], softlog[:], ACT.Exp, scale=-1.0).then_inc(expz_done, 1)
            act.wait_ge(expz_done, b + 1)
            nc.scalar.activation(softlog[:], softlog[:], ACT.Ln, bias=1.0).then_inc(softlog_ready, 1)

        gates(0)
        low_rank(0)
        gates(1)
        soft(0)
        with act.Fori(2, BATCH) as b:
            low_rank(b - 1)
            gates(b)
            soft(b - 1)
        low_rank(BATCH - 1)
        soft(BATCH - 1)
        act.wait_ge(comb_turned, 1)
        nc.scalar.copy(combT[:], comb_t[0:PARTS * EXPERTS, :]).then_inc(comb_ready, 1)
        act.wait_ge(comb_ready, 1)

    @block.vector
    def _(dve):
        for b in range(BATCH):
            dve.wait_ge(x_in[b], 16)
            for n in range(b * TPB, (b + 1) * TPB):
                nc.vector.bn_stats(stats[:, n, :], xtm[:, n, :]).then_inc(stat_done, 1)
            for n in range(b * TPB, (b + 1) * TPB):
                dve.wait_ge(stat_done, n + 1)
                nc.vector.bn_aggr(mean_var[:, n, :], stats[:, n, :]).then_inc(aggr_done, 1)
            t = slice(b * TPB, (b + 1) * TPB)
            dve.wait_ge(std_done, b + 1)
            nc.vector.reciprocal(rstd[:, t], std[:, t]).then_inc(rstd_done, 1)
            dve.wait_ge(rstd_done, b + 1)
            for n in range(b * TPB, (b + 1) * TPB):
                last = nc.vector.tensor_scalar(xn[:, n, :], xtm[:, n, :], mean_var[:, n, 0:1], rstd[:, n:n + 1],
                                               ALU.subtract, ALU.mult)
            last.then_inc(xn_ready, 1)
        dve.wait_ge(win_in, 32)
        for k in range(TAPS):
            ins = nc.vector.tensor_tensor(W_tap[:, k, :], W_in[:, 0:HALVES * P], taps[:, k, :], ALU.mult)
        ins.then_inc(tap_ready, 1)
        dve.wait_ge(a_ready, 1)
        nc.vector.tensor_scalar(A[:], A[:], -1.0, None, ALU.mult).then_inc(a_neg, 1)

        dve.wait_ge(scores_ready, 1)
        bias = gate_bias[:].unsqueeze(1).to_broadcast([P, TILES, EXPERTS])
        nc.vector.tensor_tensor(biased[:], scores[:], bias, ALU.add).then_inc(route, 1)
        dve.wait_ge(route, 1)
        for n in range(TILES):
            nc.vector.max(top_val[:, n, :], biased[:, n, :]).then_inc(top_done, 1)
        for n in range(TILES):
            dve.wait_ge(top_done, n + 1)
            nc.vector.max_index(top_idx[:, n, :], top_val[:, n, :], biased[:, n, :]).then_inc(top_done, 1)
        dve.wait_ge(top_done, 2 * TILES)
        nc.vector.tensor_copy(top_f[:], top_idx[:]).then_inc(route, 1)
        dve.wait_ge(route, 2)
        iota_b = iota[:].unsqueeze(1).to_broadcast([P, TILES, EXPERTS])
        step = 2
        for k in range(TOPK):
            chosen = top_f[:, :, k:k + 1].to_broadcast([P, TILES, EXPERTS])
            nc.vector.tensor_tensor(hit[:, min(k, 1)], iota_b, chosen, ALU.is_equal).then_inc(route, 1)
            step += 1
            dve.wait_ge(route, step)
            if k > 0:
                nc.vector.tensor_tensor(hit[:, 0], hit[:, 0], hit[:, 1], ALU.add).then_inc(route, 1)
                step += 1
                dve.wait_ge(route, step)
        nc.vector.tensor_tensor(scores[:], scores[:], hit[:, 0], ALU.mult).then_inc(route, 1)
        dve.wait_ge(route, step + 1)
        nc.vector.reduce_sum(wsum[:], scores[:], AX_X).then_inc(route, 1)
        dve.wait_ge(route, step + 2)
        nc.vector.reciprocal(winv[:], wsum[:]).then_inc(route, 1)
        dve.wait_ge(route, step + 3)
        nc.vector.tensor_tensor(scores[:], scores[:], winv[:].unsqueeze(2).to_broadcast([P, TILES, EXPERTS]),
                                ALU.mult).then_inc(route, 1)
        dve.wait_ge(route, step + 4)
        E = EXPERTS
        nc.vector.tensor_copy(parts[:, :, 0:E], scores[:]).then_inc(route, 1)
        dve.wait_ge(route, step + 5)
        nc.vector.tensor_tensor(rest[:], scores[:], parts[:, :, 0:E], ALU.subtract).then_inc(route, 1)
        dve.wait_ge(route, step + 6)
        nc.vector.tensor_copy(parts[:, :, E:2 * E], rest[:]).then_inc(route, 1)
        dve.wait_ge(route, step + 7)
        nc.vector.tensor_tensor(parts[:, :, 2 * E:3 * E], rest[:], parts[:, :, E:2 * E],
                                ALU.subtract).then_inc(comb_parts, 1)

        with dve.Fori(0, BATCH) as b:
            dve.wait_ge(bc_ready, b + 1)
            src = bank[0:PARTS * BC, BCB, :]
            nc.vector.tensor_copy(bc_hi[:], src).then_inc(bc_step, 1)
            dve.wait_ge(bc_step, b * 5 + 1)
            nc.vector.tensor_tensor(bc_rest[:], src, bc_hi[:], ALU.subtract).then_inc(bc_step, 1)
            nc.vector.tensor_copy(bc[0:BC, b, :], bc_hi[0:BC, :]).then_inc(bc_step, 1)
            dve.wait_ge(bc_step, b * 5 + 2)
            nc.vector.tensor_copy(bc_mid[:], bc_rest[:]).then_inc(bc_step, 1)
            dve.wait_ge(bc_step, b * 5 + 4)
            nc.vector.tensor_copy(bc[BC:2 * BC, b, :], bc_mid[BC:2 * BC, :]).then_inc(bc_step, 1)
            nc.vector.tensor_tensor(bc[2 * BC:, b, :], bc_rest[2 * BC:, :], bc_mid[2 * BC:, :],
                                    ALU.subtract).then_inc(bc_parts, 1)
            dve.wait_ge(abs_done, b + 1)
            for k in range(HALVES):
                ins = nc.vector.tensor_scalar(zpos[:, k, :], bank[:, Z + k, :], b_dt[:, k:k + 1], 0.0,
                                              ALU.add, ALU.max)
            ins.then_inc(zpos_done, 1)
            dve.wait_ge(zpos_done, b + 1)
            dve.wait_ge(softlog_ready, b + 1)
            nc.vector.tensor_tensor(delta[:, b], zpos[:], softlog[:], ALU.add).then_inc(delta_ready, 1)
            dve.wait_ge(delta_ready, b + 1)
        dve.wait_ge(bc_parts, BATCH)

    @block.tensor
    def _(pe):
        pe.wait_ge(small_in, 16 * n_small)
        for b in range(BATCH):
            pe.wait_ge(xn_ready, b + 1)
            for n in range(TPB):
                last = nc.tensor.transpose(bank[:, b, n * P:(n + 1) * P], xn[:, b * TPB + n, :], T["ident"][:])
            last.then_inc(turned, 1)
        for n in range(TILES):
            if n % TPB == 0:
                pe.wait_ge(xnT_ready, n // TPB + 1)
            cols = slice(PAD + (n % TPB) * P, PAD + (n % TPB + 1) * P)
            last = nc.tensor.matmul(logits[:, n * EXPERTS:(n + 1) * EXPERTS], xnP[:, n // TPB, cols], gate_w[:],
                                    start=True, stop=True)
        last.then_inc(logits_ready, 1)
        pe.wait_ge(pads_set, 1)
        pe.wait_ge(proj_in, 16 * n_proj)
        pe.wait_ge(tap_ready, 1)

        def in_proj(b):
            for k in range(HALVES):
                for tap in range(TAPS):
                    mm = nc.tensor.matmul(bank[:, XI + k, :], W_tap[:, tap, k * P:(k + 1) * P],
                                          xnP[:, b, tap:tap + SEQ], start=(tap == 0), stop=(tap == TAPS - 1))
            mm.then_inc(xi_ready, 1)
            for k in range(HALVES):
                mm = nc.tensor.matmul(bank[:, RES + k, :], W_in[:, (2 + k) * P:(3 + k) * P], xnP[:, b, PAD:],
                                      start=True, stop=True)
            mm.then_inc(res_ready, 1)

        def low_rank(b):
            pe.wait_ge(u_ready, b + 1)
            for k in range(HALVES):
                mm = nc.tensor.matmul(bank[0:DT_RANK, DT, :], W_dtr[:, k, :], u[:, b, k, :],
                                      start=(k == 0), stop=(k == 1))
            mm.then_inc(dt_ready, 1)

        def b_and_c(b, first):
            if not first:
                pe.wait_ge(bc_parts, b)
            for k in range(HALVES):
                mm = nc.tensor.matmul(bank[0:PARTS * BC, BCB, :], W_bc[:, k, :], u[:, b, k, :],
                                      start=(k == 0), stop=(k == 1))
            mm.then_inc(bc_ready, 1)

        def z(b, first):
            pe.wait_ge(dt_low_ready, b + 1)
            if not first:
                pe.wait_ge(zpos_done, b)
            for k in range(HALVES):
                mm = nc.tensor.matmul(bank[:, Z + k, :], W_dt[:, k * P:(k + 1) * P], dt_low[:, :],
                                      start=True, stop=True)
            mm.then_inc(z_ready, 1)

        in_proj(0)
        pe.wait_ge(scores_ready, 1)
        low_rank(0)
        pe.wait_ge(sres_ready, 1)
        in_proj(1)
        b_and_c(0, True)
        z(0, True)
        with pe.Fori(2, BATCH) as b:
            low_rank(b - 1)
            pe.wait_ge(sres_ready, b)
            in_proj(b)
            b_and_c(b - 1, False)
            z(b - 1, False)
        low_rank(BATCH - 1)
        b_and_c(BATCH - 1, False)
        z(BATCH - 1, False)
        pe.wait_ge(comb_parts, 1)
        pe.wait_ge(sres_ready, BATCH)
        for n in range(TILES):
            last = nc.tensor.transpose(comb_t[0:PARTS * EXPERTS, n * P:(n + 1) * P], parts[:, n, :], T["identb"][:])
        last.then_inc(comb_turned, 1)


def mix(nc, T, ctx):
    sb = lambda n, s, d=F32: ctx.enter_context(nc.sbuf_tensor(n, s, d))
    sem = lambda n: ctx.enter_context(nc.semaphore(n))
    bank = ctx.enter_context(nc.psum_tensor("bank1", [P, 8, 512], F32))
    B_BANK, C_BANK, V_BANK, W_BANK, G_BANK, O_BANK = 0, 2, 3, 4, 5, 7
    xnP, combT, A, bc = T["xnP"], T["combT"], T["A"], T["bc"]
    acc, sres, delta, du = T["u"], T["sres"], T["delta"], T["du"]
    N, M = STATES, STATES + 1

    dA = sb("dA", [P, 8, HALVES, SEQ])
    dBu = sb("dBu", [P, 2, HALVES, SEQ])
    h = sb("h", [P, 2, HALVES, SEQ])
    hC = sb("hC", [P, 2, HALVES, SEQ])
    silu_g = sb("silu_g", [P, 5, SEQ])
    hidden = sb("hidden", [P, 2, SEQ])
    w_sb = sb("w_sb", [P, 2, SEQ])
    weighted = sb("weighted", [P, 2, SEQ])
    slot = lambda i: 4 if i == SHARED else i % 4

    B_ready, C_ready, g_ready, v_ready, w_ready, w_kept = (sem(n) for n in (
        "B_ready", "C_ready", "g_ready", "v_ready", "w_ready", "w_kept"))
    dA_ready, silu_ready, dBu_done, scan_done, hC_done, hidden_done, weighted_done = (sem(n) for n in (
        "dA_ready", "silu_ready", "dBu_done", "scan_done", "hC_done", "hidden_done", "weighted_done"))
    added, down_done, out_kept, y_done = (sem(n) for n in ("added", "down_done", "out_kept", "y_done"))
    block = ctx.enter_context(nc.Block())

    def batches(eng, body):
        with eng.Fori(0, BATCH - 1) as b:
            body(b, b + 1, False)
        body(BATCH - 1, None, True)

    @block.tensor
    def _(pe):
        pe.wait_ge(T["experts_in"], 16 * len(T["expert_loads"]))

        def xs(b):
            return xnP[:, b, PAD:]

        def spread_b(b, i):
            nc.tensor.matmul(bank[:, B_BANK + i % 2, :], T["sel_bc"][:, i, :], bc[:, b, :], start=True,
                             stop=True).then_inc(B_ready, 1)

        def spread_c(b, i):
            nc.tensor.matmul(bank[:, C_BANK, :], T["sel_bc"][:, N + i, :], bc[:, b, :], start=True,
                             stop=True).then_inc(C_ready, 1)

        def gate(b, i):
            w = T["gate_g"][:, i, :] if i < SHARED else T["shared_gate"][:, P:2 * P]
            nc.tensor.matmul(bank[:, G_BANK + i % 2, :], w, xs(b), start=True, stop=True).then_inc(g_ready, 1)

        def value(b, i):
            w = T["gate_v"][:, i, :] if i < SHARED else T["shared_gate"][:, 0:P]
            nc.tensor.matmul(bank[:, V_BANK, :], w, xs(b), start=True, stop=True).then_inc(v_ready, 1)

        spread_b(0, 0)
        spread_c(0, 0)
        for i in range(4):
            if i >= 2:
                pe.wait_ge(silu_ready, i - 1)
            gate(0, i)
            if i == 0:
                value(0, 0)

        def body(b, nxt, last):
            def down(i):
                if i < SHARED:
                    pe.wait_ge(weighted_done, b * N + i + 1)
                else:
                    pe.wait_ge(hidden_done, b * M + M)
                w = T["down"][:, i, :] if i < SHARED else T["shared_down"][:]
                nc.tensor.matmul(bank[:, O_BANK, :], w, weighted[:, i % 2, :], start=(i == 0),
                                 stop=(i == SHARED)).then_inc(down_done, 1)

            def later_gate(k):
                if k >= M and last:
                    return
                before = k - 2 if k != M else SHARED
                pe.wait_ge(silu_ready, b * M + before + 1)
                if k < M:
                    gate(b, k)
                else:
                    gate(nxt, k - M)

            for i in range(N):
                if i + 1 < N:
                    if i > 0:
                        pe.wait_ge(dBu_done, b * N + i)
                    spread_b(b, i + 1)
                elif not last:
                    pe.wait_ge(dBu_done, b * N + N - 1)
                    spread_b(nxt, 0)
                if i > 0:
                    pe.wait_ge(w_kept, b * N + i)
                nc.tensor.matmul(bank[:, W_BANK, :], T["sel_pair"][:, i, :], combT[:, bass.ts(b, SEQ)],
                                 start=True, stop=True).then_inc(w_ready, 1)
                if i > 0:
                    down(i - 1)
                if i % 4 == 2:
                    later_gate(i + 2)
                    later_gate(i + 3)
                if i % 4 == 3:
                    later_gate(i + 3)
                    later_gate(i + 4)
                    if i == N - 1:
                        later_gate(i + 5)
                pe.wait_ge(hidden_done, b * M + i + 1)
                value(b, i + 1)
                if i + 1 < N:
                    pe.wait_ge(hC_done, b * N + i + 1)
                    spread_c(b, i + 1)
                elif not last:
                    pe.wait_ge(hC_done, b * N + N)
                    spread_c(nxt, 0)
            down(N - 1)
            down(SHARED)
            if not last:
                value(nxt, 0)
                pe.wait_ge(out_kept, b + 1)

        batches(pe, body)

    @block.scalar
    def _(act):
        def decay(b, i):
            for k in range(HALVES):
                ins = nc.scalar.activation(dA[:, i % 8, k, :], delta[:, b, k, :], ACT.Exp, scale=A[:, k, i:i + 1])
            ins.then_inc(dA_ready, 1)

        def silu(i):
            nc.scalar.activation(silu_g[:, slot(i), :], bank[:, G_BANK + i % 2, :], ACT.Silu).then_inc(silu_ready, 1)

        for i in range(4):
            decay(0, i)
        for i in range(4):
            act.wait_ge(g_ready, i + 1)
            silu(i)

        def body(b, nxt, last):
            def later_decay(k):
                if k >= N and last:
                    return
                act.wait_ge(dA_ready, 4)
                if k >= 8:
                    act.wait_ge(scan_done, b * N + k - 7)
                decay(b, k) if k < N else decay(nxt, k - N)

            def later_silu(k):
                if k >= M and last:
                    return
                act.wait_ge(g_ready, b * M + k + 1)
                if k == SHARED:
                    silu(k)
                    return
                before = k - 4 if k < M else k - M + 12
                act.wait_ge(hidden_done, b * M + before + 1)
                silu(k if k < M else k - M)

            for i in range(N):
                act.wait_ge(w_ready, b * N + i + 1)
                if i >= 2:
                    act.wait_ge(weighted_done, b * N + i - 1)
                nc.scalar.copy(w_sb[:, i % 2, :], bank[:, W_BANK, :]).then_inc(w_kept, 1)
                if i % 4 == 0:
                    later_decay(i + 4)
                    later_decay(i + 5)
                if i % 4 == 1:
                    later_decay(i + 5)
                    later_decay(i + 6)
                if i % 4 == 2:
                    later_silu(i + 2)
                    later_silu(i + 3)
                if i % 4 == 3:
                    later_silu(i + 3)
                    later_silu(i + 4)
                    if i == N - 1:
                        later_silu(i + 5)
            act.wait_ge(dA_ready, 4)
            act.wait_ge(down_done, b * M + M)
            nc.scalar.copy(delta[:, b, 0, :], bank[:, O_BANK, :]).then_inc(out_kept, 1)

        batches(act, body)
        act.wait_ge(out_kept, BATCH)

    @block.vector
    def _(dve):
        def spread(n):
            return bank[:, n, :].unsqueeze(1).to_broadcast([P, HALVES, SEQ])

        with dve.Fori(0, BATCH) as b:
            def expert_hidden(i):
                dve.wait_ge(v_ready, b * M + i + 1)
                dve.wait_ge(silu_ready, b * M + i + 1)
                if i >= 2 and i < SHARED:
                    dve.wait_ge(weighted_done, b * N + i - 1)
                if i == SHARED:
                    dve.wait_ge(down_done, b * M + i - 1)
                dst = hidden if i < SHARED else weighted
                nc.vector.tensor_tensor(dst[:, i % 2, :], silu_g[:, slot(i), :], bank[:, V_BANK, :],
                                        ALU.mult).then_inc(hidden_done, 1)

            for i in range(N):
                dve.wait_ge(B_ready, b * N + i + 1)
                nc.vector.tensor_tensor(dBu[:, i % 2], du[:, b], spread(B_BANK + i % 2), ALU.mult).then_inc(dBu_done, 1)
                dve.wait_ge(dBu_done, b * N + i + 1)
                dve.wait_ge(dA_ready, b * N + i + 1)
                for k in range(HALVES):
                    ins = nc.vector.tensor_tensor_scan(h[:, i % 2, k, :], dA[:, i % 8, k, :], dBu[:, i % 2, k, :],
                                                       0.0, ALU.mult, ALU.add)
                ins.then_inc(scan_done, 1)
                expert_hidden(i)
                dve.wait_ge(C_ready, b * N + i + 1)
                dve.wait_ge(scan_done, b * N + i + 1)
                if i >= 2:
                    dve.wait_ge(added, b * N + i - 1)
                nc.vector.tensor_tensor(hC[:, i % 2], h[:, i % 2], spread(C_BANK), ALU.mult).then_inc(hC_done, 1)
            expert_hidden(SHARED)
            dve.wait_ge(y_done, b + 1)

    @block.gpsimd
    def _(pool):
        with pool.Fori(0, BATCH) as b:
            for i in range(N):
                pool.wait_ge(hidden_done, b * M + i + 1)
                pool.wait_ge(w_kept, b * N + i + 1)
                if i >= 2:
                    pool.wait_ge(down_done, b * M + i - 1)
                nc.gpsimd.tensor_tensor(weighted[:, i % 2, :], hidden[:, i % 2, :], w_sb[:, i % 2, :],
                                        ALU.mult).then_inc(weighted_done, 1)
                pool.wait_ge(hC_done, 1)
                pool.wait_ge(hC_done, b * N + i + 1)
                if i > 0:
                    pool.wait_ge(added, b * N + i)
                nc.gpsimd.tensor_tensor(acc[:, b], acc[:, b], hC[:, i % 2], ALU.add).then_inc(added, 1)
            pool.wait_ge(hC_done, 1)
            pool.wait_ge(added, b * N + N)
            nc.gpsimd.tensor_tensor(acc[:, b], acc[:, b], sres[:, b], ALU.mult).then_inc(y_done, 1)
        pool.wait_ge(y_done, BATCH)


def layer1_front(nc, D, T, ctx):
    sb = lambda n, s, d=F32: ctx.enter_context(nc.sbuf_tensor(n, s, d))
    sem = lambda n: ctx.enter_context(nc.semaphore(n))
    bank = ctx.enter_context(nc.psum_tensor("bank2", [P, 8, 512], F32))
    X_BANK, ROT_BANK, VAL_BANK, HG_BANK, HV_BANK = 0, 1, 5, 6, 7
    xtm, ident, v_all = T["xtm"], T["ident"], T["v_all"]

    w_out = sb("w_out", [P, HALVES, P])
    mixed = sb("mixed", [P, SEQ])
    w_int = sb("w_int", [P, 3, HIDDEN], I32)
    w_ffn = sb("w_ffn", [P, 3, HIDDEN])
    lora_a = sb("lora_a", [LORA_R, 2, P])
    lora_b = sb("lora_b", [LORA_R, 2, P])
    w_q = sb("w_q", [P, P])
    w_k = sb("w_k", [P, P])
    w_v = sb("w_v", [P, P])
    w_qs = sb("w_qs", [P, P])
    w_ks = sb("w_ks", [P, P])
    cos = sb("cos", [P, SEQ])
    sin = sb("sin", [P, SEQ])
    eps = sb("eps1", [P, 1])
    mean = sb("mean1", [P, TPB])
    varsum = sb("varsum1", [P, TPB])
    square = sb("square1", [P, TPB, P])
    square_done = sem("square_done")
    std = sb("std1", [P, TPB])
    rstd = sb("rstd1", [P, TPB])
    xn = sb("xn1", [P, TPB, P])
    xnT = sb("xnT1", [P, SEQ])
    silu_g = sb("silu_g1", [P, 2, SEQ])
    hid = sb("hid", [P, HID_CHUNKS, SEQ])
    rot_c = sb("rot_c", [P, 2, SEQ])
    rot_s = sb("rot_s", [P, 2, SEQ])
    qk_parts = sb("qk_parts", [P, 2, PARTS, SEQ], BF16)

    w_in, lora_ready, w_ready, eps_set, w_cast = (sem(n) for n in (
        "w1_in", "lora_ready", "w_ready", "eps1_set", "w_cast"))
    stat_done, aggr_done, std_done, rstd_done, xn_ready, turned, xnT_ready = (sem(n) for n in (
        "stat1_done", "aggr1_done", "std1_done", "rstd1_done", "xn1_ready", "turned1", "xnT1_ready"))
    hg_ready, hv_ready, silu_ready, hid_done, down_ready, front_done = (sem(n) for n in (
        "hg_ready", "hv_ready", "silu1_ready", "hid_done", "down_ready", "front_done"))
    rot_ready, v_ready, v_kept, rot_step, parts_ready, parts_out = (sem(n) for n in (
        "rot_ready", "v1_ready", "v_kept", "rot_step", "parts_ready", "parts_out"))
    mid_done = sem("mid_done")
    mamba_ready, mixed_ready, mixed_turned, x1_ready = (sem(n) for n in (
        "mamba_ready", "mixed_ready", "mixed_turned", "x1_ready"))
    n_w = 11
    block = ctx.enter_context(nc.Block())

    @block.sync
    def _(sp):
        for dst, name in ((w_int[:], "w_ffn"), (lora_a[:, 0, :], "Aq_t"), (lora_a[:, 1, :], "Av_t"),
                          (lora_b[:, 0, :], "Bq"), (lora_b[:, 1, :], "Bv"), (w_q[:], "wq"), (w_k[:], "wk"),
                          (w_v[:], "wv"), (cos[:], "cos"), (sin[:], "sin"), (w_out[:], "W_out")):
            sp.dma_start(dst, D[name]).then_inc(w_in, 16)
        sp.dma_start(T["masks"][:], D["masks"]).then_inc(parts_out, 16)
        with sp.Fori(0, BATCH) as b:
            sp.wait_ge(parts_ready, b + 1)
            for name, k, runs in (("q_stack", 0, ((0, 0, 3), (3, 0, 2), (5, 0, 1))),
                                  ("k_stack", 1, ((0, 0, 1), (1, 0, 1), (2, 0, 1), (3, 1, 1), (4, 1, 1), (5, 2, 1)))):
                for c, part, n in runs:
                    for m in range(n):
                        dst = T[name][b, :, c + m, :, :]
                        sp.dma_start(dst, qk_parts[:, k, part + m, :]).then_inc(parts_out, 16)
        sp.wait_ge(parts_out, 16 + 16 * 2 * COMBOS * BATCH)

    @block.gpsimd
    def _(pool):
        nc.gpsimd.memset(eps[:], EPS).then_inc(eps_set, 1)
        nc.gpsimd.memset(T["v_aug"][:], 0.0).then_inc(eps_set, 1)
        pool.wait_ge(eps_set, 2)
        nc.gpsimd.memset(T["v_aug"][:, :, :, :, DH:DH + 1], 1.0).then_inc(eps_set, 1)
        nc.gpsimd.memset(T["q_rows"][:], 1.0).then_inc(eps_set, 1)
        nc.gpsimd.memset(T["k_rows"][:], 1.0).then_inc(eps_set, 1)
        pool.wait_ge(eps_set, 5)

    @block.scalar
    def _(act):
        act.wait_ge(eps_set, 1)
        act.wait_ge(w_in, 16 * n_w)
        for m in range(3):
            ins = nc.scalar.activation(w_ffn[:, m, :], w_int[:, m, :], ACT.Copy)
        ins.then_inc(w_cast, 1)
        with act.Fori(0, BATCH) as b:
            act.wait_ge(aggr_done, b + 1)
            nc.scalar.activation(std[:], varsum[:], ACT.Sqrt, bias=eps[:], scale=1.0 / P).then_inc(std_done, 1)
            act.wait_ge(turned, b + 1)
            nc.scalar.copy(xnT[:], bank[:, X_BANK, :]).then_inc(xnT_ready, 1)
            for m in range(HID_CHUNKS):
                act.wait_ge(hg_ready, b * HID_CHUNKS + m + 1)
                if m >= 2:
                    act.wait_ge(hid_done, b * HID_CHUNKS + m - 1)
                nc.scalar.activation(silu_g[:, m % 2, :], bank[:, HG_BANK, :], ACT.Silu).then_inc(silu_ready, 1)
            act.wait_ge(v_ready, b + 1)
            nc.scalar.copy(v_all[:, bass.ts(b, TPB), :], bank[:, VAL_BANK, :].rearrange("p (n c) -> p n c", c=P)
                           ).then_inc(v_kept, 1)

    @block.vector
    def _(dve):
        dve.wait_ge(lora_ready, 1)
        for w, k in ((w_q, 0), (w_v, 1)):
            nc.vector.scalar_tensor_tensor(out=w[:], in0=bank[:, 0, k * P:(k + 1) * P], scalar=LORA_SCALE, in1=w[:],
                                           op0=ALU.mult, op1=ALU.add).then_inc(w_ready, 1)
        dve.wait_ge(w_ready, 2)
        for w, ws in ((w_q, w_qs), (w_k, w_ks)):
            nc.vector.tensor_copy(ws[:, 0::2], w[:, 1::2]).then_inc(w_ready, 1)
            nc.vector.tensor_copy(ws[:, 1::2], w[:, 0::2]).then_inc(w_ready, 1)
        dve.wait_ge(w_cast, 1)
        nc.vector.tensor_scalar(w_ffn[:], w_ffn[:], QUANT, None, ALU.mult).then_inc(w_ready, 1)
        nc.vector.memset(mean[:], 0.0).then_inc(front_done, 1)
        with dve.Fori(0, BATCH) as b:
            dve.wait_ge(front_done, b + 1)
            dve.wait_ge(mamba_ready, b + 1)
            nc.vector.tensor_tensor(mixed[:], T["delta"][:, b, 0, :], bank[:, X_BANK, :], ALU.add).then_inc(mixed_ready, 1)
            dve.wait_ge(mixed_turned, b + 1)
            xs = xtm[:, bass.ts(b, TPB), :]
            nc.vector.tensor_tensor(xs, xs, bank[:, ROT_BANK, :].rearrange("p (n c) -> p n c", c=P),
                                    ALU.add).then_inc(x1_ready, 1)
            dve.wait_ge(lora_ready, 1)
            dve.wait_ge(x1_ready, b + 1)
            column = lambda t: t[:].unsqueeze(2).to_broadcast([P, TPB, P])
            nc.vector.reduce_sum(mean[:], xtm[:, bass.ts(b, TPB), :], AX_X).then_inc(stat_done, 1)
            dve.wait_ge(stat_done, b * 3 + 1)
            nc.vector.tensor_scalar(mean[:], mean[:], 1.0 / P, None, ALU.mult).then_inc(stat_done, 1)
            dve.wait_ge(stat_done, b * 3 + 2)
            nc.vector.tensor_tensor(xn[:], xtm[:, bass.ts(b, TPB), :], column(mean), ALU.subtract).then_inc(stat_done, 1)
            dve.wait_ge(stat_done, b * 3 + 3)
            nc.vector.tensor_tensor(square[:], xn[:], xn[:], ALU.mult).then_inc(square_done, 1)
            dve.wait_ge(square_done, b + 1)
            nc.vector.reduce_sum(varsum[:], square[:], AX_X).then_inc(aggr_done, 1)
            dve.wait_ge(std_done, b + 1)
            nc.vector.reciprocal(rstd[:], std[:]).then_inc(rstd_done, 1)
            dve.wait_ge(rstd_done, b + 1)
            nc.vector.tensor_tensor(xn[:], xn[:], column(rstd), ALU.mult).then_inc(xn_ready, 1)

            def hidden(m):
                dve.wait_ge(silu_ready, b * HID_CHUNKS + m + 1)
                dve.wait_ge(hv_ready, b * HID_CHUNKS + m + 1)
                nc.vector.tensor_tensor(hid[:, m, :], silu_g[:, m % 2, :], bank[:, HV_BANK, :],
                                        ALU.mult).then_inc(hid_done, 1)

            hidden(0)
            dve.wait_ge(rot_ready, b + 1)
            table = lambda t: t[:].unsqueeze(1).to_broadcast([P, 2, SEQ])
            nc.vector.tensor_tensor(rot_c[:], bank[:, ROT_BANK:ROT_BANK + 2, :], table(cos), ALU.mult).then_inc(rot_step, 1)
            hidden(1)
            nc.vector.tensor_tensor(rot_s[:], bank[:, ROT_BANK + 2:ROT_BANK + 4, :], table(sin),
                                    ALU.mult).then_inc(rot_step, 1)
            hidden(2)
            dve.wait_ge(rot_step, b * 5 + 2)
            nc.vector.tensor_tensor(rot_c[:], rot_c[:], rot_s[:], ALU.add).then_inc(rot_step, 1)
            dve.wait_ge(rot_step, b * 5 + 3)
            dve.wait_ge(parts_out, b * (16 * 2 * COMBOS) + 16)
            hi, mid, low = (qk_parts[:, :, m, :] for m in range(PARTS))
            nc.vector.tensor_copy(hi, rot_c[:]).then_inc(rot_step, 1)
            dve.wait_ge(rot_step, b * 5 + 4)
            nc.vector.tensor_tensor(rot_s[:], rot_c[:], hi, ALU.subtract).then_inc(rot_step, 1)
            dve.wait_ge(rot_step, b * 5 + 5)
            nc.vector.tensor_copy(mid, rot_s[:]).then_inc(mid_done, 1)
            dve.wait_ge(mid_done, b + 1)
            nc.vector.tensor_tensor(low, rot_s[:], mid, ALU.subtract).then_inc(parts_ready, 1)
            dve.wait_ge(down_ready, b + 1)
            xs = xtm[:, bass.ts(b, TPB), :]
            nc.vector.tensor_tensor(xs, xs, bank[:, X_BANK, :].rearrange("p (n c) -> p n c", c=P),
                                    ALU.add).then_inc(front_done, 1)
        dve.wait_ge(front_done, BATCH + 1)

    @block.tensor
    def _(pe):
        pe.wait_ge(w_in, 16 * n_w)
        for k in range(2):
            mm = nc.tensor.matmul(bank[:, 0, k * P:(k + 1) * P], lora_a[:, k, :], lora_b[:, k, :],
                                  start=True, stop=True)
        mm.then_inc(lora_ready, 1)
        pe.wait_ge(w_ready, 7)
        with pe.Fori(0, BATCH) as b:
            pe.wait_ge(front_done, b + 1)
            for k in range(HALVES):
                mm = nc.tensor.matmul(bank[:, X_BANK, :], w_out[:, k, :], T["u"][:, b, k, :],
                                      start=(k == 0), stop=(k == 1))
            mm.then_inc(mamba_ready, 1)
            pe.wait_ge(mixed_ready, b + 1)
            for n in range(TPB):
                mm = nc.tensor.transpose(bank[:, ROT_BANK, n * P:(n + 1) * P], mixed[:, n * P:(n + 1) * P], ident[:])
            mm.then_inc(mixed_turned, 1)
            pe.wait_ge(xn_ready, b + 1)
            for n in range(TPB):
                mm = nc.tensor.transpose(bank[:, X_BANK, n * P:(n + 1) * P], xn[:, n, :], ident[:])
            mm.then_inc(turned, 1)
            pe.wait_ge(xnT_ready, b + 1)

            def hidden(m):
                if m:
                    pe.wait_ge(silu_ready, b * HID_CHUNKS + m)
                nc.tensor.matmul(bank[:, HG_BANK, :], w_ffn[:, 0, m * P:(m + 1) * P], xnT[:], start=True,
                                 stop=True).then_inc(hg_ready, 1)
                if m:
                    pe.wait_ge(hid_done, b * HID_CHUNKS + m)
                nc.tensor.matmul(bank[:, HV_BANK, :], w_ffn[:, 1, m * P:(m + 1) * P], xnT[:], start=True,
                                 stop=True).then_inc(hv_ready, 1)

            hidden(0)
            for k, w in enumerate((w_q, w_k, w_qs, w_ks)):
                mm = nc.tensor.matmul(bank[:, ROT_BANK + k, :], w[:], xnT[:], start=True, stop=True)
            mm.then_inc(rot_ready, 1)
            hidden(1)
            for n in range(TPB):
                mm = nc.tensor.matmul(bank[:, VAL_BANK, n * P:(n + 1) * P], xnT[:, n * P:(n + 1) * P], w_v[:],
                                      start=True, stop=True)
            mm.then_inc(v_ready, 1)
            hidden(2)
            pe.wait_ge(hid_done, b * HID_CHUNKS + HID_CHUNKS)
            for n in range(TPB):
                for m in range(HID_CHUNKS):
                    mm = nc.tensor.matmul(bank[:, X_BANK, n * P:(n + 1) * P], hid[:, m, n * P:(n + 1) * P],
                                          w_ffn[:, 2, m * P:(m + 1) * P], start=(m == 0), stop=(m == HID_CHUNKS - 1))
            mm.then_inc(down_ready, 1)


def attention(nc, D, T, out, ctx):
    sb = lambda n, s, d=F32: ctx.enter_context(nc.sbuf_tensor(n, s, d))
    sem = lambda n: ctx.enter_context(nc.semaphore(n))
    bank = ctx.enter_context(nc.psum_tensor("bank3", [P, 8, 512], F32))
    S1, S2, AV_BANK, M_BANK, T_BANK = 0, 2, 5, 6, 7
    xtm, ident, identb = T["xtm"], T["ident"], T["identb"]
    q_rows, k_rows, v_aug, v_all = T["q_rows"], T["k_rows"], T["v_aug"], T["v_all"]
    mask_qk, mask_kq = T["masks"][:, 0, :], T["masks"][:, 1, :]
    NQ = TPB
    PCOLS = sum(SEQ - j * P for j in range(NQ))
    first = [sum(SEQ - i * P for i in range(j)) for j in range(NQ + 1)]
    PAIR = GH // 2

    w_o = sb("w_o", [P, P])
    rowmax = sb("rowmax", [P, NQ, 2, PAIR])
    negmax = sb("negmax", [P, NQ, 2, PAIR])
    negrest = sb("negrest", [P, NQ, 2, PAIR])
    neg_parts = sb("neg_parts", [P, 2, NQ, 2, PARTS, PAIR], BF16)
    neg_t = sb("neg_t", [2 * PARTS * PAIR, 2, SEQ], BF16)
    probs = sb("probs", [P, 2, PCOLS])
    avT = sb("avT", [P, SEQ])
    inv_sum = sb("inv_sum", [P, NQ, GH])
    att = sb("att", [P, NQ, P])
    attT = sb("attT", [P, SEQ])
    result = sb("result", [P, NQ, P])

    stack_in = [sem(f"stack_in{k}") for k in range(GROUPS)]
    m_in = [sem(f"m_in{k}") for k in range(2)]
    s1_ready, max_done, neg_step, neg_ready, m_turned, neg_t_ready = (sem(n) for n in (
        "s1_ready", "max_done", "neg_step", "neg_ready", "m_turned", "neg_t_ready"))
    v_set, s2a_ready, s2b_ready, p_a, p_b, av_done, avT_ready, av_turned, inv_done, att_done = (sem(n) for n in (
        "v_set", "s2a_ready", "s2b_ready", "p_a", "p_b", "av_done", "avT_ready", "av_turned", "inv_done", "att_done"))
    att_turned, attT_ready, o_ready, result_ready, result_out = (sem(n) for n in (
        "att_turned", "attT_ready", "o_ready", "result_ready", "result_out"))

    chunks = ([(i, heads) for i in (0, 1) for heads in ((0, 2), (1, 3))]
              + [(i, (hl,)) for i in (2, 3) for hl in range(GH)])
    NCH = len(chunks)
    PER_SLOT = NCH // GH
    G, H = GROUPS, HEADS
    out_dram = out.rearrange("b (n p) c -> b p n c", p=P)
    block = ctx.enter_context(nc.Block())

    def stages(eng, stage):
        stage(0, 0, True, False)
        with eng.Fori(0, BATCH - 1) as b:
            for g in range(1, G + 1):
                stage(b, g, True, False)
        for g in range(1, G + 1):
            stage(BATCH - 1, g, g < G, True)

    @block.sync
    def _(sp):
        sp.dma_start(w_o[:], D["wo"]).then_inc(result_out, 16)

        def load_stack(b, g):
            for par in range(2):
                for rows, name in ((q_rows, "q_stack"), (k_rows, "k_stack")):
                    src = T[name][b].rearrange("h c r t -> h (c r) t")
                    src = src[GH * g + par:GH * (g + 1):2].rearrange("h r t -> r h t")
                    sp.dma_start(rows[64 * par:64 * par + QROWS, g, :, :], src).then_inc(stack_in[g], 16)

        def place_max(b, g):
            sp.wait_ge(neg_t_ready, b * G + g + 1)
            for par in range(2):
                dst = q_rows[64 * par + QROWS:64 * par + QROWS + PARTS, g % G, :, :]
                rows = slice(par * PARTS * PAIR, (par + 1) * PARTS * PAIR)
                sp.dma_start(dst, neg_t[rows, g % 2, :]).then_inc(m_in[g % 2], 16)

        def stage(b, g, run, last):
            if not (last and g + 3 >= G):
                if g > 0:
                    sp.wait_ge(s2b_ready, b * H + g * GH)
                load_stack(b + (g + 3) // G, (g + 3) % G)
            if not (last and g + 1 >= G):
                place_max(b, g + 1)
            if g == G:
                sp.wait_ge(result_ready, b + 2)
                sp.dma_start(out_dram[b], result[:]).then_inc(result_out, 16)

        for g in range(3):
            load_stack(0, g)
        place_max(0, 0)
        stages(sp, stage)
        sp.wait_ge(result_out, 16 + 16 * BATCH)

    @block.gpsimd
    def _(pool):
        def set_values(b, g):
            for hl in range(GH):
                c = (GH * (g % G) + hl) * DH
                ins = nc.gpsimd.tensor_copy(v_aug[:, g % 2, :, hl, 0:DH],
                                            v_all[:, bass.ts(b + g // G, TPB), c:c + DH])
            ins.then_inc(v_set, 1)

        def stage(b, g, run, last):
            if last and g + 1 >= G:
                return
            if g > 0:
                pool.wait_ge(av_done, b * H + g * GH)
            set_values(b, g + 1)

        set_values(0, 0)
        stages(pool, stage)
        pool.wait_ge(v_set, BATCH * G)

    @block.tensor
    def _(pe):
        def stack(t, g, hl, rows, cols):
            lo = 64 * (hl % 2)
            return t[lo:lo + rows, g % G, hl // 2, cols]

        def max_chunk(b, g, n):
            if n == 0:
                pe.wait_ge(stack_in[g % G], (b + g // G + 1) * 64)
            i, heads = chunks[n]
            done = g * NCH + n
            if not isinstance(b, int) or b * G * NCH + done >= 2:
                pe.wait_ge(max_done, b * (G * NCH) + done - 1)
            width = (i + 1) * P
            for s, hl in enumerate(heads):
                dst = bank[:, S1 + done % 2, s * width:(s + 1) * width]
                nc.tensor.matmul(dst, stack(q_rows, g, hl, QROWS, slice(i * P, (i + 1) * P)),
                                 stack(k_rows, g, hl, QROWS, slice(0, width)), start=True, stop=False)
                mm = nc.tensor.matmul(dst[:, i * P:], identb[:], mask_qk, start=False, stop=True)
            mm.then_inc(s1_ready, 1)

        def turn_max(b, g):
            pe.wait_ge(neg_ready, b * G + g + 1)
            if not isinstance(b, int) or b * G + g > 0:
                pe.wait_ge(neg_t_ready, b * G + g)
            for i in range(NQ):
                src = neg_parts[:, g % 2, i].rearrange("p a j h -> p (a j h)")
                mm = nc.tensor.matmul(bank[0:2 * PARTS * PAIR, M_BANK, i * P:(i + 1) * P], src, identb[:],
                                      start=True, stop=True)
            mm.then_inc(m_turned, 1)

        def scores(b, g, hl, half):
            h = g * GH + hl
            if hl == 0 and half == 0:
                pe.wait_ge(m_in[g % 2], b * (16 * G) + 32 * (g // 2 + 1))
            if not isinstance(b, int) or b * H + h > 0:
                pe.wait_ge((p_a, p_b)[half], b * H + h)
            for j in (2 * half, 2 * half + 1):
                width = SEQ - j * P
                at = 2 * P if j == 3 else 0
                dst = bank[:, S2 + min(j, 2), at:at + width]
                nc.tensor.matmul(dst, stack(k_rows, g, hl, QROWS + PARTS, slice(j * P, (j + 1) * P)),
                                 stack(q_rows, g, hl, QROWS + PARTS, slice(j * P, SEQ)), start=True, stop=False)
                mm = nc.tensor.matmul(dst[:, 0:P], identb[:], mask_kq, start=False, stop=True)
            mm.then_inc((s2a_ready, s2b_ready)[half], 1)

        def values(b, g, hl):
            h = g * GH + hl
            if hl == 0:
                pe.wait_ge(v_set, b * G + g + 1)
                if g > 0:
                    pe.wait_ge(avT_ready, b * G + g)
            pe.wait_ge(p_b, b * H + h + 1)
            for j in range(NQ):
                mm = nc.tensor.matmul(bank[32 * hl:32 * hl + 32, AV_BANK, j * P:SEQ], v_aug[:, g % 2, j, hl, :],
                                      probs[:, h % 2, first[j]:first[j + 1]], start=(j == 0), stop=(j == NQ - 1))
            mm.then_inc(av_done, 1)

        def turn_values(b, g):
            pe.wait_ge(avT_ready, b * G + g + 1)
            if g > 0:
                pe.wait_ge(att_done, b * G + g)
            else:
                pe.wait_ge(result_ready, b + 1)
            for n in range(NQ):
                mm = nc.tensor.transpose(bank[:, T_BANK, n * P:(n + 1) * P], avT[:, n * P:(n + 1) * P], ident[:])
            mm.then_inc(av_turned, 1)

        def turn_att(b):
            pe.wait_ge(att_done, b * G + G)
            for n in range(NQ):
                mm = nc.tensor.transpose(bank[:, M_BANK, n * P:(n + 1) * P], att[:, n, :], ident[:])
            mm.then_inc(att_turned, 1)

        def project(b):
            pe.wait_ge(attT_ready, b + 1)
            for n in range(NQ):
                mm = nc.tensor.matmul(bank[:, T_BANK, n * P:(n + 1) * P], attT[:, n * P:(n + 1) * P], w_o[:],
                                      start=True, stop=True)
            mm.then_inc(o_ready, 1)

        def stage(b, g, run, last):
            ahead = not (last and g + 2 >= G)
            for hl in range(GH):
                n = hl * PER_SLOT
                if run:
                    follow = (g, hl + 1) if hl + 1 < GH else (g + 1, 0)
                    if last and follow[0] >= G:
                        follow = None
                    if follow:
                        scores(b, *follow, 0)
                    if ahead:
                        max_chunk(b, g + 2, n)
                    if follow:
                        scores(b, *follow, 1)
                    if ahead:
                        max_chunk(b, g + 2, n + 1)
                    values(b, g, hl)
                    if ahead:
                        max_chunk(b, g + 2, n + 2)
                if hl == 0 and not (last and g + 1 >= G):
                    turn_max(b, g + 1)
                if hl == 1 and g > 0:
                    turn_values(b, g - 1)
                if hl == 2 and g == G:
                    if not last:
                        pe.wait_ge(neg_t_ready, b * G + g + 2)
                    turn_att(b)
                if hl == 3 and g == G:
                    project(b)

        pe.wait_ge(result_out, 16)
        for g in range(2):
            for n in range(NCH):
                max_chunk(0, g, n)
            if g == 0:
                turn_max(0, 0)
        scores(0, 0, 0, 0)
        scores(0, 0, 0, 1)
        stages(pe, stage)

    @block.scalar
    def _(act):
        def keep_max(b, g):
            act.wait_ge(m_turned, b * G + g + 1)
            if not isinstance(b, int) or b * G + g >= 2:
                act.wait_ge(m_in[g % 2], b * (16 * G) + 32 * (g // 2))
            nc.scalar.copy(neg_t[:, g % 2, :], bank[0:2 * PARTS * PAIR, M_BANK, :]).then_inc(neg_t_ready, 1)

        def exps(b, g, hl):
            h = g * GH + hl
            act.wait_ge(s2a_ready, b * H + h + 1)
            if not isinstance(b, int) or b * H + h >= 2:
                act.wait_ge(av_done, b * H + h - 1)
            src = bank[:, S2:S2 + 2, :].rearrange("p a c -> p (a c)")[:, 0:first[2]]
            nc.scalar.activation(probs[:, h % 2, 0:first[2]], src, ACT.Exp, scale=SCALE).then_inc(p_a, 1)
            act.wait_ge(s2b_ready, b * H + h + 1)
            nc.scalar.activation(probs[:, h % 2, first[2]:PCOLS], bank[:, S2 + 2, 0:PCOLS - first[2]],
                                 ACT.Exp, scale=SCALE).then_inc(p_b, 1)

        def stage(b, g, run, last):
            for hl in range(GH):
                if run:
                    exps(b, g, hl)
                if hl == 0 and g > 0:
                    act.wait_ge(av_done, b * H + g * GH)
                    if g > 1:
                        act.wait_ge(av_turned, b * G + g - 1)
                    nc.scalar.copy(avT[:], bank[:, AV_BANK, :]).then_inc(avT_ready, 1)
                if hl == 1 and not (last and g + 1 >= G):
                    keep_max(b, g + 1)
                if hl == 3 and g == G:
                    act.wait_ge(att_turned, b + 1)
                    nc.scalar.copy(attT[:], bank[:, M_BANK, :]).then_inc(attT_ready, 1)

        keep_max(0, 0)
        stages(act, stage)

    @block.vector
    def _(dve):
        nc.vector.memset(result[:], 0.0).then_inc(result_ready, 1)

        def reduce_chunk(b, g, n):
            i, heads = chunks[n]
            done = g * NCH + n
            dve.wait_ge(s1_ready, b * (G * NCH) + done + 1)
            width = (i + 1) * P
            src = bank[:, S1 + done % 2, 0:len(heads) * width].rearrange("p (h k) -> p h k", k=width)
            dst = rowmax[:, i, heads[0] % 2, heads[0] // 2:heads[-1] // 2 + 1]
            nc.vector.reduce_max(dst, src, AX_X).then_inc(max_done, 1)

        def split_max(b, g):
            dve.wait_ge(max_done, b * (G * NCH) + (g + 1) * NCH)
            s = 4 * g
            nc.vector.tensor_scalar(negmax[:], rowmax[:], -1.0, None, ALU.mult).then_inc(neg_step, 1)
            dve.wait_ge(neg_step, b * (4 * G) + s + 1)
            if not isinstance(b, int) or b * G + g >= 2:
                dve.wait_ge(m_turned, b * G + g - 1)
            hi, mid, low = (neg_parts[:, g % 2, :, :, j, :] for j in range(PARTS))
            nc.vector.tensor_copy(hi, negmax[:]).then_inc(neg_step, 1)
            dve.wait_ge(neg_step, b * (4 * G) + s + 2)
            nc.vector.tensor_tensor(negrest[:], negmax[:], hi, ALU.subtract).then_inc(neg_step, 1)
            dve.wait_ge(neg_step, b * (4 * G) + s + 3)
            nc.vector.tensor_copy(mid, negrest[:]).then_inc(neg_step, 1)
            dve.wait_ge(neg_step, b * (4 * G) + s + 4)
            nc.vector.tensor_tensor(low, negrest[:], mid, ALU.subtract).then_inc(neg_ready, 1)

        def normalise(b, g):
            dve.wait_ge(av_turned, b * G + g + 1)
            src = bank[:, T_BANK, :].rearrange("p (n h d) -> p n h d", n=NQ, h=GH)
            nc.vector.reciprocal(inv_sum[:], src[:, :, :, DH]).then_inc(inv_done, 1)
            dve.wait_ge(inv_done, b * G + g + 1)
            dst = att[:, :, g * GH * DH:(g + 1) * GH * DH].rearrange("p n (h d) -> p n h d", h=GH)
            nc.vector.tensor_tensor(dst, src[:, :, :, 0:DH], inv_sum[:].unsqueeze(3).to_broadcast([P, NQ, GH, DH]),
                                    ALU.mult).then_inc(att_done, 1)

        def stage(b, g, run, last):
            ahead = not (last and g + 2 >= G)
            for n in range(NCH):
                if ahead:
                    reduce_chunk(b, g + 2, n)
                if n == 2 * PER_SLOT - 1 and g > 0:
                    normalise(b, g - 1)
            if ahead:
                split_max(b, g + 2)
            if g == G:
                dve.wait_ge(o_ready, b + 1)
                dve.wait_ge(result_out, b * 16 + 16)
                nc.vector.tensor_tensor(result[:], xtm[:, bass.ts(b, TPB), :],
                                        bank[:, T_BANK, :].rearrange("p (n c) -> p n c", c=P),
                                        ALU.add).then_inc(result_ready, 1)

        for g in range(2):
            for n in range(NCH):
                reduce_chunk(0, g, n)
            split_max(0, g)
        stages(dve, stage)
        dve.wait_ge(result_ready, BATCH + 1)


def program(nc, D, out):
    with ExitStack() as ctx:
        T = {}

        def tensors(stack, table):
            for name, (shape, dt) in table.items():
                T[name] = stack.enter_context(nc.sbuf_tensor(name, shape, dt))

        tensors(ctx, {
            "xtm": ([P, TILES, P], F32), "ident": ([P, P], F32), "identb": ([P, P], BF16),
            "u": ([P, BATCH, HALVES, SEQ], F32), "delta": ([P, BATCH, HALVES, SEQ], F32)})
        T["experts_in"] = ctx.enter_context(nc.semaphore("experts_in"))
        with ExitStack() as layer0:
            loaded = {
                "sel_bc": ([PARTS * BC, BC, P], BF16), "sel_pair": ([PARTS * EXPERTS, PAIRS, P], BF16),
                "gate_g": ([P, PAIRS, P], F32), "gate_v": ([P, PAIRS, P], F32), "down": ([P, PAIRS, P], F32),
                "shared_gate": ([P, 2 * P], F32), "shared_down": ([P, P], F32)}
            tensors(layer0, loaded)
            tensors(layer0, {
                "xnP": ([P, BATCH, PAD + SEQ], F32), "combT": ([PARTS * EXPERTS, BATCH * SEQ], BF16),
                "A": ([P, HALVES, STATES], F32), "sres": ([P, BATCH, HALVES, SEQ], F32),
                "du": ([P, BATCH, HALVES, SEQ], F32), "bc": ([PARTS * BC, BATCH, SEQ], BF16)})
            T["expert_loads"] = [(T[name][:], D[name]) for name in loaded]
            with ExitStack() as stage:
                prepare(nc, D, T, stage)
            with ExitStack() as stage:
                mix(nc, T, stage)
        with ExitStack() as layer1:
            tensors(layer1, {
                "v_all": ([P, TILES, P], F32), "v_aug": ([P, 2, TPB, GH, 32], F32),
                "q_rows": ([P, GROUPS, GH // 2, SEQ], BF16), "k_rows": ([P, GROUPS, GH // 2, SEQ], BF16),
                "masks": ([P, 2, P], BF16)})
            for name in ("q_stack", "k_stack"):
                T[name] = nc.dram_tensor(name, (BATCH, HEADS, COMBOS, DH, SEQ), BF16, kind="Internal").ap()
            with ExitStack() as stage:
                layer1_front(nc, D, T, stage)
            with ExitStack() as stage:
                attention(nc, D, T, out, stage)


def kernel(**inputs):
    import ml_dtypes
    import numpy as np
    import concourse.bacc as bacc
    from concourse import mybir as mb
    from concourse.bass_utils import run_bass_kernel_spmd

    I = {k: np.asarray(v) for k, v in inputs.items()}
    bf16 = ml_dtypes.bfloat16

    def halves(a):
        return a.reshape((HALVES, P) + a.shape[1:]).swapaxes(0, 1)

    ident = np.eye(P, dtype=np.float32)
    sel_bc = np.zeros((PARTS, BC, BC, P), np.float32)
    sel_pair = np.zeros((PARTS, EXPERTS, PAIRS, 2, EH), np.float32)
    for r in range(BC):
        sel_bc[:, r, r, :] = 1
    for e in range(EXPERTS):
        sel_pair[:, e, e // 2, e % 2, :] = 1

    w_x = halves(I["L0_attn_W_x"])
    gate = I["L0_ffn_expert_gate_w"].transpose(1, 0, 2)
    theta = (np.arange(SEQ, dtype=np.float32)[:, None]
             / np.float32(10000.0) ** (np.arange(0, DH, 2, dtype=np.float32) / DH)[None, :])
    spread = lambda t: np.tile(np.repeat(t.T, 2, axis=0), (HEADS, 1))
    sign = np.tile(np.array([-1, 1], np.float32), P // 2)[:, None]
    later = np.triu(np.full((P, P), MASKED, np.float32), k=1)
    ffn = np.stack([I["L1_ffn_w_gate"].T, I["L1_ffn_w_up"].T,
                    I["L1_ffn_w_down"].T.reshape(HID_CHUNKS, P, P).swapaxes(0, 1).reshape(P, HIDDEN)], axis=1)
    arrays = {
        "cos": spread(np.cos(theta)), "sin": spread(np.sin(theta)) * sign,
        "masks": np.stack([later, later.T], axis=1).astype(bf16), "w_ffn": ffn,
        "Aq_t": I["L1_attn_Aq"].T, "Av_t": I["L1_attn_Av"].T, "Bq": I["L1_attn_Bq"], "Bv": I["L1_attn_Bv"],
        "wq": I["L1_attn_wq"], "wk": I["L1_attn_wk"], "wv": I["L1_attn_wv"], "wo": I["L1_attn_wo"],
        "x": I["L0_attn_x"], "W_in": I["L0_attn_W_in"], 
        "taps": np.broadcast_to(I["L0_attn_conv_w"][:, 0, :].T[None], (P, TAPS, HALVES * P)),
        "conv_b": halves(I["L0_attn_conv_b"]), "W_dtr": w_x[:, :, 0:DT_RANK],
        "W_bc": np.concatenate([w_x[:, :, DT_RANK:]] * PARTS, axis=2), "W_dt": I["L0_attn_W_dt"],
        "b_dt": halves(I["L0_attn_b_dt"]), "a_log": halves(I["L0_attn_A_log"]), "D": halves(I["L0_attn_D"]),
        "W_out": halves(I["L0_attn_W_out"]), "gate_w": I["L0_ffn_gate_w"],
        "gate_bias": np.broadcast_to(I["L0_ffn_gate_bias"][None, :], (P, EXPERTS)),
        "gate_v": gate[:, :, 0:EH].reshape(P, PAIRS, P), "gate_g": gate[:, :, EH:].reshape(P, PAIRS, P),
        "down": I["L0_ffn_expert_down_w"].reshape(PAIRS, P, P).swapaxes(0, 1),
        "shared_gate": I["L0_ffn_shared_gate_w"], "shared_down": I["L0_ffn_shared_down_w"],
        "ident": ident, "identb": ident.astype(bf16), "sel_bc": sel_bc.reshape(PARTS * BC, BC, P).astype(bf16),
        "sel_pair": sel_pair.reshape(PARTS * EXPERTS, PAIRS, P).astype(bf16),
        "iota": np.broadcast_to(np.arange(EXPERTS, dtype=np.float32)[None, :], (P, EXPERTS)),
    }
    nc = bacc.Bacc("TRN2", target_bir_lowering=False, num_devices=1)
    feed, D = {}, {}
    for name, a in arrays.items():
        a = np.ascontiguousarray(a)
        feed["in_" + name] = a
        D[name] = nc.dram_tensor("in_" + name, a.shape, mb.dt.from_np(a.dtype), kind="ExternalInput").ap()
    out = nc.dram_tensor("out_0", (BATCH, SEQ, P), mb.dt.float32, kind="ExternalOutput").ap()
    program(nc, D, out)
    r = run_bass_kernel_spmd(nc, [feed], core_ids=[0])
    return r.results[0]["out_0"]
```

```python
from contextlib import ExitStack

import concourse.bass as bass
from concourse import mybir

F32 = mybir.dt.float32
BF16 = mybir.dt.bfloat16
I32 = mybir.dt.int32
U32 = mybir.dt.uint32
ALU = mybir.AluOpType
ACT = mybir.ActivationFunctionType
AX_X = mybir.AxisListType.X

P = 128
BATCH, SEQ = 4, 512
TILES = BATCH * SEQ // P
TPB = SEQ // P
HALVES = 2
STATES = 16
TAPS = 4
PAD = TAPS - 1
DT_RANK = 8
BC = 2 * STATES
PARTS = 3
EXPERTS, TOPK, EH = 32, 4, 64
PAIRS = EXPERTS // 2
SHARED = PAIRS
EPS = 1e-5
HEADS, DH = 16, 8
GROUPS, GH = 4, 4
COMBOS = 6
QROWS = COMBOS * DH
HIDDEN, HID_CHUNKS = 384, 3
LORA_R, LORA_SCALE = 8, 32.0 / 8.0
QUANT = 1.0 / 127.0
MASKED = -1e30
N_STORES = 6
SCALE = float(DH) ** -0.5




def prepare(nc, D, T, ctx):
    sb = lambda n, s, d=F32: ctx.enter_context(nc.sbuf_tensor(n, s, d))
    sem = lambda n: ctx.enter_context(nc.semaphore(n))
    bank = ctx.enter_context(nc.psum_tensor("bank0", [P, 8, 512], F32))
    XI, RES, BCB, Z = 0, 2, 5, 6
    TURN, LOGITS = 4, 5
    logits = bank[:, LOGITS, :]
    COMB, ROUND = 4, TILES // 2
    comb_t = bank[:, COMB, :].bitcast(BF16)

    stats = sb("stats", [P, TILES, 6])
    mean_var = sb("mean_var", [P, TILES, 2])
    std = sb("std", [P, TILES])
    rstd = sb("rstd", [P, TILES])
    eps = sb("eps", [P, 1])
    xn = sb("xn", [P, TILES, P])
    gate_w = sb("gate_w", [P, EXPERTS])
    gate_bias = sb("gate_bias", [P, EXPERTS])
    iota = sb("iota", [P, EXPERTS])
    scores = sb("scores", [P, TILES, EXPERTS])
    biased = sb("biased", [P, TILES, EXPERTS])
    top_val = sb("top_val", [P, TILES, 8])
    top_idx = sb("top_idx", [P, TILES, 8], U32)
    top_f = sb("top_f", [P, TILES, 8])
    hit = sb("hit", [P, 2, TILES, EXPERTS])
    wsum = sb("wsum", [P, TILES])
    winv = sb("winv", [P, TILES])
    rest = sb("rest", [P, TILES, EXPERTS])
    parts = sb("parts", [P, TILES, PARTS * EXPERTS], BF16)
    W_in = sb("W_in", [P, 4 * P])
    taps = sb("taps", [P, TAPS, P])
    W_tap = sb("W_tap", [P, TAPS, P])
    tap_columns = sb("tap_columns", [P, TAPS])
    conv_b = sb("conv_b", [P, HALVES])
    LOW = PARTS * BC
    W_x = sb("W_x", [P, HALVES, LOW + DT_RANK])
    W_dt = sb("W_dt", [LOW + DT_RANK, HALVES * P])
    b_dt = sb("b_dt", [P, HALVES])
    skip = sb("skip", [P, HALVES])
    dt_low = sb("dt_low", [LOW + DT_RANK, SEQ])
    conv = sb("conv", [P, SEQ])
    bc_hi = sb("bc_hi", [PARTS * BC, SEQ], BF16)
    bc_mid = sb("bc_mid", [PARTS * BC, SEQ], BF16)
    bc_rest = sb("bc_rest", [PARTS * BC, SEQ])
    zpos = sb("zpos", [P, BATCH, HALVES, SEQ])
    u = sb("u_in", [P, BATCH, HALVES, SEQ])

    xtm, xnP, combT, A = T["xtm"], T["xnP"], T["combT"], T["A"]
    uD, sres, delta, du, bc = T["u"], T["sres"], T["delta"], T["du"], T["bc"]

    x_in = [sem(f"x_in{g}") for g in range(BATCH)]
    ident_in, small_in, win_in, proj_in = sem("ident_in"), sem("small_in"), sem("win_in"), sem("proj_in")
    eps_set, pads_set, a_ready, a_neg, tap_ready = (sem(n) for n in ("eps_set", "pads_set", "a_ready", "a_neg", "tap_ready"))
    stat_done, aggr_done, std_done, rstd_done, xn_ready, turned, xnT_ready = (sem(n) for n in (
        "stat_done", "aggr_done", "std_done", "rstd_done", "xn_ready", "turned", "xnT_ready"))
    logits_ready, scores_ready, top_done, route, comb_parts, comb_turned, comb_ready = (sem(n) for n in (
        "logits_ready", "scores_ready", "top_done", "route", "comb_parts", "comb_turned", "comb_ready"))
    xi_ready, res_ready, u_ready, sres_ready, dt_low_ready, bc_ready, z_ready = (sem(n) for n in (
        "xi_ready", "res_ready", "u_ready", "sres_ready", "dt_low_ready", "bc_ready", "z_ready"))
    conv_step, conv_ready, conv0_ready, u0_ready = (sem(n) for n in ("conv_step", "conv_ready", "conv0_ready",
                                                                     "u0_ready"))
    bc_step, bc_parts, abs_done, expz_done, softlog_ready, zpos_done, delta_ready, du_ready, skip_ready = (
        sem(n) for n in ("bc_step", "bc_parts", "abs_done", "expz_done", "softlog_ready", "zpos_done",
                         "delta_ready", "du_ready", "skip_ready"))
    x_dram = D["x"].rearrange("b (n p) c -> b p n c", p=P)
    small = ((T["identb"], "identb"), (gate_w, "gate_w"), (gate_bias, "gate_bias"),
             (iota, "iota"), (A, "a_log"))
    proj = ((tap_columns[:], "tap_columns"), (conv_b[:], "conv_b"), (W_x[:], "W_x"), (W_dt[LOW:, :], "W_dt"),
            (b_dt[:], "b_dt"), (skip[:], "D"))
    n_small, n_proj = len(small), len(proj)
    block = ctx.enter_context(nc.Block())

    @block.sync
    def _(sp):
        def load_x(b):
            sp.dma_start(xtm[:, b * TPB:(b + 1) * TPB, :], x_dram[b]).then_inc(x_in[b], 16)

        load_x(0)
        sp.dma_start(T["ident"][:], D["ident"]).then_inc(ident_in, 16)
        load_x(1)
        sp.dma_start(W_in[:], D["W_in"]).then_inc(win_in, 16)
        sp.dma_start(taps[:], D["taps"]).then_inc(win_in, 16)
        load_x(2)
        load_x(3)
        for dst, name in proj:
            sp.dma_start(dst, D[name]).then_inc(proj_in, 16)
        for dst, src in T["expert_loads"]:
            sp.dma_start(dst, src).then_inc(T["experts_in"], 16)
        sp.wait_ge(T["experts_in"], 16 * len(T["expert_loads"]))

    @block.gpsimd
    def _(pool):
        nc.gpsimd.memset(eps[:], EPS).then_inc(eps_set, 1)
        nc.gpsimd.memset(xnP[:, :, 0:PAD], 0.0).then_inc(pads_set, 1)
        for dst, name in small:
            pool.dma_start(dst[:], D[name]).then_inc(small_in, 16)
        pool.wait_ge(proj_in, 16 * n_proj)
        with pool.Fori(0, BATCH) as b:
            pool.wait_ge(pads_set, 1)
            pool.wait_ge(u_ready, b + 1)
            nc.gpsimd.tensor_tensor(uD[:, b], u[:, b], skip[:].unsqueeze(2).to_broadcast([P, HALVES, SEQ]),
                                    ALU.mult).then_inc(skip_ready, 1)
        for b in range(0, BATCH, 2):
            pool.wait_ge(delta_ready, b + 1)
            nc.gpsimd.tensor_tensor(du[:, b], delta[:, b], u[:, b], ALU.mult).then_inc(du_ready, 1)
        pool.wait_ge(du_ready, BATCH)
        pool.wait_ge(skip_ready, BATCH)

    @block.scalar
    def _(act):
        def std_of(b):
            t = slice(b * TPB, (b + 1) * TPB)
            act.wait_ge(aggr_done, (b + 1) * TPB)
            if b == 0:
                act.wait_ge(eps_set, 1)
            nc.scalar.activation(std[:, t], mean_var[:, t, 1], ACT.Sqrt, bias=eps[:]).then_inc(std_done, 1)

        def keep_xnT(b):
            act.wait_ge(turned, b + 1)
            nc.scalar.copy(xnP[:, b, PAD:], bank[:, TURN + b, :]).then_inc(xnT_ready, 1)

        def constant_wait(b):
            if not isinstance(b, int):
                act.wait_ge(eps_set, 1)

        def gates(b):
            constant_wait(b)
            act.wait_ge(conv0_ready, b + 1)
            nc.scalar.activation(u[:, b, 0, :], bank[:, XI, :], ACT.Silu, bias=conv_b[:, 0:1]).then_inc(u0_ready, 1)
            constant_wait(b)
            act.wait_ge(res_ready, b + 1)
            nc.scalar.activation(sres[:, b], bank[:, RES:RES + 2, :], ACT.Silu).then_inc(sres_ready, 1)
            constant_wait(b)
            act.wait_ge(conv_ready, b + 1)
            nc.scalar.activation(u[:, b, 1, :], conv[:], ACT.Silu, bias=conv_b[:, 1:2]).then_inc(u_ready, 1)

        def low_rank(b):
            act.wait_ge(bc_ready, b + 1)
            nc.scalar.copy(dt_low[LOW:, :], bank[LOW:LOW + DT_RANK, BCB, :]).then_inc(dt_low_ready, 1)

        def absolute(b):
            constant_wait(b)
            act.wait_ge(z_ready, b + 1)
            for k in range(HALVES):
                ins = nc.scalar.activation(delta[:, b, k, :], bank[:, Z + k, :], ACT.Abs, bias=b_dt[:, k:k + 1])
            ins.then_inc(abs_done, 1)

        def exponential(b):
            act.wait_ge(abs_done, b + 1)
            nc.scalar.activation(delta[:, b], delta[:, b], ACT.Exp, scale=-1.0).then_inc(expz_done, 1)

        def logarithm(b):
            act.wait_ge(expz_done, b + 1)
            nc.scalar.activation(delta[:, b], delta[:, b], ACT.Ln, bias=1.0).then_inc(softlog_ready, 1)

        std_of(0)
        std_of(1)
        keep_xnT(0)
        std_of(2)
        keep_xnT(1)
        std_of(3)
        keep_xnT(2)
        keep_xnT(3)
        act.wait_ge(proj_in, 16 * n_proj)
        gates(0)
        act.wait_ge(logits_ready, 1)
        nc.scalar.activation(scores[:].rearrange("p a b -> p (a b)"), logits, ACT.Sigmoid).then_inc(scores_ready, 1)
        gates(1)
        low_rank(0)
        with act.Fori(2, BATCH) as b:
            gates(b)
            absolute(b - 2)
            low_rank(b - 1)
        def keep_weights(r):
            act.wait_ge(comb_turned, r + 1)
            nc.scalar.copy(combT[:, r * ROUND * P:(r + 1) * ROUND * P], comb_t[0:PARTS * EXPERTS, :]
                           ).then_inc(comb_ready, 1)

        L = BATCH - 1
        keep_weights(0)
        for b in range(L - 1):
            exponential(b)
        absolute(L - 1)
        keep_weights(1)
        exponential(L - 1)
        low_rank(L)
        act.wait_ge(small_in, 16 * n_small)
        nc.scalar.activation(A[:], A[:], ACT.Exp).then_inc(a_ready, 1)
        for b in range(L):
            logarithm(b)
        absolute(L)
        exponential(L)
        logarithm(L)
        act.wait_ge(comb_ready, 2)

    @block.vector
    def _(dve):
        def statistics(b):
            dve.wait_ge(x_in[b], 16)
            for n in range(b * TPB, (b + 1) * TPB):
                nc.vector.bn_stats(stats[:, n, :], xtm[:, n, :]).then_inc(stat_done, 1)
            for n in range(b * TPB, (b + 1) * TPB):
                dve.wait_ge(stat_done, n + 1)
                nc.vector.bn_aggr(mean_var[:, n, :], stats[:, n, :]).then_inc(aggr_done, 1)

        def normalise(b):
            t = slice(b * TPB, (b + 1) * TPB)
            dve.wait_ge(std_done, b + 1)
            nc.vector.reciprocal(rstd[:, t], std[:, t]).then_inc(rstd_done, 1)
            dve.wait_ge(rstd_done, b + 1)
            for n in range(b * TPB, (b + 1) * TPB):
                last = nc.vector.tensor_scalar(xn[:, n, :], xtm[:, n, :], mean_var[:, n, 0:1], rstd[:, n:n + 1],
                                               ALU.subtract, ALU.mult)
            last.then_inc(xn_ready, 1)

        statistics(0)
        for b in range(BATCH):
            if b + 1 < BATCH:
                statistics(b + 1)
            normalise(b)
            if b == 0:
                dve.wait_ge(win_in, 32)
                for k in range(TAPS):
                    ins = nc.vector.tensor_tensor(W_tap[:, k, :], W_in[:, 0:P], taps[:, k, :], ALU.mult)
                ins.then_inc(tap_ready, 1)

        def convolve(b):
            dve.wait_ge(xi_ready, b + 1)
            if not isinstance(b, int) or b > 0:
                dve.wait_ge(u_ready, b)
            xi = bank[:, XI + 1, :]
            nc.vector.tensor_scalar(conv[:], xi, tap_columns[:, TAPS - 1:TAPS], None, ALU.mult).then_inc(conv_step, 1)
            for back in range(1, TAPS):
                dve.wait_ge(conv_step, b * (TAPS - 1) + back)
                tap = TAPS - 1 - back
                nc.vector.scalar_tensor_tensor(
                    out=conv[:, back:], in0=xi[:, 0:SEQ - back], scalar=tap_columns[:, tap:tap + 1],
                    in1=conv[:, back:], op0=ALU.mult, op1=ALU.add
                ).then_inc(conv_step if back < TAPS - 1 else conv_ready, 1)

        def split_rows(b):
            dve.wait_ge(bc_ready, b + 1)
            src = bank[0:PARTS * BC, BCB, :]
            nc.vector.tensor_copy(bc_hi[:], src).then_inc(bc_step, 1)
            dve.wait_ge(bc_step, b * 5 + 1)
            nc.vector.tensor_tensor(bc_rest[:], src, bc_hi[:], ALU.subtract).then_inc(bc_step, 1)
            nc.vector.tensor_copy(bc[0:BC, b, :], bc_hi[0:BC, :]).then_inc(bc_step, 1)
            dve.wait_ge(bc_step, b * 5 + 2)
            nc.vector.tensor_copy(bc_mid[:], bc_rest[:]).then_inc(bc_step, 1)
            dve.wait_ge(bc_step, b * 5 + 4)
            nc.vector.tensor_copy(bc[BC:2 * BC, b, :], bc_mid[BC:2 * BC, :]).then_inc(bc_step, 1)
            nc.vector.tensor_tensor(bc[2 * BC:, b, :], bc_rest[2 * BC:, :], bc_mid[2 * BC:, :],
                                    ALU.subtract).then_inc(bc_parts, 1)

        def positive(b):
            dve.wait_ge(abs_done, b + 1)
            for k in range(HALVES):
                ins = nc.vector.tensor_scalar(zpos[:, b, k, :], bank[:, Z + k, :], b_dt[:, k:k + 1], 0.0,
                                              ALU.add, ALU.max)
            ins.then_inc(zpos_done, 1)

        def split(b):
            split_rows(b)
            positive(b)

        dve.wait_ge(proj_in, 16 * n_proj)
        convolve(0)
        dve.wait_ge(small_in, 16 * n_small)
        dve.wait_ge(scores_ready, 1)
        bias = gate_bias[:].unsqueeze(1).to_broadcast([P, TILES, EXPERTS])
        nc.vector.tensor_tensor(biased[:], scores[:], bias, ALU.add).then_inc(route, 1)
        dve.wait_ge(route, 1)
        for n in range(TILES):
            nc.vector.max(top_val[:, n, :], biased[:, n, :]).then_inc(top_done, 1)
        convolve(1)
        for n in range(TILES):
            dve.wait_ge(top_done, n + 1)
            nc.vector.max_index(top_idx[:, n, :], top_val[:, n, :], biased[:, n, :]).then_inc(top_done, 1)
        dve.wait_ge(top_done, 2 * TILES)
        nc.vector.tensor_copy(top_f[:], top_idx[:]).then_inc(route, 1)
        dve.wait_ge(route, 2)
        iota_b = iota[:].unsqueeze(1).to_broadcast([P, TILES, EXPERTS])
        step = 2
        for k in range(TOPK):
            chosen = top_f[:, :, k:k + 1].to_broadcast([P, TILES, EXPERTS])
            nc.vector.tensor_tensor(hit[:, min(k, 1)], iota_b, chosen, ALU.is_equal).then_inc(route, 1)
            step += 1
            dve.wait_ge(route, step)
            if k > 0:
                nc.vector.tensor_tensor(hit[:, 0], hit[:, 0], hit[:, 1], ALU.add).then_inc(route, 1)
                step += 1
                dve.wait_ge(route, step)
        convolve(2)
        split(0)
        nc.vector.tensor_tensor(scores[:], scores[:], hit[:, 0], ALU.mult).then_inc(route, 1)
        dve.wait_ge(route, step + 1)
        nc.vector.reduce_sum(wsum[:], scores[:], AX_X).then_inc(route, 1)
        dve.wait_ge(route, step + 2)
        nc.vector.reciprocal(winv[:], wsum[:]).then_inc(route, 1)
        dve.wait_ge(route, step + 3)
        nc.vector.tensor_tensor(scores[:], scores[:], winv[:].unsqueeze(2).to_broadcast([P, TILES, EXPERTS]),
                                ALU.mult).then_inc(route, 1)
        dve.wait_ge(route, step + 4)
        E = EXPERTS
        nc.vector.tensor_copy(parts[:, :, 0:E], scores[:]).then_inc(route, 1)
        dve.wait_ge(route, step + 5)
        nc.vector.tensor_tensor(rest[:], scores[:], parts[:, :, 0:E], ALU.subtract).then_inc(route, 1)
        dve.wait_ge(route, step + 6)
        nc.vector.tensor_copy(parts[:, :, E:2 * E], rest[:]).then_inc(route, 1)
        dve.wait_ge(route, step + 7)
        nc.vector.tensor_tensor(parts[:, :, 2 * E:3 * E], rest[:], parts[:, :, E:2 * E],
                                ALU.subtract).then_inc(comb_parts, 1)

        for b in range(3, BATCH):
            convolve(b)
        def finish(b):
            dve.wait_ge(softlog_ready, b + 1)
            nc.vector.tensor_tensor(delta[:, b], zpos[:, b], delta[:, b], ALU.add).then_inc(delta_ready, 1)
            if b % 2:
                dve.wait_ge(delta_ready, b + 1)
                nc.vector.tensor_tensor(du[:, b], delta[:, b], u[:, b], ALU.mult).then_inc(du_ready, 1)

        for b in range(1, BATCH - 1):
            split(b)
        dve.wait_ge(zpos_done, BATCH - 1)
        split_rows(BATCH - 1)
        for b in range(BATCH - 1):
            finish(b)
        dve.wait_ge(a_ready, 1)
        nc.vector.tensor_scalar(A[:], A[:], -1.0, None, ALU.mult).then_inc(a_neg, 1)
        positive(BATCH - 1)
        dve.wait_ge(zpos_done, BATCH)
        finish(BATCH - 1)
        dve.wait_ge(a_neg, 1)

    @block.tensor
    def _(pe):
        def turn(b):
            pe.wait_ge(xn_ready, b + 1)
            for n in range(TPB):
                last = nc.tensor.transpose(bank[:, TURN + b, n * P:(n + 1) * P], xn[:, b * TPB + n, :], T["ident"][:])
            last.then_inc(turned, 1)

        def in_proj(b, first):
            if not first:
                pe.wait_ge(conv_ready, b)
            nc.tensor.matmul(bank[:, XI + 1, :], W_in[:, P:2 * P], xnP[:, b, PAD:], start=True, stop=True
                             ).then_inc(xi_ready, 1)
            if not first:
                pe.wait_ge(u0_ready, b)
            for tap in range(TAPS):
                mm = nc.tensor.matmul(bank[:, XI, :], W_tap[:, tap, :], xnP[:, b, tap:tap + SEQ],
                                      start=(tap == 0), stop=(tap == TAPS - 1))
            mm.then_inc(conv0_ready, 1)
            if not first:
                pe.wait_ge(sres_ready, b)
            for k in range(HALVES):
                mm = nc.tensor.matmul(bank[:, RES + k, :], W_in[:, (2 + k) * P:(3 + k) * P], xnP[:, b, PAD:],
                                      start=True, stop=True)
            mm.then_inc(res_ready, 1)

        def b_and_c(b, first):
            pe.wait_ge(u_ready, b + 1)
            if not first:
                pe.wait_ge(bc_parts, b)
            for k in range(HALVES):
                mm = nc.tensor.matmul(bank[0:LOW + DT_RANK, BCB, :], W_x[:, k, :], u[:, b, k, :],
                                      start=(k == 0), stop=(k == 1))
            mm.then_inc(bc_ready, 1)

        def z(b):
            pe.wait_ge(dt_low_ready, b + 1)
            if b > 0:
                pe.wait_ge(zpos_done, b)
            for k in range(HALVES):
                mm = nc.tensor.matmul(bank[:, Z + k, :], W_dt[LOW:, k * P:(k + 1) * P], dt_low[LOW:, :],
                                      start=True, stop=True)
            mm.then_inc(z_ready, 1)

        pe.wait_ge(ident_in, 16)
        turn(0)
        turn(1)
        pe.wait_ge(pads_set, 1)
        pe.wait_ge(xnT_ready, 1)
        pe.wait_ge(tap_ready, 1)
        in_proj(0, True)
        turn(2)
        turn(3)
        pe.wait_ge(small_in, 16 * n_small)
        pe.wait_ge(xnT_ready, BATCH)
        for n in range(TILES):
            cols = slice(PAD + (n % TPB) * P, PAD + (n % TPB + 1) * P)
            last = nc.tensor.matmul(logits[:, n * EXPERTS:(n + 1) * EXPERTS], xnP[:, n // TPB, cols], gate_w[:],
                                    start=True, stop=True)
        last.then_inc(logits_ready, 1)
        pe.wait_ge(proj_in, 16 * n_proj)
        in_proj(1, False)
        pe.wait_ge(scores_ready, 1)
        b_and_c(0, True)
        for b in range(2, BATCH):
            in_proj(b, False)
            z(b - 2)
            b_and_c(b - 1, False)
        def turn_weights(r):
            for n in range(ROUND):
                last = nc.tensor.transpose(comb_t[0:PARTS * EXPERTS, n * P:(n + 1) * P],
                                           parts[:, r * ROUND + n, :], T["identb"][:])
            last.then_inc(comb_turned, 1)

        pe.wait_ge(comb_parts, 1)
        turn_weights(0)
        z(BATCH - 2)
        pe.wait_ge(comb_ready, 1)
        turn_weights(1)
        b_and_c(BATCH - 1, False)
        z(BATCH - 1)


def mix(nc, T, ctx):
    sb = lambda n, s, d=F32: ctx.enter_context(nc.sbuf_tensor(n, s, d))
    sem = lambda n: ctx.enter_context(nc.semaphore(n))
    bank = ctx.enter_context(nc.psum_tensor("bank1", [P, 8, 512], F32))
    B_BANK, C_BANK, V_BANK, W_BANK, G_BANK, O_BANK = 0, 2, 3, 4, 5, 7
    xnP, combT, A, bc = T["xnP"], T["combT"], T["A"], T["bc"]
    acc, sres, delta, du = T["u"], T["sres"], T["delta"], T["du"]
    N, M = STATES, STATES + 1

    dA = sb("dA", [P, 8, HALVES, SEQ])
    dBu = sb("dBu", [P, 2, HALVES, SEQ])
    h = sb("h", [P, 2, HALVES, SEQ])
    hC = sb("hC", [P, 2, HALVES, SEQ])
    silu_g = sb("silu_g", [P, 5, SEQ])
    hidden = sb("hidden", [P, 2, SEQ])
    w_sb = sb("w_sb", [P, 2, SEQ])
    weighted = sb("weighted", [P, 2, SEQ])
    slot = lambda i: 4 if i == SHARED else i % 4

    B_ready, C_ready, g_ready, v_ready, w_ready, w_kept = (sem(n) for n in (
        "B_ready", "C_ready", "g_ready", "v_ready", "w_ready", "w_kept"))
    dA_ready, silu_ready, dBu_done, scan_done, hC_done, hidden_done, weighted_done = (sem(n) for n in (
        "dA_ready", "silu_ready", "dBu_done", "scan_done", "hC_done", "hidden_done", "weighted_done"))
    zero_set, added, down_done, out_kept, y_done = (sem(n) for n in ("zero_set", "added", "down_done", "out_kept", "y_done"))
    block = ctx.enter_context(nc.Block())

    def batches(eng, body):
        with eng.Fori(0, BATCH - 1) as b:
            body(b, b + 1, False)
        body(BATCH - 1, None, True)

    @block.tensor
    def _(pe):
        pe.wait_ge(T["experts_in"], 16 * len(T["expert_loads"]))

        def xs(b):
            return xnP[:, b, PAD:]

        def spread_b(b, i):
            nc.tensor.matmul(bank[:, B_BANK + i % 2, :], T["sel_bc"][:, i, :], bc[:, b, :], start=True,
                             stop=True).then_inc(B_ready, 1)

        def spread_c(b, i):
            nc.tensor.matmul(bank[:, C_BANK, :], T["sel_bc"][:, N + i, :], bc[:, b, :], start=True,
                             stop=True).then_inc(C_ready, 1)

        def gate(b, i):
            w = T["gate_g"][:, i, :] if i < SHARED else T["shared_gate"][:, P:2 * P]
            nc.tensor.matmul(bank[:, G_BANK + i % 2, :], w, xs(b), start=True, stop=True).then_inc(g_ready, 1)

        def value(b, i):
            w = T["gate_v"][:, i, :] if i < SHARED else T["shared_gate"][:, 0:P]
            nc.tensor.matmul(bank[:, V_BANK, :], w, xs(b), start=True, stop=True).then_inc(v_ready, 1)

        spread_b(0, 0)
        spread_c(0, 0)
        for i in range(4):
            if i >= 2:
                pe.wait_ge(silu_ready, i - 1)
            gate(0, i)
            if i == 0:
                value(0, 0)

        def body(b, nxt, last):
            def down(i):
                if i < SHARED:
                    pe.wait_ge(weighted_done, b * N + i + 1)
                else:
                    pe.wait_ge(hidden_done, b * M + M)
                w = T["down"][:, i, :] if i < SHARED else T["shared_down"][:]
                nc.tensor.matmul(bank[:, O_BANK, :], w, weighted[:, i % 2, :], start=(i == 0),
                                 stop=(i == SHARED)).then_inc(down_done, 1)

            def later_gate(k):
                if k >= M and last:
                    return
                before = k - 2 if k != M else SHARED
                pe.wait_ge(silu_ready, b * M + before + 1)
                if k < M:
                    gate(b, k)
                else:
                    gate(nxt, k - M)

            for i in range(N):
                if i + 1 < N:
                    if i > 0:
                        pe.wait_ge(dBu_done, b * N + i)
                    spread_b(b, i + 1)
                elif not last:
                    pe.wait_ge(dBu_done, b * N + N - 1)
                    spread_b(nxt, 0)
                if i > 0:
                    pe.wait_ge(w_kept, b * N + i)
                nc.tensor.matmul(bank[:, W_BANK, :], T["sel_pair"][:, i, :], combT[:, bass.ts(b, SEQ)],
                                 start=True, stop=True).then_inc(w_ready, 1)
                if 0 < i < N - 1:
                    down(i - 1)
                if i % 4 == 2:
                    later_gate(i + 2)
                    later_gate(i + 3)
                if i % 4 == 3 and i < N - 1:
                    later_gate(i + 3)
                    later_gate(i + 4)
                pe.wait_ge(hidden_done, b * M + i + 1)
                value(b, i + 1)
                if i == N - 1:
                    down(i - 1)
                    for k in (3, 4, 5):
                        later_gate(i + k)
                if i + 1 < N:
                    pe.wait_ge(hC_done, b * N + i + 1)
                    spread_c(b, i + 1)
                elif not last:
                    pe.wait_ge(hC_done, b * N + N)
                    spread_c(nxt, 0)
            down(N - 1)
            down(SHARED)
            if not last:
                value(nxt, 0)
                pe.wait_ge(out_kept, b + 1)

        batches(pe, body)

    @block.scalar
    def _(act):
        def decay(b, i):
            for k in range(HALVES):
                ins = nc.scalar.activation(dA[:, i % 8, k, k:], delta[:, b, k, k:], ACT.Exp, scale=A[:, k, i:i + 1])
            ins.then_inc(dA_ready, 1)

        def silu(i):
            nc.scalar.activation(silu_g[:, slot(i), :], bank[:, G_BANK + i % 2, :], ACT.Silu).then_inc(silu_ready, 1)

        for i in range(4):
            decay(0, i)
        for i in range(4):
            act.wait_ge(g_ready, i + 1)
            silu(i)

        def body(b, nxt, last):
            def later_decay(k):
                if k >= N and last:
                    return
                act.wait_ge(dA_ready, 4)
                if k >= 8:
                    act.wait_ge(scan_done, b * N + k - 7)
                decay(b, k) if k < N else decay(nxt, k - N)

            def later_silu(k):
                if k >= M and last:
                    return
                act.wait_ge(g_ready, b * M + k + 1)
                if k == SHARED:
                    silu(k)
                    return
                before = k - 4 if k < M else k - M + 12
                act.wait_ge(hidden_done, b * M + before + 1)
                silu(k if k < M else k - M)

            for i in range(N):
                act.wait_ge(w_ready, b * N + i + 1)
                if i >= 2:
                    act.wait_ge(weighted_done, b * N + i - 1)
                nc.scalar.copy(w_sb[:, i % 2, :], bank[:, W_BANK, :]).then_inc(w_kept, 1)
                if i % 4 == 0:
                    later_decay(i + 4)
                    later_decay(i + 5)
                if i % 4 == 1:
                    later_decay(i + 5)
                    later_decay(i + 6)
                if i % 4 == 2:
                    later_silu(i + 2)
                    later_silu(i + 3)
                if i % 4 == 3:
                    later_silu(i + 3)
                    later_silu(i + 4)
                    if i == N - 1:
                        later_silu(i + 5)
            act.wait_ge(dA_ready, 4)
            act.wait_ge(down_done, b * M + M)
            nc.scalar.copy(delta[:, b, 0, :], bank[:, O_BANK, :]).then_inc(out_kept, 1)

        batches(act, body)
        act.wait_ge(out_kept, BATCH)

    @block.vector
    def _(dve):
        def spread(n):
            return bank[:, n, :].unsqueeze(1).to_broadcast([P, HALVES, SEQ])

        nc.vector.memset(dA[:, :, 1, 0:1], 0.0).then_inc(zero_set, 1)
        dve.wait_ge(zero_set, 1)
        with dve.Fori(0, BATCH) as b:
            def expert_hidden(i):
                dve.wait_ge(v_ready, b * M + i + 1)
                dve.wait_ge(silu_ready, b * M + i + 1)
                if i >= 2 and i < SHARED:
                    dve.wait_ge(weighted_done, b * N + i - 1)
                if i == SHARED:
                    dve.wait_ge(down_done, b * M + i - 1)
                dst = hidden if i < SHARED else weighted
                nc.vector.tensor_tensor(dst[:, i % 2, :], silu_g[:, slot(i), :], bank[:, V_BANK, :],
                                        ALU.mult).then_inc(hidden_done, 1)

            for i in range(N):
                dve.wait_ge(B_ready, b * N + i + 1)
                nc.vector.tensor_tensor(dBu[:, i % 2], du[:, b], spread(B_BANK + i % 2), ALU.mult).then_inc(dBu_done, 1)
                if i == N - 1:
                    expert_hidden(i)
                dve.wait_ge(dBu_done, b * N + i + 1)
                dve.wait_ge(dA_ready, b * N + i + 1)
                row = lambda t: t.rearrange("p k t -> p (k t)")
                nc.vector.tensor_tensor_scan(row(h[:, i % 2]), row(dA[:, i % 8]), row(dBu[:, i % 2]), 0.0,
                                             ALU.mult, ALU.add).then_inc(scan_done, 1)
                if i < N - 1:
                    expert_hidden(i)
                dve.wait_ge(C_ready, b * N + i + 1)
                dve.wait_ge(scan_done, b * N + i + 1)
                if i >= 1:
                    dve.wait_ge(added, b * N + i)
                nc.vector.tensor_tensor(hC[:, i % 2], h[:, i % 2], spread(C_BANK), ALU.mult).then_inc(hC_done, 1)
            expert_hidden(SHARED)

    @block.gpsimd
    def _(pool):
        nc.gpsimd.memset(hC[:, 1], 0.0).then_inc(added, 1)
        with pool.Fori(0, BATCH) as b:
            for i in range(N):
                pool.wait_ge(hidden_done, b * M + i + 1)
                pool.wait_ge(w_kept, b * N + i + 1)
                if i >= 2:
                    pool.wait_ge(down_done, b * M + i - 1)
                nc.gpsimd.tensor_tensor(weighted[:, i % 2, :], hidden[:, i % 2, :], w_sb[:, i % 2, :],
                                        ALU.mult).then_inc(weighted_done, 1)
                pool.wait_ge(hC_done, 1)
                pool.wait_ge(hC_done, b * N + i + 1)
                if i > 0:
                    pool.wait_ge(added, b * N + i + 1)
                nc.gpsimd.tensor_tensor(acc[:, b], acc[:, b], hC[:, i % 2], ALU.add).then_inc(added, 1)
            pool.wait_ge(hC_done, 1)
            pool.wait_ge(added, b * N + N + 1)
            nc.gpsimd.tensor_tensor(acc[:, b], acc[:, b], sres[:, b], ALU.mult).then_inc(y_done, 1)
        pool.wait_ge(y_done, BATCH)


def layer1_front(nc, D, T, ctx):
    sb = lambda n, s, d=F32: ctx.enter_context(nc.sbuf_tensor(n, s, d))
    sem = lambda n: ctx.enter_context(nc.semaphore(n))
    bank = ctx.enter_context(nc.psum_tensor("bank2", [P, 8, 512], F32))
    MAMBA, MIXED, XN, LORA = 1, (0, 5), (6, 7), 1
    X_BANK, ROT_BANK, VAL_BANK, HG_BANK, HV_BANK = 0, 1, 5, 6, 7
    xtm, ident, v_all = T["xtm"], T["ident"], T["v_all"]

    mixed = sb("mixed", [P, 2, SEQ])
    w_int = sb("w_int", [P, 3, HIDDEN], I32)
    w_ffn = sb("w_ffn", [P, 3, HIDDEN])
    lora_a = sb("lora_a", [LORA_R, 2, P])
    lora_b = sb("lora_b", [LORA_R, 2, P])
    w_q = sb("w_q", [P, P])
    w_k = sb("w_k", [P, P])
    w_v = sb("w_v", [P, P])
    w_qs = sb("w_qs", [P, P])
    w_ks = sb("w_ks", [P, P])
    cos = sb("cos", [P, SEQ])
    sin = sb("sin", [P, SEQ])
    eps = sb("eps1", [P, 1])
    stats = sb("stats1", [P, TILES, 6])
    mean_var = sb("mean_var1", [P, TILES, 2])
    std = sb("std1", [P, TILES])
    rstd = sb("rstd1", [P, TILES])
    xn = sb("xn1", [P, TILES, P])
    xnT = sb("xnT1", [P, BATCH, SEQ])
    xnT_now = sb("xnT_now", [P, SEQ])
    silu_g = sb("silu_g1", [P, HID_CHUNKS, SEQ])
    hid = sb("hid", [P, HID_CHUNKS, SEQ])
    rot_c = sb("rot_c", [P, 2, SEQ])
    rot_s = sb("rot_s", [P, 2, SEQ])
    qk_parts = T["qk_parts"]

    w_in, masks_in, lora_ready, w_ready, eps_set, rows_set, w_cast = (sem(n) for n in (
        "w1_in", "masks_in", "lora_ready", "w_ready", "eps1_set", "rows_set", "w_cast"))
    mamba_ready, mixed_ready, mixed_turned, x1_ready = (sem(n) for n in (
        "mamba_ready", "mixed_ready", "mixed_turned", "x1_ready"))
    stat_done, aggr_done, std_done, rstd_done, xn_ready, turned, xnT_ready, now_ready = (sem(n) for n in (
        "stat1_done", "aggr1_done", "std1_done", "rstd1_done", "xn1_ready", "turned1", "xnT1_ready", "now_ready"))
    hg_ready, hv_ready, silu_ready, hid_done, down_ready, x2_done = (sem(n) for n in (
        "hg_ready", "hv_ready", "silu1_ready", "hid_done", "down_ready", "x2_done"))
    rot_ready, v_ready, v_kept, cos_done, sin_done, rot_done, hi_done, rest_done, mid_done, parts_ready = (
        sem(n) for n in ("rot_ready", "v1_ready", "v_kept", "cos_done", "sin_done", "rot_done", "hi_done",
                         "rest_done", "mid_done", "parts_ready"))
    parts_out = T["parts_out"]
    n_w = 10
    C = HID_CHUNKS
    block = ctx.enter_context(nc.Block())

    def batches(eng, body):
        with eng.Fori(0, BATCH - 1) as b:
            body(b, b + 1, False)
        body(BATCH - 1, None, True)

    @block.sync
    def _(sp):
        for dst, name in ((lora_a[:, 0, :], "Aq_t"), (lora_a[:, 1, :], "Av_t"),
                          (lora_b[:, 0, :], "Bq"), (lora_b[:, 1, :], "Bv"), (w_q[:], "wq"), (w_k[:], "wk"),
                          (w_v[:], "wv"), (w_int[:], "w_ffn"), (cos[:], "cos"), (sin[:], "sin")):
            sp.dma_start(dst, D[name]).then_inc(w_in, 16)
        sp.dma_start(T["masks"][:], D["masks"]).then_inc(masks_in, 16)

        def store_parts(b, out):
            sp.wait_ge(parts_ready, b + 1)
            for c, n in ((0, 3), (3, 2), (5, 1)):
                dst = T["q_stack"][b, :, :, c:c + n, :].rearrange("h r c t -> (h r) c t")
                sp.dma_start(dst, qk_parts[:, b, 0, 0:n, :]).then_inc(out, 16)
            for c, part, n in ((0, 0, 3), (3, 1, 2), (5, 2, 1)):
                dst = T["k_stack"][b, :, :, c:c + n, :].rearrange("h r c t -> (h r) c t")
                src = qk_parts[:, b, 1, part:part + 1, :].to_broadcast([P, n, SEQ])
                sp.dma_start(dst, src).then_inc(out, 16)

        store_parts(0, parts_out[0])
        sp.wait_ge(parts_out[0], 16 * N_STORES)
        sp.wait_ge(rows_set, 4)
        for g in range(3):
            load_stack(sp, T, 0, g)
        with sp.Fori(1, BATCH) as b:
            store_parts(b, parts_out[1])
        sp.wait_ge(masks_in, 16)

    @block.gpsimd
    def _(pool):
        nc.gpsimd.memset(eps[:], EPS).then_inc(eps_set, 1)
        nc.gpsimd.memset(T["v_aug"][:], 0.0).then_inc(rows_set, 1)
        pool.wait_ge(rows_set, 1)
        nc.gpsimd.memset(T["v_aug"][:, :, :, :, DH:DH + 1], 1.0).then_inc(rows_set, 1)
        nc.gpsimd.memset(T["q_rows"][:], 1.0).then_inc(rows_set, 1)
        nc.gpsimd.memset(T["k_rows"][:], 1.0).then_inc(rows_set, 1)
        pool.wait_ge(xnT_ready, BATCH)
        nc.gpsimd.tensor_copy(xnT_now[:], xnT[:, 0, :]).then_inc(now_ready, 1)

        def body(b, nxt, last):
            pool.wait_ge(rows_set, 1)
            pool.wait_ge(cos_done, b + 1)
            pool.wait_ge(sin_done, b + 1)
            nc.gpsimd.tensor_tensor(rot_c[:], rot_c[:], rot_s[:], ALU.add).then_inc(rot_done, 1)
            if not last:
                pool.wait_ge(rows_set, 1)
                pool.wait_ge(v_ready, b + 1)
                nc.gpsimd.tensor_copy(xnT_now[:], xnT[:, nxt, :]).then_inc(now_ready, 1)

        batches(pool, body)
        pool.wait_ge(rot_done, BATCH)

    @block.scalar
    def _(act):
        for b in range(BATCH):
            t = slice(b * TPB, (b + 1) * TPB)
            act.wait_ge(aggr_done, (b + 1) * TPB)
            if b == 0:
                act.wait_ge(eps_set, 1)
            nc.scalar.activation(std[:, t], mean_var[:, t, 1], ACT.Sqrt, bias=eps[:]).then_inc(std_done, 1)
            if b == 0:
                act.wait_ge(w_in, 16 * n_w)
                for m in range(3):
                    ins = nc.scalar.activation(w_ffn[:, m, :], w_int[:, m, :], ACT.Copy, scale=QUANT)
                ins.then_inc(w_cast, 1)
            if b > 0:
                act.wait_ge(turned, b)
                nc.scalar.copy(xnT[:, b - 1, :], bank[:, XN[(b - 1) % 2], :]).then_inc(xnT_ready, 1)
        act.wait_ge(turned, BATCH)
        nc.scalar.copy(xnT[:, BATCH - 1, :], bank[:, XN[(BATCH - 1) % 2], :]).then_inc(xnT_ready, 1)

        def silu(b, m):
            act.wait_ge(hg_ready, b * C + m + 1)
            nc.scalar.activation(silu_g[:, m % C, :], bank[:, HG_BANK, :], ACT.Silu).then_inc(silu_ready, 1)

        def body(b, nxt, last):
            silu(b, 1)
            silu(b, 2)
            act.wait_ge(rows_set, 1)
            act.wait_ge(v_ready, b + 1)
            nc.scalar.copy(v_all[:, bass.ts(b, TPB), :], bank[:, VAL_BANK, :].rearrange("p (n c) -> p n c", c=P)
                           ).then_inc(v_kept, 1)
            if not last:
                silu(b, C)

        silu(0, 0)
        batches(act, body)
        act.wait_ge(v_kept, BATCH)

    @block.vector
    def _(dve):
        def layer_norm_input(b):
            dve.wait_ge(mixed_turned, b + 1)
            xs = xtm[:, b * TPB:(b + 1) * TPB, :]
            nc.vector.tensor_tensor(xs, xs, bank[:, MIXED[b % 2], :].rearrange("p (n c) -> p n c", c=P),
                                    ALU.add).then_inc(x1_ready, 1)
            dve.wait_ge(x1_ready, b + 1)
            for n in range(b * TPB, (b + 1) * TPB):
                nc.vector.bn_stats(stats[:, n, :], xtm[:, n, :]).then_inc(stat_done, 1)
            for n in range(b * TPB, (b + 1) * TPB):
                dve.wait_ge(stat_done, n + 1)
                nc.vector.bn_aggr(mean_var[:, n, :], stats[:, n, :]).then_inc(aggr_done, 1)

        def normalise(b):
            t = slice(b * TPB, (b + 1) * TPB)
            dve.wait_ge(std_done, b + 1)
            nc.vector.reciprocal(rstd[:, t], std[:, t]).then_inc(rstd_done, 1)
            dve.wait_ge(rstd_done, b + 1)
            for n in range(b * TPB, (b + 1) * TPB):
                ins = nc.vector.tensor_scalar(xn[:, n, :], xtm[:, n, :], mean_var[:, n, 0:1], rstd[:, n:n + 1],
                                              ALU.subtract, ALU.mult)
            ins.then_inc(xn_ready, 1)

        for b in range(BATCH):
            dve.wait_ge(mamba_ready, b + 1)
            if b >= 2:
                dve.wait_ge(mixed_turned, b - 1)
            nc.vector.tensor_tensor(mixed[:, b % 2, :], T["delta"][:, b, 0, :], bank[:, MAMBA + b, :],
                                    ALU.add).then_inc(mixed_ready, 1)
            if b > 0:
                layer_norm_input(b - 1)
            if b > 1:
                normalise(b - 2)
        layer_norm_input(BATCH - 1)
        dve.wait_ge(lora_ready, 1)
        for w, k in ((w_q, 0), (w_v, 1)):
            nc.vector.scalar_tensor_tensor(out=w[:], in0=bank[:, LORA, k * P:(k + 1) * P], scalar=LORA_SCALE,
                                           in1=w[:], op0=ALU.mult, op1=ALU.add).then_inc(w_ready, 1)
        dve.wait_ge(w_ready, 2)
        for w, ws in ((w_q, w_qs), (w_k, w_ks)):
            nc.vector.tensor_copy(ws[:, 0::2], w[:, 1::2]).then_inc(w_ready, 1)
            nc.vector.tensor_copy(ws[:, 1::2], w[:, 0::2]).then_inc(w_ready, 1)
        normalise(BATCH - 2)
        normalise(BATCH - 1)

        def hidden(b, m):
            dve.wait_ge(silu_ready, b * C + m + 1)
            dve.wait_ge(hv_ready, b * C + m + 1)
            if m == 0 and (not isinstance(b, int) or b > 0):
                dve.wait_ge(down_ready, b)
            if m == C:
                dve.wait_ge(down_ready, b + 1)
            nc.vector.tensor_tensor(hid[:, m % C, :], silu_g[:, m % C, :], bank[:, HV_BANK, :],
                                    ALU.mult).then_inc(hid_done, 1)

        def split(b):
            hi, mid, low = (qk_parts[:, b, :, m, :] for m in range(PARTS))
            dve.wait_ge(lora_ready, 1)
            dve.wait_ge(rot_done, b + 1)
            nc.vector.tensor_copy(hi, rot_c[:]).then_inc(hi_done, 1)
            dve.wait_ge(hi_done, b + 1)
            nc.vector.tensor_tensor(rot_s[:], rot_c[:], hi, ALU.subtract).then_inc(rest_done, 1)
            dve.wait_ge(lora_ready, 1)
            dve.wait_ge(rest_done, b + 1)
            nc.vector.tensor_copy(mid, rot_s[:]).then_inc(mid_done, 1)
            dve.wait_ge(mid_done, b + 1)
            nc.vector.tensor_tensor(low, rot_s[:], mid, ALU.subtract).then_inc(parts_ready, 1)

        def body(b, nxt, last):
            table = lambda t: t[:].unsqueeze(1).to_broadcast([P, 2, SEQ])
            dve.wait_ge(rot_ready, b + 1)
            nc.vector.tensor_tensor(rot_c[:], bank[:, ROT_BANK:ROT_BANK + 2, :], table(cos), ALU.mult
                                    ).then_inc(cos_done, 1)
            nc.vector.tensor_tensor(rot_s[:], bank[:, ROT_BANK + 2:ROT_BANK + 4, :], table(sin),
                                    ALU.mult).then_inc(sin_done, 1)
            hidden(b, 1)
            hidden(b, 2)
            split(b)
            dve.wait_ge(down_ready, b + 1)
            xs = xtm[:, bass.ts(b, TPB), :]
            nc.vector.tensor_tensor(xs, xs, bank[:, X_BANK, :].rearrange("p (n c) -> p n c", c=P),
                                    ALU.add).then_inc(x2_done, 1)
            if not last:
                hidden(b, C)
                dve.wait_ge(parts_ready, b + 1)

        hidden(0, 0)
        batches(dve, body)
        dve.wait_ge(x2_done, BATCH)

    @block.tensor
    def _(pe):
        def mamba(b):
            for k in range(HALVES):
                mm = nc.tensor.matmul(bank[:, MAMBA + b, :], T["w_out"][:, k, :], T["u"][:, b, k, :],
                                      start=(k == 0), stop=(k == 1))
            mm.then_inc(mamba_ready, 1)

        def turn_mixed(b):
            pe.wait_ge(mixed_ready, b + 1)
            if b >= 2:
                pe.wait_ge(x1_ready, b - 1)
            for n in range(TPB):
                mm = nc.tensor.transpose(bank[:, MIXED[b % 2], n * P:(n + 1) * P], mixed[:, b % 2, n * P:(n + 1) * P],
                                         ident[:])
            mm.then_inc(mixed_turned, 1)

        def turn_xn(b):
            pe.wait_ge(xn_ready, b + 1)
            if b >= 2:
                pe.wait_ge(xnT_ready, b - 1)
            for n in range(TPB):
                mm = nc.tensor.transpose(bank[:, XN[b % 2], n * P:(n + 1) * P], xn[:, b * TPB + n, :], ident[:])
            mm.then_inc(turned, 1)

        for b in range(BATCH):
            mamba(b)
            if b > 0:
                turn_mixed(b - 1)
        turn_mixed(BATCH - 1)
        pe.wait_ge(w_in, 16 * n_w)
        for k in range(2):
            mm = nc.tensor.matmul(bank[:, LORA, k * P:(k + 1) * P], lora_a[:, k, :], lora_b[:, k, :],
                                  start=True, stop=True)
        mm.then_inc(lora_ready, 1)

        def gate(b, m):
            if not isinstance(b, int) or b * C + m > 0:
                pe.wait_ge(silu_ready, b * C + m)
            rhs = xnT[:, b, :] if m < C else xnT[:, b + 1, :]
            w = slice(m % C * P, (m % C + 1) * P)
            nc.tensor.matmul(bank[:, HG_BANK, :], w_ffn[:, 0, w], rhs, start=True, stop=True).then_inc(hg_ready, 1)

        def up(b, m):
            if not isinstance(b, int) or b * C + m > 0:
                pe.wait_ge(hid_done, b * C + m)
            rhs = xnT[:, b, :] if m < C else xnT[:, b + 1, :]
            w = slice(m % C * P, (m % C + 1) * P)
            nc.tensor.matmul(bank[:, HV_BANK, :], w_ffn[:, 1, w], rhs, start=True, stop=True).then_inc(hv_ready, 1)

        def rotated(b):
            for k, w in enumerate((w_q, w_k, w_qs, w_ks)):
                mm = nc.tensor.matmul(bank[:, ROT_BANK + k, :], w[:], xnT[:, b, :], start=True, stop=True)
            mm.then_inc(rot_ready, 1)

        def body(b, nxt, last):
            gate(b, 1)
            up(b, 1)
            gate(b, 2)
            pe.wait_ge(now_ready, b + 1)
            for n in range(TPB):
                mm = nc.tensor.matmul(bank[:, VAL_BANK, n * P:(n + 1) * P], xnT_now[:, n * P:(n + 1) * P], w_v[:],
                                      start=True, stop=True)
            mm.then_inc(v_ready, 1)
            up(b, 2)
            if not last:
                pe.wait_ge(sin_done, b + 1)
                rotated(nxt)
                gate(b, C)
            pe.wait_ge(hid_done, b * C + C)
            for n in range(TPB):
                for m in range(C):
                    mm = nc.tensor.matmul(bank[:, X_BANK, n * P:(n + 1) * P], hid[:, m, n * P:(n + 1) * P],
                                          w_ffn[:, 2, m * P:(m + 1) * P], start=(m == 0), stop=(m == C - 1))
            mm.then_inc(down_ready, 1)
            if not last:
                up(b, C)
                pe.wait_ge(x2_done, b + 1)
                pe.wait_ge(v_kept, b + 1)

        turn_xn(0)
        turn_xn(1)
        pe.wait_ge(w_ready, 6)
        pe.wait_ge(xnT_ready, 1)
        pe.wait_ge(mixed_ready, BATCH)
        rotated(0)
        turn_xn(2)
        turn_xn(3)
        pe.wait_ge(w_cast, 1)
        pe.wait_ge(xnT_ready, BATCH)
        gate(0, 0)
        up(0, 0)
        batches(pe, body)


def load_stack(sp, T, b, g):
    for par in range(2):
        for rows, name in ((T["q_rows"], "q_stack"), (T["k_rows"], "k_stack")):
            src = T[name][b].rearrange("h r c t -> h (r c) t")
            src = src[GH * g + par:GH * (g + 1):2].rearrange("h r t -> r h t")
            sp.dma_start(rows[64 * par:64 * par + QROWS, g, :, :], src).then_inc(T["stack_in"][g], 16)


def attention(nc, D, T, out, ctx):
    sb = lambda n, s, d=F32: ctx.enter_context(nc.sbuf_tensor(n, s, d))
    sem = lambda n: ctx.enter_context(nc.semaphore(n))
    bank = ctx.enter_context(nc.psum_tensor("bank3", [P, 8, 512], F32))
    S1, S2, AV_BANK, M_BANK, T_BANK = 0, 2, 5, 6, 7
    xtm, ident, identb = T["xtm"], T["ident"], T["identb"]
    q_rows, k_rows, v_aug, v_all = T["q_rows"], T["k_rows"], T["v_aug"], T["v_all"]
    mask_qk, mask_kq = T["masks"][:, 0, :], T["masks"][:, 1, :]
    NQ = TPB
    PCOLS = sum(SEQ - j * P for j in range(NQ))
    first = [sum(SEQ - i * P for i in range(j)) for j in range(NQ + 1)]
    PAIR = GH // 2

    w_o = sb("w_o", [P, P])
    rowmax = sb("rowmax", [P, NQ, 2, PAIR])
    negmax = sb("negmax", [P, NQ, 2, PAIR])
    negrest = sb("negrest", [P, NQ, 2, PAIR])
    neg_parts = sb("neg_parts", [P, 2, NQ, 2, PARTS, PAIR], BF16)
    neg_t = sb("neg_t", [2 * PARTS * PAIR, 2, SEQ], BF16)
    probs = sb("probs", [P, 2, PCOLS])
    avT = sb("avT", [P, SEQ])
    inv_sum = sb("inv_sum", [P, NQ, GH])
    att = sb("att", [P, NQ, P])
    attT = sb("attT", [P, SEQ])
    result = sb("result", [P, NQ, P])

    stack_in = T["stack_in"]
    m_in = [sem(f"m_in{k}") for k in range(2)]
    s1_ready, max_done, neg_step, neg_ready, m_turned, neg_t_ready = (sem(n) for n in (
        "s1_ready", "max_done", "neg_step", "neg_ready", "m_turned", "neg_t_ready"))
    v_set, s2a_ready, s2b_ready, p_a, p_b, av_done, avT_ready, av_turned, inv_done, att_done = (sem(n) for n in (
        "v_set", "s2a_ready", "s2b_ready", "p_a", "p_b", "av_done", "avT_ready", "av_turned", "inv_done", "att_done"))
    att_turned, attT_ready, o_ready, result_ready, result_out = (sem(n) for n in (
        "att_turned", "attT_ready", "o_ready", "result_ready", "result_out"))

    chunks = ([(i, heads) for i in (0, 1) for heads in ((0, 2), (1, 3))]
              + [(i, (hl,)) for i in (2, 3) for hl in range(GH)])
    NCH = len(chunks)
    PER_SLOT = NCH // GH
    G, H = GROUPS, HEADS
    out_dram = out.rearrange("b (n p) c -> b p n c", p=P)
    block = ctx.enter_context(nc.Block())

    def stages(eng, stage):
        stage(0, 0, True, False)
        with eng.Fori(0, BATCH - 1) as b:
            for g in range(1, G + 1):
                stage(b, g, True, False)
        for g in range(1, G + 1):
            stage(BATCH - 1, g, g < G, True)

    @block.sync
    def _(sp):
        sp.dma_start(w_o[:], D["wo"]).then_inc(result_out, 16)

        def place_max(b, g):
            sp.wait_ge(neg_t_ready, b * G + g + 1)
            for par in range(2):
                dst = q_rows[64 * par + QROWS:64 * par + QROWS + PARTS, g % G, :, :]
                rows = slice(par * PARTS * PAIR, (par + 1) * PARTS * PAIR)
                sp.dma_start(dst, neg_t[rows, g % 2, :]).then_inc(m_in[g % 2], 16)

        def stage(b, g, run, last):
            if not (last and g + 3 >= G):
                if g > 0:
                    sp.wait_ge(s2b_ready, b * H + g * GH)
                load_stack(sp, T, b + (g + 3) // G, (g + 3) % G)
            if not (last and g + 1 >= G):
                place_max(b, g + 1)
            if g == G:
                sp.wait_ge(result_ready, b + 2)
                sp.dma_start(out_dram[b], result[:]).then_inc(result_out, 16)

        place_max(0, 0)
        sp.wait_ge(T["parts_out"][1], 16 * N_STORES * (BATCH - 1))
        stages(sp, stage)
        sp.wait_ge(result_out, 16 + 16 * BATCH)

    @block.gpsimd
    def _(pool):
        def set_values(b, g):
            for hl in range(GH):
                c = (GH * (g % G) + hl) * DH
                ins = nc.gpsimd.tensor_copy(v_aug[:, g % 2, :, hl, 0:DH],
                                            v_all[:, bass.ts(b + g // G, TPB), c:c + DH])
            ins.then_inc(v_set, 1)

        def stage(b, g, run, last):
            if last and g + 1 >= G:
                return
            if g > 0:
                pool.wait_ge(av_done, b * H + g * GH)
            set_values(b, g + 1)

        set_values(0, 0)
        stages(pool, stage)
        pool.wait_ge(v_set, BATCH * G)

    @block.tensor
    def _(pe):
        def stack(t, g, hl, rows, cols):
            lo = 64 * (hl % 2)
            return t[lo:lo + rows, g % G, hl // 2, cols]

        def max_chunk(b, g, n):
            if n == 0:
                pe.wait_ge(stack_in[g % G], (b + g // G + 1) * 64)
            i, heads = chunks[n]
            done = g * NCH + n
            if not isinstance(b, int) or b * G * NCH + done >= 2:
                pe.wait_ge(max_done, b * (G * NCH) + done - 1)
            width = (i + 1) * P
            for s, hl in enumerate(heads):
                dst = bank[:, S1 + done % 2, s * width:(s + 1) * width]
                nc.tensor.matmul(dst, stack(q_rows, g, hl, QROWS, slice(i * P, (i + 1) * P)),
                                 stack(k_rows, g, hl, QROWS, slice(0, width)), start=True, stop=False)
                mm = nc.tensor.matmul(dst[:, i * P:], identb[:], mask_qk, start=False, stop=True)
            mm.then_inc(s1_ready, 1)

        def turn_max(b, g):
            pe.wait_ge(neg_ready, b * G + g + 1)
            if not isinstance(b, int) or b * G + g > 0:
                pe.wait_ge(neg_t_ready, b * G + g)
            for i in range(NQ):
                src = neg_parts[:, g % 2, i].rearrange("p a j h -> p (a j h)")
                mm = nc.tensor.matmul(bank[0:2 * PARTS * PAIR, M_BANK, i * P:(i + 1) * P], src, identb[:],
                                      start=True, stop=True)
            mm.then_inc(m_turned, 1)

        def scores(b, g, hl, half):
            h = g * GH + hl
            if hl == 0 and half == 0:
                pe.wait_ge(m_in[g % 2], b * (16 * G) + 32 * (g // 2 + 1))
            if not isinstance(b, int) or b * H + h > 0:
                pe.wait_ge((p_a, p_b)[half], b * H + h)
            for j in (2 * half, 2 * half + 1):
                width = SEQ - j * P
                at = 2 * P if j == 3 else 0
                dst = bank[:, S2 + min(j, 2), at:at + width]
                nc.tensor.matmul(dst, stack(k_rows, g, hl, QROWS + PARTS, slice(j * P, (j + 1) * P)),
                                 stack(q_rows, g, hl, QROWS + PARTS, slice(j * P, SEQ)), start=True, stop=False)
                mm = nc.tensor.matmul(dst[:, 0:P], identb[:], mask_kq, start=False, stop=True)
            mm.then_inc((s2a_ready, s2b_ready)[half], 1)

        def values(b, g, hl, tiles):
            h = g * GH + hl
            if tiles[0] == 0:
                if hl == 0:
                    pe.wait_ge(v_set, b * G + g + 1)
                    if g > 0:
                        pe.wait_ge(avT_ready, b * G + g)
                pe.wait_ge(p_b, b * H + h + 1)
            for j in tiles:
                mm = nc.tensor.matmul(bank[32 * hl:32 * hl + 32, AV_BANK, j * P:SEQ], v_aug[:, g % 2, j, hl, :],
                                      probs[:, h % 2, first[j]:first[j + 1]], start=(j == 0), stop=(j == NQ - 1))
            if tiles[-1] == NQ - 1:
                mm.then_inc(av_done, 1)

        def turn_values(b, g):
            pe.wait_ge(avT_ready, b * G + g + 1)
            if g > 0:
                pe.wait_ge(att_done, b * G + g)
            else:
                pe.wait_ge(result_ready, b + 1)
            for n in range(NQ):
                mm = nc.tensor.transpose(bank[:, T_BANK, n * P:(n + 1) * P], avT[:, n * P:(n + 1) * P], ident[:])
            mm.then_inc(av_turned, 1)

        def turn_att(b):
            pe.wait_ge(att_done, b * G + G)
            for n in range(NQ):
                mm = nc.tensor.transpose(bank[:, M_BANK, n * P:(n + 1) * P], att[:, n, :], ident[:])
            mm.then_inc(att_turned, 1)

        def project(b):
            pe.wait_ge(result_out, 16)
            pe.wait_ge(attT_ready, b + 1)
            for n in range(NQ):
                mm = nc.tensor.matmul(bank[:, T_BANK, n * P:(n + 1) * P], attT[:, n * P:(n + 1) * P], w_o[:],
                                      start=True, stop=True)
            mm.then_inc(o_ready, 1)

        def stage(b, g, run, last):
            ahead = not (last and g + 2 >= G)
            for hl in range(GH):
                n = hl * PER_SLOT
                if run:
                    follow = (g, hl + 1) if hl + 1 < GH else (g + 1, 0)
                    if last and follow[0] >= G:
                        follow = None
                    if follow:
                        scores(b, *follow, 0)
                    if ahead:
                        max_chunk(b, g + 2, n)
                    if follow:
                        scores(b, *follow, 1)
                    values(b, g, hl, (0,))
                    if ahead:
                        max_chunk(b, g + 2, n + 1)
                    values(b, g, hl, (1, 2, 3))
                    if ahead:
                        max_chunk(b, g + 2, n + 2)
                if hl == 0 and not (last and g + 1 >= G):
                    turn_max(b, g + 1)
                if hl == 1 and g > 0:
                    turn_values(b, g - 1)
                if hl == 2 and g == G:
                    if not last:
                        pe.wait_ge(neg_t_ready, b * G + g + 2)
                    turn_att(b)
                if hl == 3 and g == G:
                    project(b)

        for g in range(2):
            for n in range(NCH):
                max_chunk(0, g, n)
            if g == 0:
                turn_max(0, 0)
        scores(0, 0, 0, 0)
        scores(0, 0, 0, 1)
        stages(pe, stage)

    @block.scalar
    def _(act):
        def keep_max(b, g):
            act.wait_ge(m_turned, b * G + g + 1)
            if not isinstance(b, int) or b * G + g >= 2:
                act.wait_ge(m_in[g % 2], b * (16 * G) + 32 * (g // 2))
            nc.scalar.copy(neg_t[:, g % 2, :], bank[0:2 * PARTS * PAIR, M_BANK, :]).then_inc(neg_t_ready, 1)

        def exps(b, g, hl):
            h = g * GH + hl
            act.wait_ge(s2a_ready, b * H + h + 1)
            if not isinstance(b, int) or b * H + h >= 2:
                act.wait_ge(av_done, b * H + h - 1)
            src = bank[:, S2:S2 + 2, :].rearrange("p a c -> p (a c)")[:, 0:first[2]]
            nc.scalar.activation(probs[:, h % 2, 0:first[2]], src, ACT.Exp, scale=SCALE).then_inc(p_a, 1)
            act.wait_ge(s2b_ready, b * H + h + 1)
            nc.scalar.activation(probs[:, h % 2, first[2]:PCOLS], bank[:, S2 + 2, 0:PCOLS - first[2]],
                                 ACT.Exp, scale=SCALE).then_inc(p_b, 1)

        def stage(b, g, run, last):
            for hl in range(GH):
                if run:
                    exps(b, g, hl)
                if hl == 0 and g > 0:
                    act.wait_ge(av_done, b * H + g * GH)
                    if g > 1:
                        act.wait_ge(av_turned, b * G + g - 1)
                    nc.scalar.copy(avT[:], bank[:, AV_BANK, :]).then_inc(avT_ready, 1)
                if hl == 1 and not (last and g + 1 >= G):
                    keep_max(b, g + 1)
                if hl == 3 and g == G:
                    act.wait_ge(att_turned, b + 1)
                    nc.scalar.copy(attT[:], bank[:, M_BANK, :]).then_inc(attT_ready, 1)

        keep_max(0, 0)
        stages(act, stage)

    @block.vector
    def _(dve):
        nc.vector.memset(result[:], 0.0).then_inc(result_ready, 1)

        def reduce_chunk(b, g, n):
            i, heads = chunks[n]
            done = g * NCH + n
            dve.wait_ge(s1_ready, b * (G * NCH) + done + 1)
            width = (i + 1) * P
            src = bank[:, S1 + done % 2, 0:len(heads) * width].rearrange("p (h k) -> p h k", k=width)
            dst = rowmax[:, i, heads[0] % 2, heads[0] // 2:heads[-1] // 2 + 1]
            nc.vector.reduce_max(dst, src, AX_X).then_inc(max_done, 1)

        def split_max(b, g):
            dve.wait_ge(max_done, b * (G * NCH) + (g + 1) * NCH)
            s = 4 * g
            nc.vector.tensor_scalar(negmax[:], rowmax[:], -1.0, None, ALU.mult).then_inc(neg_step, 1)
            dve.wait_ge(neg_step, b * (4 * G) + s + 1)
            if not isinstance(b, int) or b * G + g >= 2:
                dve.wait_ge(m_turned, b * G + g - 1)
            hi, mid, low = (neg_parts[:, g % 2, :, :, j, :] for j in range(PARTS))
            nc.vector.tensor_copy(hi, negmax[:]).then_inc(neg_step, 1)
            dve.wait_ge(neg_step, b * (4 * G) + s + 2)
            nc.vector.tensor_tensor(negrest[:], negmax[:], hi, ALU.subtract).then_inc(neg_step, 1)
            dve.wait_ge(neg_step, b * (4 * G) + s + 3)
            nc.vector.tensor_copy(mid, negrest[:]).then_inc(neg_step, 1)
            dve.wait_ge(neg_step, b * (4 * G) + s + 4)
            nc.vector.tensor_tensor(low, negrest[:], mid, ALU.subtract).then_inc(neg_ready, 1)

        def normalise(b, g):
            dve.wait_ge(av_turned, b * G + g + 1)
            src = bank[:, T_BANK, :].rearrange("p (n h d) -> p n h d", n=NQ, h=GH)
            nc.vector.reciprocal(inv_sum[:], src[:, :, :, DH]).then_inc(inv_done, 1)
            dve.wait_ge(inv_done, b * G + g + 1)
            dst = att[:, :, g * GH * DH:(g + 1) * GH * DH].rearrange("p n (h d) -> p n h d", h=GH)
            nc.vector.tensor_tensor(dst, src[:, :, :, 0:DH], inv_sum[:].unsqueeze(3).to_broadcast([P, NQ, GH, DH]),
                                    ALU.mult).then_inc(att_done, 1)

        def stage(b, g, run, last):
            ahead = not (last and g + 2 >= G)
            for n in range(NCH):
                if ahead:
                    reduce_chunk(b, g + 2, n)
                if n == 2 * PER_SLOT - 1 and g > 0:
                    normalise(b, g - 1)
            if ahead:
                split_max(b, g + 2)
            if g == G:
                dve.wait_ge(o_ready, b + 1)
                dve.wait_ge(result_out, b * 16 + 16)
                nc.vector.tensor_tensor(result[:], xtm[:, bass.ts(b, TPB), :],
                                        bank[:, T_BANK, :].rearrange("p (n c) -> p n c", c=P),
                                        ALU.add).then_inc(result_ready, 1)

        for g in range(2):
            for n in range(NCH):
                reduce_chunk(0, g, n)
            split_max(0, g)
        stages(dve, stage)
        dve.wait_ge(result_ready, BATCH + 1)


def program(nc, D, out):
    with ExitStack() as ctx:
        T = {}

        def tensors(stack, table):
            for name, (shape, dt) in table.items():
                T[name] = stack.enter_context(nc.sbuf_tensor(name, shape, dt))

        tensors(ctx, {
            "xtm": ([P, TILES, P], F32), "ident": ([P, P], F32), "identb": ([P, P], BF16),
            "u": ([P, BATCH, HALVES, SEQ], F32), "delta": ([P, BATCH, HALVES, SEQ], F32),
            "w_out": ([P, HALVES, P], F32)})
        T["experts_in"] = ctx.enter_context(nc.semaphore("experts_in"))
        with ExitStack() as layer0:
            loaded = {
                "sel_bc": ([PARTS * BC, BC, P], BF16), "sel_pair": ([PARTS * EXPERTS, PAIRS, P], BF16),
                "gate_g": ([P, PAIRS, P], F32), "gate_v": ([P, PAIRS, P], F32), "down": ([P, PAIRS, P], F32),
                "shared_gate": ([P, 2 * P], F32), "shared_down": ([P, P], F32)}
            tensors(layer0, loaded)
            tensors(layer0, {
                "xnP": ([P, BATCH, PAD + SEQ], F32), "combT": ([PARTS * EXPERTS, BATCH * SEQ], BF16),
                "A": ([P, HALVES, STATES], F32), "sres": ([P, BATCH, HALVES, SEQ], F32),
                "du": ([P, BATCH, HALVES, SEQ], F32), "bc": ([PARTS * BC, BATCH, SEQ], BF16)})
            T["expert_loads"] = [(T[name][:], D[name]) for name in loaded] + [(T["w_out"][:], D["W_out"])]
            with ExitStack() as stage:
                prepare(nc, D, T, stage)
            with ExitStack() as stage:
                mix(nc, T, stage)
        with ExitStack() as layer1:
            tensors(layer1, {
                "v_all": ([P, TILES, P], F32), "v_aug": ([P, 2, TPB, GH, 32], F32),
                "q_rows": ([P, GROUPS, GH // 2, SEQ], BF16), "k_rows": ([P, GROUPS, GH // 2, SEQ], BF16),
                "masks": ([P, 2, P], BF16), "qk_parts": ([P, BATCH, 2, PARTS, SEQ], BF16)})
            for name in ("q_stack", "k_stack"):
                T[name] = nc.dram_tensor(name, (BATCH, HEADS, DH, COMBOS, SEQ), BF16, kind="Internal").ap()
            T["parts_out"] = [layer1.enter_context(nc.semaphore(f"parts_out{k}")) for k in range(2)]
            T["stack_in"] = [layer1.enter_context(nc.semaphore(f"stack_in{g}")) for g in range(GROUPS)]
            with ExitStack() as stage:
                layer1_front(nc, D, T, stage)
            with ExitStack() as stage:
                attention(nc, D, T, out, stage)


def kernel(**inputs):
    import ml_dtypes
    import numpy as np
    import concourse.bacc as bacc
    from concourse import mybir as mb
    from concourse.bass_utils import run_bass_kernel_spmd

    I = {k: np.asarray(v) for k, v in inputs.items()}
    bf16 = ml_dtypes.bfloat16

    def halves(a):
        return a.reshape((HALVES, P) + a.shape[1:]).swapaxes(0, 1)

    ident = np.eye(P, dtype=np.float32)
    sel_bc = np.zeros((PARTS, BC, BC, P), np.float32)
    sel_pair = np.zeros((PARTS, EXPERTS, PAIRS, 2, EH), np.float32)
    for r in range(BC):
        sel_bc[:, r, r, :] = 1
    for e in range(EXPERTS):
        sel_pair[:, e, e // 2, e % 2, :] = 1

    w_x = halves(I["L0_attn_W_x"])
    gate = I["L0_ffn_expert_gate_w"].transpose(1, 0, 2)
    theta = (np.arange(SEQ, dtype=np.float32)[:, None]
             / np.float32(10000.0) ** (np.arange(0, DH, 2, dtype=np.float32) / DH)[None, :])
    spread = lambda t: np.tile(np.repeat(t.T, 2, axis=0), (HEADS, 1))
    sign = np.tile(np.array([-1, 1], np.float32), P // 2)[:, None]
    later = np.triu(np.full((P, P), MASKED, np.float32), k=1)
    ffn = np.stack([I["L1_ffn_w_gate"].T, I["L1_ffn_w_up"].T,
                    I["L1_ffn_w_down"].T.reshape(HID_CHUNKS, P, P).swapaxes(0, 1).reshape(P, HIDDEN)], axis=1)
    arrays = {
        "cos": spread(np.cos(theta)), "sin": spread(np.sin(theta)) * sign,
        "masks": np.stack([later, later.T], axis=1).astype(bf16), "w_ffn": ffn,
        "Aq_t": I["L1_attn_Aq"].T, "Av_t": I["L1_attn_Av"].T, "Bq": I["L1_attn_Bq"], "Bv": I["L1_attn_Bv"],
        "wq": I["L1_attn_wq"], "wk": I["L1_attn_wk"], "wv": I["L1_attn_wv"], "wo": I["L1_attn_wo"],
        "x": I["L0_attn_x"], "W_in": I["L0_attn_W_in"],
        "taps": np.broadcast_to(I["L0_attn_conv_w"][0:P, 0, :].T[None], (P, TAPS, P)),
        "conv_b": halves(I["L0_attn_conv_b"]), "tap_columns": I["L0_attn_conv_w"][P:, 0, :],
        "W_x": np.concatenate([w_x[:, :, DT_RANK:]] * PARTS + [w_x[:, :, 0:DT_RANK]], axis=2), "W_dt": I["L0_attn_W_dt"],
        "b_dt": halves(I["L0_attn_b_dt"]), "a_log": halves(I["L0_attn_A_log"]), "D": halves(I["L0_attn_D"]),
        "W_out": halves(I["L0_attn_W_out"]), "gate_w": I["L0_ffn_gate_w"],
        "gate_bias": np.broadcast_to(I["L0_ffn_gate_bias"][None, :], (P, EXPERTS)),
        "gate_v": gate[:, :, 0:EH].reshape(P, PAIRS, P), "gate_g": gate[:, :, EH:].reshape(P, PAIRS, P),
        "down": I["L0_ffn_expert_down_w"].reshape(PAIRS, P, P).swapaxes(0, 1),
        "shared_gate": I["L0_ffn_shared_gate_w"], "shared_down": I["L0_ffn_shared_down_w"],
        "ident": ident, "identb": ident.astype(bf16), "sel_bc": sel_bc.reshape(PARTS * BC, BC, P).astype(bf16),
        "sel_pair": sel_pair.reshape(PARTS * EXPERTS, PAIRS, P).astype(bf16),
        "iota": np.broadcast_to(np.arange(EXPERTS, dtype=np.float32)[None, :], (P, EXPERTS)),
    }
    nc = bacc.Bacc("TRN2", target_bir_lowering=False, num_devices=1)
    feed, D = {}, {}
    for name, a in arrays.items():
        a = np.ascontiguousarray(a)
        feed["in_" + name] = a
        D[name] = nc.dram_tensor("in_" + name, a.shape, mb.dt.from_np(a.dtype), kind="ExternalInput").ap()
    out = nc.dram_tensor("out_0", (BATCH, SEQ, P), mb.dt.float32, kind="ExternalOutput").ap()
    program(nc, D, out)
    r = run_bass_kernel_spmd(nc, [feed], core_ids=[0])
    return r.results[0]["out_0"]
```
